# Optimizing a Trainium2 kernel written in Bass

```python
import numpy as np
import jax
import jax.numpy as jnp

def _softmax(x, axis=-1):
    return jax.nn.softmax(x, axis=axis)

def _gelu(x):
    return jax.nn.gelu(x, approximate=True)

def _silu(x):
    return jax.nn.silu(x)

def _sigmoid(x):
    return jax.nn.sigmoid(x)

def _layernorm(x, axis=-1, eps=1e-05):
    m = jnp.mean(x, axis=axis, keepdims=True)
    v = jnp.var(x, axis=axis, keepdims=True)
    return (x - m) / jnp.sqrt(v + eps)

def _scatter_add(tgt, idx, src, axis=0):
    return tgt.at[idx].add(src)

def _segment_sum(src, seg, n):
    return jax.ops.segment_sum(src, seg, n)
kernel_name = 'mk_recurrent_d2_jaxref_r8_3ac51d'

def setup_inputs(seed: int=0):
    np.random.seed(seed)
    _w = jnp.asarray

    def _L0_attn_setup():
        import jax, jax.numpy as jnp
        import numpy as np
        import math
        DK = 128
        key = jax.random.key(seed)
        k1, k2 = jax.random.split(key)
        x = jax.random.normal(k1, (4, 256, 128), dtype=jnp.float32)
        W = jax.random.normal(k2, (128, 3 * DK), dtype=jnp.float32) * (1.0 / math.sqrt(128))
        b = jnp.zeros((3 * DK,), dtype=jnp.float32)
        return {'x': x, 'W': W, 'b': b}
    _L0_attn_in = _L0_attn_setup()

    def _L0_ffn_setup():
        import jax, jax.numpy as jnp
        import numpy as np
        from jax.scipy.linalg import expm
        D = 128
        E = 6
        K = 2
        H = 2 * D
        A4 = 4 * D
        NROT = 4
        LN_EPS = 1e-05

        def _xavier(key, shape):
            fan_in, fan_out = (shape[-2], shape[-1])
            lim = np.sqrt(6.0 / (fan_in + fan_out))
            return jax.random.uniform(key, shape, jnp.float32, -lim, lim)

        def _layernorm(x, g, b):
            mu = jnp.mean(x, axis=-1, keepdims=True)
            var = jnp.var(x, axis=-1, keepdims=True)
            return (x - mu) * jax.lax.rsqrt(var + LN_EPS) * g + b

        def _moe(xn, gate_w, gate_b, ew1, eb1, ew2, eb2):
            logits = xn @ gate_w + gate_b
            tw, ti = jax.lax.top_k(logits, K)
            tw = jax.nn.softmax(tw, axis=-1)
            w_full = jnp.sum(tw[..., None] * jax.nn.one_hot(ti, E, dtype=tw.dtype), axis=-2)
            h = jax.nn.gelu(jnp.einsum('bsd,edh->besh', xn, ew1) + eb1[None, :, None, :], approximate=False)
            eo = jnp.einsum('besh,ehd->besd', h, ew2) + eb2[None, :, None, :]
            return jnp.einsum('bse,besd->bsd', w_full, eo)

        def _rotate(x, gens):
            for i in range(NROT):
                x = x @ expm(gens[i])
            return x
        key = jax.random.key(seed)
        ks = jax.random.split(key, 16)
        x = jax.random.normal(ks[0], (4, 256, D), jnp.float32)
        gens_raw = _xavier(ks[1], (NROT, D, D))
        gens = 0.5 * (gens_raw - jnp.swapaxes(gens_raw, -1, -2))
        return {'x': x, 'ln_g': jnp.ones((D,), jnp.float32), 'ln_b': jnp.zeros((D,), jnp.float32), 'aw1': _xavier(ks[2], (D, A4)), 'ab1': jnp.zeros((A4,), jnp.float32), 'aw2': _xavier(ks[3], (A4, D)), 'ab2': jnp.zeros((D,), jnp.float32), 'gate_w': _xavier(ks[4], (D, E)), 'gate_b': jnp.zeros((E,), jnp.float32), 'ew1': _xavier(ks[5], (E, D, H)), 'eb1': jnp.zeros((E, H), jnp.float32), 'ew2': _xavier(ks[6], (E, H, D)), 'eb2': jnp.zeros((E, D), jnp.float32), 'gens': gens, 'gc_w': _xavier(ks[7], (2 * D, 1)), 'gc_b': jnp.zeros((1,), jnp.float32)}
    _L0_ffn_in = _L0_ffn_setup()

    def _L1_attn_setup():
        import jax, jax.numpy as jnp
        import numpy as np
        HEADS = 8
        K_SIZE = 64
        key = jax.random.key(seed)
        k1, k2, k3, k4 = jax.random.split(key, 4)
        B, C, D = (4, 256, 128)
        return {'x': jax.random.normal(k1, (B, C, D), dtype=jnp.float32), 'Mq': jax.random.normal(k2, (D, HEADS * K_SIZE), dtype=jnp.float32) * 0.02, 'Mk': jax.random.normal(k3, (D, HEADS * K_SIZE), dtype=jnp.float32) * 0.02, 'Mv': jax.random.normal(k4, (D, 128), dtype=jnp.float32) * 0.02}
    _L1_attn_in = _L1_attn_setup()

    def _L1_ffn_setup():
        import jax, jax.numpy as jnp
        import numpy as np
        B, T, D, H, E = (4, 256, 128, 512, 8)
        key = jax.random.key(seed)
        ks = jax.random.split(key, 7)
        x = jax.random.normal(ks[0], (B, T, D), dtype=jnp.float32)
        Wg = jax.random.normal(ks[1], (D, E), dtype=jnp.float32) / np.sqrt(D)
        bg = jax.random.normal(ks[2], (E,), dtype=jnp.float32) * 0.01
        W1 = jax.random.normal(ks[3], (E, D, H), dtype=jnp.float32) / np.sqrt(D)
        b1 = jax.random.normal(ks[4], (E, H), dtype=jnp.float32) * 0.01
        W2 = jax.random.normal(ks[5], (E, H, D), dtype=jnp.float32) / np.sqrt(H)
        b2 = jax.random.normal(ks[6], (E, D), dtype=jnp.float32) * 0.01
        return {'x': x, 'Wg': Wg, 'bg': bg, 'W1': W1, 'b1': b1, 'W2': W2, 'b2': b2}
    _L1_ffn_in = _L1_ffn_setup()
    _d = {'L0_attn_x': _L0_attn_in['x'], 'L0_attn_W': _L0_attn_in['W'], 'L0_attn_b': _L0_attn_in['b'], 'L0_ffn_ln_g': _L0_ffn_in['ln_g'], 'L0_ffn_ln_b': _L0_ffn_in['ln_b'], 'L0_ffn_aw1': _L0_ffn_in['aw1'], 'L0_ffn_ab1': _L0_ffn_in['ab1'], 'L0_ffn_aw2': _L0_ffn_in['aw2'], 'L0_ffn_ab2': _L0_ffn_in['ab2'], 'L0_ffn_gate_w': _L0_ffn_in['gate_w'], 'L0_ffn_gate_b': _L0_ffn_in['gate_b'], 'L0_ffn_ew1': _L0_ffn_in['ew1'], 'L0_ffn_eb1': _L0_ffn_in['eb1'], 'L0_ffn_ew2': _L0_ffn_in['ew2'], 'L0_ffn_eb2': _L0_ffn_in['eb2'], 'L0_ffn_gens': _L0_ffn_in['gens'], 'L0_ffn_gc_w': _L0_ffn_in['gc_w'], 'L0_ffn_gc_b': _L0_ffn_in['gc_b'], 'L1_attn_Mq': _L1_attn_in['Mq'], 'L1_attn_Mk': _L1_attn_in['Mk'], 'L1_attn_Mv': _L1_attn_in['Mv'], 'L1_ffn_Wg': _L1_ffn_in['Wg'], 'L1_ffn_bg': _L1_ffn_in['bg'], 'L1_ffn_W1': _L1_ffn_in['W1'], 'L1_ffn_b1': _L1_ffn_in['b1'], 'L1_ffn_W2': _L1_ffn_in['W2'], 'L1_ffn_b2': _L1_ffn_in['b2']}
    _x0 = _d['L0_attn_x']
    _d['L0_attn_x'] = jax.random.normal(jax.random.fold_in(jax.random.key(seed), 1), (8, 512, 128), dtype=_x0.dtype)
    del _x0
    return _d

def reference(L0_attn_x, L0_attn_W, L0_attn_b, L0_ffn_ln_g, L0_ffn_ln_b, L0_ffn_aw1, L0_ffn_ab1, L0_ffn_aw2, L0_ffn_ab2, L0_ffn_gate_w, L0_ffn_gate_b, L0_ffn_ew1, L0_ffn_eb1, L0_ffn_ew2, L0_ffn_eb2, L0_ffn_gens, L0_ffn_gc_w, L0_ffn_gc_b, L1_attn_Mq, L1_attn_Mk, L1_attn_Mv, L1_ffn_Wg, L1_ffn_bg, L1_ffn_W1, L1_ffn_b1, L1_ffn_W2, L1_ffn_b2):

    def _L0_attn_ref(x, W, b):
        import jax, jax.numpy as jnp
        import numpy as np
        import math
        DK = 128
        qkv = jnp.einsum('btc,cd->btd', x, W) + b
        q, k, v = jnp.split(qkv, 3, axis=-1)
        scale = 1.0 / math.sqrt(DK)
        weights = jnp.einsum('btc,bTc->btT', q, k) * scale
        T = weights.shape[-1]
        mask = jnp.tril(jnp.ones((T, T), dtype=jnp.float32))
        logits = jnp.where(mask == 0, jnp.float32(-9000000000000000.0), weights)
        attention = jax.nn.softmax(logits, axis=-1)
        values = jnp.einsum('btT,bTc->btc', attention, v)
        return values

    def _L0_ffn_ref(x, ln_g, ln_b, aw1, ab1, aw2, ab2, gate_w, gate_b, ew1, eb1, ew2, eb2, gens, gc_w, gc_b):
        import jax, jax.numpy as jnp
        import numpy as np
        from jax.scipy.linalg import expm
        D = 128
        E = 6
        K = 2
        H = 2 * D
        A4 = 4 * D
        NROT = 4
        LN_EPS = 1e-05

        def _xavier(key, shape):
            fan_in, fan_out = (shape[-2], shape[-1])
            lim = np.sqrt(6.0 / (fan_in + fan_out))
            return jax.random.uniform(key, shape, jnp.float32, -lim, lim)

        def _layernorm(x, g, b):
            mu = jnp.mean(x, axis=-1, keepdims=True)
            var = jnp.var(x, axis=-1, keepdims=True)
            return (x - mu) * jax.lax.rsqrt(var + LN_EPS) * g + b

        def _moe(xn, gate_w, gate_b, ew1, eb1, ew2, eb2):
            logits = xn @ gate_w + gate_b
            tw, ti = jax.lax.top_k(logits, K)
            tw = jax.nn.softmax(tw, axis=-1)
            w_full = jnp.sum(tw[..., None] * jax.nn.one_hot(ti, E, dtype=tw.dtype), axis=-2)
            h = jax.nn.gelu(jnp.einsum('bsd,edh->besh', xn, ew1) + eb1[None, :, None, :], approximate=False)
            eo = jnp.einsum('besh,ehd->besd', h, ew2) + eb2[None, :, None, :]
            return jnp.einsum('bse,besd->bsd', w_full, eo)

        def _rotate(x, gens):
            for i in range(NROT):
                x = x @ expm(gens[i])
            return x
        residual = x
        xn = _layernorm(x, ln_g, ln_b)
        abel = jax.nn.gelu(xn @ aw1 + ab1, approximate=False) @ aw2 + ab2
        nonabel = _rotate(_moe(xn, gate_w, gate_b, ew1, eb1, ew2, eb2), gens)
        combined = jnp.concatenate([abel, nonabel], axis=-1)
        gate = jax.nn.sigmoid(combined @ gc_w + gc_b)
        mixed = abel * (1.0 - gate) + nonabel * gate
        return residual + mixed

    def _L1_attn_ref(x, Mq, Mk, Mv):
        import jax, jax.numpy as jnp
        import numpy as np
        HEADS = 8
        K_SIZE = 64
        B, C, _ = x.shape
        H, K = (HEADS, K_SIZE)
        V = Mv.shape[1] // H
        q = (x @ Mq).reshape(B, H, C, K)
        k = (x @ Mk).reshape(B, H, C, K)
        v = (x @ Mv).reshape(B, H, C, V)
        scores = jnp.einsum('bhqk,bhck->bhqc', q, k).reshape(B * H, C, C)
        att = jax.nn.softmax(scores / jnp.sqrt(jnp.float32(K)), axis=1)
        att4 = att.reshape(B, C, H, C)
        out = jnp.einsum('bqhc,bhcd->bqhd', att4, v)
        return out.reshape(B, C, H * V)

    def _L1_ffn_ref(x, Wg, bg, W1, b1, W2, b2):
        import jax, jax.numpy as jnp
        import numpy as np
        B, T, D, H, E = (4, 256, 128, 512, 8)
        gate_scores = x @ Wg + bg
        top1 = jnp.argmax(gate_scores, axis=-1)
        onehot = jax.nn.one_hot(top1, Wg.shape[-1], dtype=x.dtype)
        h = jax.nn.relu(jnp.einsum('btd,edh->beth', x, W1) + b1[None, :, None, :])
        y = jnp.einsum('beth,ehd->betd', h, W2) + b2[None, :, None, :]
        out = jnp.einsum('betd,bte->btd', y, onehot)
        return out
    x = L0_attn_x
    xn = _layernorm(x, axis=-1)
    s = _L0_attn_ref(xn, L0_attn_W, L0_attn_b)
    g = _silu(_L0_ffn_ref(xn, L0_ffn_ln_g, L0_ffn_ln_b, L0_ffn_aw1, L0_ffn_ab1, L0_ffn_aw2, L0_ffn_ab2, L0_ffn_gate_w, L0_ffn_gate_b, L0_ffn_ew1, L0_ffn_eb1, L0_ffn_ew2, L0_ffn_eb2, L0_ffn_gens, L0_ffn_gc_w, L0_ffn_gc_b))
    x = x + s * g
    xn = _layernorm(x, axis=-1)
    s = _L1_attn_ref(xn, L1_attn_Mq, L1_attn_Mk, L1_attn_Mv)
    g = _silu(_L1_ffn_ref(xn, L1_ffn_Wg, L1_ffn_bg, L1_ffn_W1, L1_ffn_b1, L1_ffn_W2, L1_ffn_b2))
    x = x + s * g
    return x

_drawn_inputs = setup_inputs


def setup_inputs(seed=0):
    import zlib

    import numpy as np

    out = dict(_drawn_inputs(seed))
    spreads = {'L0_attn_b': (0.0, 0.1),
     'L0_ffn_ln_g': (1.0, 0.6),
     'L0_ffn_ln_b': (0.0, 0.8),
     'L0_ffn_ab1': (0.0, 0.8),
     'L0_ffn_ab2': (0.0, 0.8),
     'L0_ffn_gate_b': (0.0, 0.8),
     'L0_ffn_eb1': (0.0, 0.8),
     'L0_ffn_eb2': (0.0, 0.8)}
    factors = {'L0_ffn_gc_w': 3.356,
     'L1_attn_Mq': 8.0,
     'L1_attn_Mk': 8.0,
     'L1_attn_Mv': 8.0,
     'L1_ffn_Wg': 8.0,
     'L1_ffn_bg': 8.0,
     'L1_ffn_W1': 8.0,
     'L1_ffn_b1': 44.624,
     'L1_ffn_W2': 8.0,
     'L1_ffn_b2': 200.0}
    for name, (base, spread) in spreads.items():
        noise = np.random.default_rng([zlib.crc32(name.encode()), seed]).standard_normal(out[name].shape)
        drawn = base * np.exp(spread * noise) if base else spread * noise
        out[name] = jnp.asarray(drawn.astype(out[name].dtype))
    for name, factor in factors.items():
        out[name] = (out[name] * factor).astype(out[name].dtype)
    return out
```

```python
from contextlib import ExitStack

import concourse.bass as bass
from concourse import mybir

F32 = mybir.dt.float32
F32R = mybir.dt.float32r
ALU = mybir.AluOpType
ACT = mybir.ActivationFunctionType
AX = mybir.AxisListType

P = 128
EPS = 1e-5
BIG = 3.0e38
TAYLOR = 12
SQUARE = 4


def recurrent_d2_kernel(nc, x, W, b, ln_g, ln_b, aw1, ab1, aw2, ab2, gate_w, gate_b, ew1, eb1, ew2, eb2,
                        gens, gc_w, gc_b, Mq, Mk, Mv, Wg, bg, W1, b1, W2, b2, out):
    B, T, D = x.shape
    TT = T // P
    NT = B * TT
    AC = aw1.shape[1] // P
    E0, H0 = ew1.shape[0], ew1.shape[2]
    EC = H0 // P
    E1, H1 = W1.shape[0], W1.shape[2]
    HC = H1 // P
    G = gens.shape[0]
    HEADS = 8
    KS = Mq.shape[1] // HEADS
    HT = T // HEADS
    VD = D // HEADS
    SC0 = float(D) ** -0.5
    SC1 = float(KS) ** -0.5
    LOOPS = B // 2
    ROW_B, ROW_G, ROW_LB, ROW_AB1 = 0, 3, 4, 5
    ROW_EB1 = ROW_AB1 + AC
    ROW_B1 = ROW_EB1 + E0 * EC
    ROWS = ROW_B1 + E1 * HC

    with ExitStack() as ctx:
        def sb(name, shape, dt=F32):
            return ctx.enter_context(nc.sbuf_tensor(name, shape, dt))

        early = ctx.enter_context(ExitStack())

        def sbe(name, shape, dt=F32):
            return early.enter_context(nc.sbuf_tensor(name, shape, dt))

        def sem(name):
            return ctx.enter_context(nc.semaphore(name))

        x_all = sb("x_all", [P, NT, D])
        ident = sb("ident", [P, P])
        cols = sb("cols", [P, ROWS])
        mq_d = sb("mq_d", [P, HEADS, 2, KS])
        mk_d = sb("mk_d", [P, HEADS, 2, KS])
        mv = sb("mv", [P, D])
        wg = sb("wg", [P, E1])
        bg_c = sb("bg_c", [E1, 1])
        w_1 = sb("w_1", [P, E1, H1])
        w_2 = sb("w_2", [P, E1 * HC, D])
        b2_sb = sb("b2_sb", [E1, D])
        lgT = sb("lgT", [P, T])
        rev = sb("rev", [P, TT, E1])
        half_neg = sb("half_neg", [P, NT])
        xn_all = sbe("xn_all", [P, NT, D])
        xn2T = sbe("xn2T", [P, B * T])
        s_all = sbe("s_all", [P, NT, D])
        cmask = sbe("cmask", [P, P])
        rows = sbe("rows", [ROWS, P])
        bqs = sbe("bqs", [P, 1])
        w_qkv = sbe("w_qkv", [P, 3 * D])
        bv_bc = sbe("bv_bc", [P, D])
        w_a1 = sbe("w_a1", [P, AC * P])
        w_a2 = sbe("w_a2", [P, AC, D])
        ab2_bc = sbe("ab2_bc", [P, D])
        w_gate = sbe("w_gate", [P, E0])
        gate_bc = sbe("gate_bc", [E0, 1])
        w_e1 = sbe("w_e1", [P, E0, H0])
        w_e2 = sbe("w_e2", [P, E0 * EC, D])
        w_e2T = sbe("w_e2T", [P, E0 * EC, D])
        eb2_sb = sbe("eb2_sb", [E0, D])
        eb2T = sbe("eb2T", [P, E0])
        eb2R = sbe("eb2R", [E0, D])
        gA = sbe("gA", [P, G, D])
        gAT = sbe("gAT", [P, G, D])
        gE = sbe("gE", [P, G, D])
        gET = sbe("gET", [P, G, D])
        rot = sbe("rot", [P, D])
        gc_bc = sbe("gc_bc", [P, 2, D])
        gcb_bc = sbe("gcb_bc", [P, 1])
        gcb_half = sbe("gcb_half", [P, 1])
        bn = sbe("bn", [P, NT, 6])
        mv_st = sbe("mv_st", [P, NT, 2])
        ve = sbe("ve", [P, NT])
        rs1 = sbe("rs1", [P, NT])
        rs2 = sbe("rs2", [P, NT])

        psum = [ctx.enter_context(nc.psum_tensor(f"bank{i}", [P, T], F32)) for i in range(8)]

        ld_x = [sem(f"ld_x{i}") for i in range(B)]
        ld_w = sem("ld_w")
        ld_late = sem("ld_late")
        cst = sem("cst")
        blk = ctx.enter_context(nc.Block())

        col = lambda i: cols[:, i:i + 1]
        batch = lambda t, n, i: t[:, bass.ds(i * n, n)]

        N_LD, N_LATE = 16 * 20, 16 * 10

        colsT = sem("colsT")
        cols_ok = sem("cols_ok")
        bias_ok = sem("bias_ok")
        bn_ok = sem("bn_ok")
        st_ok = sem("st_ok")
        st_pool = sem("st_pool")
        e_mm = sem("e_mm")
        e_ev = sem("e_ev")
        r_mm = sem("r_mm")
        r_ev = sem("r_ev")

        @blk.sync
        def _(sp):
            xv = x.rearrange("b (t p) d -> p b t d", p=P)
            for i in range(B):
                sp.dma_start(x_all[:, i * TT:(i + 1) * TT, :], xv[:, i]).then_inc(ld_x[i], 16)
            rw = lambda a, n: a.rearrange("(c p) -> c p", p=P) if n else a
            sp.dma_start(gA[:, :, :], gens.rearrange("g r c -> r g c")).then_inc(ld_w, 16)
            sp.dma_start(rows[ROW_B:ROW_B + 3, :], rw(b, 3)).then_inc(ld_w, 16)
            sp.dma_start(rows[ROW_G:ROW_G + 1, :], rw(ln_g, 1)).then_inc(ld_w, 16)
            sp.dma_start(rows[ROW_LB:ROW_LB + 1, :], rw(ln_b, 1)).then_inc(ld_w, 16)
            sp.dma_start(rows[ROW_AB1:ROW_AB1 + AC, :], rw(ab1, AC)).then_inc(ld_w, 16)
            sp.dma_start(rows[ROW_EB1:ROW_EB1 + E0 * EC, :],
                         eb1.rearrange("e (c p) -> (e c) p", p=P)).then_inc(ld_w, 16)
            sp.dma_start(rows[ROW_B1:ROWS, :], b1.rearrange("e (c p) -> (e c) p", p=P)).then_inc(ld_w, 16)
            sp.dma_start(w_qkv[:, :], W).then_inc(ld_w, 16)
            sp.dma_start(bv_bc[:, :], b[2 * D:3 * D].partition_broadcast(P)).then_inc(ld_w, 16)
            sp.dma_start(w_a1[:, :], aw1).then_inc(ld_w, 16)
            sp.dma_start(w_a2[:, :, :], aw2.rearrange("(c p) d -> p c d", p=P)).then_inc(ld_w, 16)
            sp.dma_start(ab2_bc[:, :], ab2.partition_broadcast(P)).then_inc(ld_w, 16)
            sp.dma_start(w_gate[:, :], gate_w).then_inc(ld_w, 16)
            sp.dma_start(gate_bc[:, :], gate_b.rearrange("(e a) -> e a", a=1)).then_inc(ld_w, 16)
            sp.dma_start(w_e1[:, :, :], ew1.rearrange("e d h -> d e h")).then_inc(ld_w, 16)
            sp.dma_start(w_e2[:, :, :], ew2.rearrange("e (c p) d -> p (e c) d", p=P)).then_inc(ld_w, 16)
            sp.dma_start(eb2_sb[:, :], eb2).then_inc(ld_w, 16)
            sp.dma_start(gc_bc[:, 0, :], gc_w[0:D, :].rearrange("d a -> (d a)").partition_broadcast(P)).then_inc(ld_w, 16)
            sp.dma_start(gc_bc[:, 1, :], gc_w[D:2 * D, :].rearrange("d a -> (d a)").partition_broadcast(P)).then_inc(ld_w, 16)
            sp.dma_start(gcb_bc[:, :], gc_b.partition_broadcast(P)).then_inc(ld_w, 16)
            for m, src in ((mq_d, Mq), (mk_d, Mk)):
                for c in range(2):
                    sp.dma_start(m[:, :, c, :], src.rearrange("d (r k) -> d r k", k=KS)).then_inc(ld_late, 16)
            sp.dma_start(mv[:, :], Mv).then_inc(ld_late, 16)
            sp.dma_start(wg[:, :], Wg).then_inc(ld_late, 16)
            sp.dma_start(bg_c[:, :], bg.rearrange("(e a) -> e a", a=1)).then_inc(ld_late, 16)
            sp.dma_start(w_1[:, :, :], W1.rearrange("e d h -> d e h")).then_inc(ld_late, 16)
            sp.dma_start(w_2[:, :, :], W2.rearrange("e (c p) d -> p (e c) d", p=P)).then_inc(ld_late, 16)
            sp.dma_start(b2_sb[:, :], b2).then_inc(ld_late, 16)

        @blk.gpsimd
        def _(pool):
            pool.memset(ident[:, :], 0.0).then_inc(cst, 1)
            pool.memset(cmask[:, :], 0.0).then_inc(cst, 1)
            pool.memset(half_neg[:, :], -0.5).then_inc(cst, 1)
            for e in range(E1):
                pool.memset(rev[:, :, e:e + 1], float(E1 - e)).then_inc(cst, 1)
            pool.memset(lgT[:, :], 0.0).then_inc(cst, 1)
            pool.wait_ge(cst, 4 + E1)
            pool.affine_select(out=ident[:, :], in_=ident[:, :], compare_op=ALU.not_equal, fill=1.0,
                               base=0, pattern=[[-1, P]], channel_multiplier=1).then_inc(cst, 1)
            pool.affine_select(out=cmask[:, :], in_=cmask[:, :], compare_op=ALU.is_ge, fill=-9.0e15,
                               base=0, pattern=[[-1, P]], channel_multiplier=1).then_inc(cst, 1)
            pool.wait_ge(bn_ok, 1)
            n = [0]

            def step(ins):
                ins.then_inc(st_pool, 1)
                n[0] += 1
                pool.wait_ge(st_pool, n[0])

            var = mv_st[:, :, 1]
            step(pool.tensor_scalar(ve[:, :], var, EPS, None, ALU.add))
            step(pool.tensor_tensor(rs1[:, :], ve[:, :], half_neg[:, :], ALU.pow))
            step(pool.tensor_tensor(ve[:, :], rs1[:, :], rs1[:, :], ALU.mult))
            step(pool.tensor_tensor(ve[:, :], ve[:, :], var, ALU.mult))
            step(pool.tensor_scalar(ve[:, :], ve[:, :], EPS, None, ALU.add))
            pool.tensor_tensor(rs2[:, :], ve[:, :], half_neg[:, :], ALU.pow).then_inc(st_ok, 1)

        N_CST = 6 + E1

        @blk.tensor
        def _(pe):
            pe.wait_ge(cst, N_CST)
            pe.wait_ge(ld_w, N_LD)
            pe.transpose(psum[0][:, 0:ROWS], rows[:, :], ident[0:ROWS, 0:ROWS]).then_inc(colsT, 1)
            for g in range(G):
                mm = pe.transpose(psum[1][:, g * P:(g + 1) * P], gA[:, g, :], ident[:, :])
            mm.then_inc(e_mm, 1)
            for n in range(TAYLOR - 1):
                pe.wait_ge(e_ev, n + 1)
                for g in range(G):
                    mm = pe.matmul(psum[2][:, g * P:(g + 1) * P], gAT[:, g, :], gE[:, g, :], start=True, stop=True)
                mm.then_inc(e_mm, 1)
            pe.wait_ge(e_ev, TAYLOR)
            for g in range(G):
                mm = pe.transpose(psum[3][:, g * P:(g + 1) * P], gE[:, g, :], ident[:, :])
            mm.then_inc(e_mm, 1)
            for s in range(SQUARE):
                pe.wait_ge(e_ev, TAYLOR + 1 + s)
                for g in range(G):
                    pe.matmul(psum[2][:, g * P:(g + 1) * P], gET[:, g, :], gE[:, g, :], start=True, stop=True)
                for g in range(G):
                    mm = pe.matmul(psum[3][:, g * P:(g + 1) * P], gE[:, g, :], gET[:, g, :], start=True, stop=True)
                mm.then_inc(e_mm, 1)
            pe.wait_ge(e_ev, TAYLOR + 1 + SQUARE)
            for n, g in enumerate(range(G - 2, -1, -1)):
                if n:
                    pe.wait_ge(r_ev, n)
                pe.matmul(psum[4][:, 0:D], gET[:, g, :], gE[:, G - 1, :] if n == 0 else rot[:, :],
                          start=True, stop=True).then_inc(r_mm, 1)
            for q in range(E0 * EC // 4):
                for i in range(4):
                    mm = pe.transpose(psum[5 + q][:, i * P:(i + 1) * P], w_e2[:, 4 * q + i, :], ident[:, :])
            mm.then_inc(r_mm, 1)
            pe.transpose(psum[1][:, 0:E0], eb2_sb[:, :], ident[0:E0, 0:E0]).then_inc(r_mm, 1)
            pe.wait_ge(r_ev, G - 1 + 2)
            for q in range(E0 * EC // 4):
                for i in range(4):
                    mm = pe.matmul(psum[5 + q][:, i * P:(i + 1) * P], w_e2T[:, 4 * q + i, :], rot[:, :],
                                   start=True, stop=True)
            pe.matmul(psum[1][0:E0, 0:D], eb2T[:, :], rot[:, :], start=True, stop=True).then_inc(r_mm, 1)

        @blk.vector
        def _(dve):
            for i in range(B):
                dve.wait_ge(ld_x[i], 16)
                for t in range(i * TT, (i + 1) * TT):
                    dve.bn_stats(bn[:, t, :], x_all[:, t, :]).then_inc(bias_ok, 1)
            dve.wait_ge(bias_ok, NT)
            for t in range(NT):
                mm = dve.bn_aggr(mv_st[:, t, :], bn[:, t, :])
            mm.then_inc(bn_ok, 1)
            dve.wait_ge(colsT, 1)
            dve.tensor_copy(cols[:, :], psum[0][:, 0:ROWS]).then_inc(cols_ok, 1)
            dve.wait_ge(cols_ok, 1)
            dve.tensor_scalar(bqs[:, :], col(ROW_B), SC0, None, ALU.mult).then_inc(cols_ok, 1)
            dve.wait_ge(ld_w, N_LD)
            dve.tensor_scalar(gcb_half[:, :], gcb_bc[:, :], 0.5, None, ALU.mult).then_inc(cols_ok, 1)
            idb = ident[:, :].unsqueeze(1).broadcast_to([P, G, D])
            dve.wait_ge(e_mm, 1)
            dve.tensor_scalar(gAT[:, :, :], psum[1][:, :].rearrange("p (g d) -> p g d", g=G),
                              2.0 ** -SQUARE, None, ALU.mult).then_inc(cols_ok, 1)
            dve.scalar_tensor_tensor(gE[:, :, :], gA[:, :, :], 2.0 ** -SQUARE / TAYLOR, idb,
                                     ALU.mult, ALU.add).then_inc(cols_ok, 1)
            dve.wait_ge(cols_ok, 5)
            dve.engine_nop().then_inc(e_ev, 1)
            for n in range(TAYLOR - 1):
                dve.wait_ge(e_mm, n + 2)
                dve.scalar_tensor_tensor(gE[:, :, :], psum[2][:, :].rearrange("p (g d) -> p g d", g=G),
                                         1.0 / (TAYLOR - 1 - n), idb, ALU.mult, ALU.add).then_inc(e_ev, 1)
            dve.wait_ge(e_mm, TAYLOR + 1)
            dve.tensor_copy(gET[:, :, :], psum[3][:, :].rearrange("p (g d) -> p g d", g=G)).then_inc(e_ev, 1)
            for s in range(SQUARE):
                dve.wait_ge(e_mm, TAYLOR + 2 + s)
                dve.tensor_copy(gE[:, :, :], psum[2][:, :].rearrange("p (g d) -> p g d", g=G)).then_inc(cols_ok, 1)
                dve.tensor_copy(gET[:, :, :], psum[3][:, :].rearrange("p (g d) -> p g d", g=G)).then_inc(cols_ok, 1)
                dve.wait_ge(cols_ok, 5 + 2 * (s + 1))
                dve.engine_nop().then_inc(e_ev, 1)
            for n in range(G - 1):
                dve.wait_ge(r_mm, n + 1)
                dve.tensor_copy(rot[:, :], psum[4][:, 0:D]).then_inc(r_ev, 1)
            dve.wait_ge(r_mm, G)
            for q in range(E0 * EC // 4):
                mm = dve.tensor_copy(w_e2T[:, 4 * q:4 * q + 4, :],
                                     psum[5 + q][:, :].rearrange("p (i d) -> p i d", i=4))
            mm.then_inc(r_ev, 1)
            dve.wait_ge(r_mm, G + 1)
            dve.tensor_copy(eb2T[:, :], psum[1][:, 0:E0]).then_inc(r_ev, 1)
            dve.wait_ge(r_mm, G + 2)
            for q in range(E0 * EC // 4):
                dve.tensor_copy(w_e2[:, 4 * q:4 * q + 4, :],
                                psum[5 + q][:, :].rearrange("p (i d) -> p i d", i=4)).then_inc(r_ev, 1)
            dve.tensor_copy(eb2R[:, :], psum[1][0:E0, 0:D]).then_inc(r_ev, 1)

        N_REV = G + 1 + E0 * EC // 4 + 1

        xs = [sbe(f"xs{i}", [P, TT, D]) for i in range(2)]
        xh = [sbe(f"xh{i}", [P, TT, D]) for i in range(2)]
        xT = [sbe(f"xT{i}", [P, T]) for i in range(2)]
        qT = [sbe(f"qT{i}", [P, T]) for i in range(2)]
        kT = [sbe(f"kT{i}", [P, T]) for i in range(2)]
        va = [sbe(f"va{i}", [P, TT, D]) for i in range(2)]
        pr = [sbe(f"pr{i}", [P, T]) for i in range(2)]
        prT = [sbe(f"prT{i}", [P, T]) for i in range(2)]
        VBANK = (7, 3)
        nm0 = sbe("nm0", [P, 2])
        z0 = sbe("z0", [P, 2])
        rz0 = sbe("rz0", [P, 2])
        nms0 = sbe("nms0", [P, 2])
        a_xs = sem("a_xs")
        a_xh = sem("a_xh")
        a_keep = sem("a_keep")
        a_T = sem("a_T")
        a_xT = sem("a_xT")
        a_x2T = sem("a_x2T")
        a_qkv = sem("a_qkv")
        a_q = sem("a_q")
        a_v = sem("a_v")
        a_s = sem("a_s")
        a_dm = sem("a_dm")
        a_mx = sem("a_mx")
        a_nm = sem("a_nm")
        a_p = sem("a_p")
        a_rz = sem("a_rz")
        a_pT = sem("a_pT")
        a_pTs = sem("a_pTs")
        a_o = sem("a_o")
        a_os = sem("a_os")

        @blk.gpsimd
        def _(pool):
            with pool.Fori(0, LOOPS) as i:
                for par in range(2):
                    bt = 2 * i + par
                    pool.wait_ge(a_T, bt * 2 + 1)
                    for t in range(TT):
                        pool.wait_ge(a_xs, bt * TT + t + 1)
                        pool.tensor_tensor(xh[par][:, t, :], xs[par][:, t, :],
                                           rs2[:, bass.ds(bt * TT + t, 1)].broadcast_to([P, D]), ALU.mult)\
                            .then_inc(a_xh, 1)
                    pool.tensor_copy(xn_all[:, bass.ds(bt * TT, TT), :], xs[par][:, :, :]).then_inc(a_keep, 1)

        @blk.tensor
        def _(pe):
            pe.wait_ge(r_ev, N_REV)
            with pe.Fori(0, LOOPS) as i:
                for par in range(2):
                    bt = 2 * i + par
                    pe.wait_ge(a_xs, (bt + 1) * TT)
                    pe.wait_ge(a_xT, bt + 1)
                    for t in range(TT):
                        mm = pe.transpose(psum[0][:, t * P:(t + 1) * P], xs[par][:, t, :], ident[:, :])
                    mm.then_inc(a_T, 1)
                    pe.wait_ge(a_xh, (bt + 1) * TT)
                    pe.wait_ge(a_x2T, bt + 1)
                    for t in range(TT):
                        mm = pe.transpose(psum[1][:, t * P:(t + 1) * P], xh[par][:, t, :], ident[:, :])
                    mm.then_inc(a_T, 1)
                    pe.wait_ge(a_xT, bt + 2)
                    pe.wait_ge(a_v, bt + 1)
                    pe.matmul(psum[2][:, :], w_qkv[:, 0:D], xT[par][:, :], start=True, stop=True).then_inc(a_qkv, 1)
                    pe.wait_ge(a_os, bt * TT + 2)
                    pe.matmul(psum[3][:, :], w_qkv[:, D:2 * D], xT[par][:, :], start=True, stop=True).then_inc(a_qkv, 1)
                    pe.wait_ge(a_q, bt * 2 + 3)
                    for t in range(TT):
                        mm = pe.matmul(psum[2][:, t * P:(t + 1) * P], xT[par][:, t * P:(t + 1) * P],
                                       w_qkv[:, 2 * D:3 * D], start=True, stop=True)
                    mm.then_inc(a_qkv, 1)
                    pe.wait_ge(a_q, bt * 2 + 4)

                    def scores(t):
                        pe.wait_ge(a_p, bt * TT + t + 1)
                        pe.matmul(psum[4 + t % 2][:, 0:(t + 1) * P], qT[par][:, t * P:(t + 1) * P],
                                  kT[par][:, 0:(t + 1) * P], start=True, stop=True).then_inc(a_s, 1)

                    def turn(t):
                        pe.wait_ge(a_p, bt * TT + t + 3)
                        pe.wait_ge(a_pTs, bt * TT + t + 1)
                        for c in range(t + 1):
                            mm = pe.transpose(psum[6][:, c * P:(c + 1) * P], pr[t % 2][:, c * P:(c + 1) * P],
                                              ident[:, :])
                        mm.then_inc(a_pT, 1)

                    def values(t):
                        pe.wait_ge(a_pTs, bt * TT + t + 2)
                        if t == 0:
                            pe.wait_ge(a_v, bt + 2)
                        pe.wait_ge(a_os, bt * TT + t + 1)
                        for c in range(t + 1):
                            mm = pe.matmul(psum[VBANK[t % 2]][:, 0:P], prT[t % 2][:, c * P:(c + 1) * P],
                                           va[par][:, c, :], start=(c == 0), stop=(c == t))
                        mm.then_inc(a_o, 1)

                    scores(0)
                    scores(1)
                    turn(0)
                    scores(2)
                    turn(1)
                    values(0)
                    scores(3)
                    turn(2)
                    values(1)
                    turn(3)
                    values(2)
                    values(3)

        @blk.scalar
        def _(act):
            act.sem_inc(a_xT, 1)
            act.sem_inc(a_q, 2)
            act.sem_inc(a_p, 2)
            act.wait_ge(cols_ok, 2)
            with act.Fori(0, LOOPS) as i:
                for par in range(2):
                    bt = 2 * i + par
                    act.wait_ge(a_T, bt * 2 + 1 + 4)
                    act.activation(xT[par][:, :], psum[0][:, :], ACT.Copy).then_inc(a_xT, 1)
                    act.wait_ge(a_qkv, bt * 3 + 1)
                    act.activation(qT[par][:, :], psum[2][:, :], ACT.Identity, bias=bqs[:, 0:1], scale=SC0)\
                        .then_inc(a_q, 1)
                    act.wait_ge(a_qkv, bt * 3 + 2)
                    act.activation(kT[par][:, :], psum[3][:, :], ACT.Identity, bias=col(ROW_B + 1), scale=1.0)\
                        .then_inc(a_q, 1)
                    for t in range(TT):
                        act.wait_ge(a_mx, bt * TT + t + 1)
                        act.wait_ge(a_pT, bt * TT + t + 1)
                        act.wait_ge(a_rz, bt * TT + t + 1)
                        act.activation(pr[t % 2][:, 0:(t + 1) * P], psum[4 + t % 2][:, 0:(t + 1) * P], ACT.Exp,
                                       bias=nm0[:, t % 2:t % 2 + 1], scale=1.0,
                                       accum_out=z0[:, t % 2:t % 2 + 1]).then_inc(a_p, 1)

        @blk.vector
        def _(dve):
            dve.sem_inc(a_T, 4)
            dve.sem_inc(a_x2T, 1)
            dve.sem_inc(a_v, 1)
            dve.sem_inc(a_pT, 2)
            dve.sem_inc(a_rz, 2)
            dve.sem_inc(a_pTs, 1)
            dve.sem_inc(a_os, 2)
            dve.wait_ge(st_ok, 1)
            with dve.Fori(0, LOOPS) as i:
                for par in range(2):
                    bt = 2 * i + par
                    dve.wait_ge(a_T, bt * 2 + 1)
                    dve.wait_ge(a_keep, bt + 1)
                    for t in range(TT):
                        g = bt * TT + t
                        dve.tensor_scalar(xs[par][:, t, :], x_all[:, bass.ds(g, 1), :].rearrange("p a d -> p (a d)"),
                                          mv_st[:, bass.ds(g, 1), 0], rs1[:, bass.ds(g, 1)],
                                          ALU.subtract, ALU.mult).then_inc(a_xs, 1)
                    dve.wait_ge(a_T, bt * 2 + 2 + 4)
                    dve.tensor_scalar(xn2T[:, bass.ds(bt * T, T)], psum[1][:, :], col(ROW_G), col(ROW_LB),
                                      ALU.mult, ALU.add).then_inc(a_x2T, 1)
                    dve.wait_ge(a_qkv, bt * 3 + 3)
                    dve.tensor_tensor(va[par][:, :, :], psum[2][:, :].rearrange("p (t d) -> p t d", t=TT),
                                      bv_bc[:, :].unsqueeze(1).broadcast_to([P, TT, D]), ALU.add).then_inc(a_v, 1)

                    def top(t):
                        s = psum[4 + t % 2]
                        dve.wait_ge(a_s, bt * TT + t + 1)
                        dve.tensor_tensor(s[:, t * P:(t + 1) * P], s[:, t * P:(t + 1) * P], cmask[:, :],
                                          ALU.add).then_inc(a_dm, 1)
                        dve.wait_ge(a_dm, bt * TT + t + 1)
                        dve.wait_ge(a_p, bt * TT + t + 1)
                        dve.tensor_reduce(nm0[:, t % 2:t % 2 + 1], s[:, 0:(t + 1) * P], AX.X, ALU.max,
                                          negate=True).then_inc(a_mx, 1)

                    def store_turned(t):
                        dve.wait_ge(a_pT, bt * TT + t + 3)
                        dve.wait_ge(a_o, bt * TT + t + 1)
                        dve.tensor_copy(prT[t % 2][:, 0:(t + 1) * P], psum[6][:, 0:(t + 1) * P]).then_inc(a_pTs, 1)
                        dve.reciprocal(rz0[:, t % 2:t % 2 + 1], z0[:, t % 2:t % 2 + 1]).then_inc(a_rz, 1)

                    def store_values(t):
                        dve.wait_ge(a_rz, bt * TT + t + 3)
                        dve.wait_ge(a_o, bt * TT + t + 3)
                        dve.tensor_scalar(s_all[:, bass.ds(bt * TT + t, 1), :].rearrange("p a d -> p (a d)"),
                                          psum[VBANK[t % 2]][:, 0:P], rz0[:, t % 2:t % 2 + 1], None,
                                          ALU.mult).then_inc(a_os, 1)

                    top(0)
                    top(1)
                    store_turned(0)
                    top(2)
                    store_turned(1)
                    store_values(0)
                    top(3)
                    store_values(1)
                    store_turned(2)
                    store_turned(3)
                    store_values(2)
                    store_values(3)

        @blk.sync
        def _(sp):
            sp.sem_inc(a_keep, 2)
            sp.sem_inc(a_o, 2)

        NU = 4
        CH = AC + E0 * EC
        hid = [sbe(f"hid{i}", [P, T]) for i in range(NU)]
        lg = sbe("lg", [P, TT, E1])
        lg0, oh1, oh2, tie, wf = (sbe(n, [P, TT, E0]) for n in ("lg0", "oh1", "oh2", "tie", "wf"))
        m1, m2, dm, th, w1t, w2t, gz, gt = (sbe(n, [P, TT]) for n in ("m1", "m2", "dm", "th", "w1t", "w2t", "gz", "gt"))
        wT = sbe("wT", [E1, T])
        acc, abel, ta, tb, tanh_r = (sbe(n, [P, TT, D]) for n in ("acc", "abel", "ta", "tb", "tanh_r"))
        f_lg = sem("f_lg")
        f_lgs = sem("f_lgs")
        f_c = sem("f_c")
        f_dm = sem("f_dm")
        f_th = sem("f_th")
        f_w = sem("f_w")
        f_wT = sem("f_wT")
        f_wTs = sem("f_wTs")
        f_b = sem("f_b")
        f_ba = sem("f_ba")
        f_up = sem("f_up")
        f_h = sem("f_h")
        f_dn = sem("f_dn")
        f_ab = sem("f_ab")
        f_ea = sem("f_ea")
        f_gz = sem("f_gz")
        f_gt = sem("f_gt")
        f_r = sem("f_r")
        f_tr = sem("f_tr")
        f_x1 = sem("f_x1")

        @blk.tensor
        def _(pe):
            pe.wait_ge(a_os, B * TT + 2)
            pe.wait_ge(a_x2T, B + 1)
            with pe.Fori(0, B) as bt:
                xb = xn2T[:, bass.ds(bt * T, T)]

                def up(n):
                    pe.wait_ge(f_h, bt * CH + n + 1)
                    w = w_a1[:, n * P:(n + 1) * P] if n < AC else \
                        w_e1[:, (n - AC) // EC, (n - AC) % EC * P:((n - AC) % EC + 1) * P]
                    pe.matmul(psum[n % NU][:, :], w, xb, start=True, stop=True).then_inc(f_up, 1)

                def down(n):
                    pe.wait_ge(f_h, bt * CH + n + 1 + NU)
                    if n < AC:
                        dst, w, first, last = psum[4], w_a2[:, n, :], n == 0, n == AC - 1
                        if first:
                            pe.wait_ge(f_ab, bt + 1)
                    else:
                        e, c = (n - AC) // EC, (n - AC) % EC
                        dst, w, first, last = psum[5 + e % 2], w_e2[:, n - AC, :], c == 0, c == EC - 1
                        if first:
                            pe.wait_ge(f_ea, bt * E0 + e + 1)
                    for t in range(TT):
                        mm = pe.matmul(dst[:, t * P:(t + 1) * P], hid[n % NU][:, t * P:(t + 1) * P], w,
                                       start=(first and t == 0), stop=last, skip_group_check=True)
                    mm.then_inc(f_dn, 1)

                pe.wait_ge(f_ba, bt + 1)
                pe.matmul(psum[7][0:E0, :], w_gate[:, :], xb, start=True, stop=True).then_inc(f_lg, 1)
                up(0)
                up(1)
                pe.wait_ge(f_lgs, bt + 1)
                for t in range(TT):
                    mm = pe.transpose(psum[7][:, t * P:(t + 1) * P], lgT[:, t * P:(t + 1) * P], ident[:, :])
                mm.then_inc(f_lg, 1)
                for n in range(CH):
                    if n + 2 < CH:
                        up(n + 2)
                    down(n)
                    if n == 6:
                        pe.wait_ge(f_w, bt + 1)
                        for t in range(TT):
                            mm = pe.transpose(psum[7][0:E0, t * P:(t + 1) * P], wf[:, t, :], ident[:, :])
                        mm.then_inc(f_wT, 1)
                    if n == 7:
                        pe.wait_ge(f_wTs, bt + 1)
                        for t in range(TT):
                            mm = pe.matmul(psum[7][:, t * P:(t + 1) * P], wT[0:E0, t * P:(t + 1) * P], eb2R[:, :],
                                           start=True, stop=True)
                        mm.then_inc(f_b, 1)

        @blk.scalar
        def _(act):
            act.sem_inc(f_h, NU)
            act.wait_ge(cols_ok, 3)

            def gate_tanh(bt):
                act.wait_ge(f_gz, bt + 1)
                act.activation(gt[:, :], gz[:, :], ACT.Tanh, bias=gcb_half[:, 0:1], scale=0.5).then_inc(f_gt, 1)

            def silu_tanh(bt):
                act.wait_ge(f_r, bt + 1)
                act.activation(tanh_r[:, :, :], ta[:, :, :], ACT.Tanh, scale=0.5).then_inc(f_tr, 1)

            def chunks(bt, follow):
                for n in range(CH):
                    act.wait_ge(f_up, bt * CH + n + 1)
                    act.wait_ge(f_dn, bt * CH + n + 1)
                    act.activation(hid[n % NU][:, :], psum[n % NU][:, :], ACT.Gelu,
                                   bias=col((ROW_AB1 if n < AC else ROW_EB1 - AC) + n), scale=1.0).then_inc(f_h, 1)
                    if n == 0 and follow:
                        gate_tanh(bt - 1)
                    if n == 3:
                        act.wait_ge(f_dm, bt + 1)
                        act.activation(th[:, :], dm[:, :], ACT.Tanh, scale=0.5).then_inc(f_th, 1)
                    if n == 5 and follow:
                        silu_tanh(bt - 1)

            chunks(0, False)
            with act.Fori(1, B) as bt:
                chunks(bt, True)
            gate_tanh(B - 1)
            silu_tanh(B - 1)

        @blk.vector
        def _(dve):
            dve.sem_inc(f_dn, NU)
            dve.sem_inc(f_ab, 1)
            dve.sem_inc(f_ba, 1)
            dve.sem_inc(f_ea, 2)
            dve.wait_ge(a_keep, B + 2)
            b3 = lambda a: a.unsqueeze(2).broadcast_to([P, TT, E0])
            STEPS_R, STEPS_E, STEPS_Z = 11, E0 * TT, 4
            STEPS_G, STEPS_F = TT + 1, 3

            def chain(base):
                k = [0]

                def step(ins, last=False):
                    ins.then_inc(f_c, 1)
                    k[0] += 1
                    dve.wait_ge(f_c, base + k[0])
                return step, k

            def gate_mix(bt, step):
                dve.wait_ge(f_gt, bt + 1)
                step(dve.tensor_scalar(gt[:, :], gt[:, :], 0.5, 0.5, ALU.mult, ALU.add))
                for t in range(TT):
                    step(dve.scalar_tensor_tensor(ta[:, t, :], tb[:, t, :], gt[:, t:t + 1], abel[:, t, :],
                                                  ALU.mult, ALU.add))
                dve.tensor_tensor(ta[:, :, :], ta[:, :, :], xn_all[:, bass.ds(bt * TT, TT), :], ALU.add)\
                   .then_inc(f_r, 1)

            def finish(bt, step):
                dve.wait_ge(f_tr, bt + 1)
                step(dve.scalar_tensor_tensor(ta[:, :, :], tanh_r[:, :, :], 1.0, ta[:, :, :], ALU.add, ALU.mult))
                step(dve.scalar_tensor_tensor(ta[:, :, :], ta[:, :, :], 0.5, s_all[:, bass.ds(bt * TT, TT), :],
                                              ALU.mult, ALU.mult))
                xb = x_all[:, bass.ds(bt * TT, TT), :]
                dve.tensor_tensor(xb, xb, ta[:, :, :], ALU.add).then_inc(f_x1, 1)

            def batch_steps(bt, base, follow):
                step, k = chain(base)
                dve.wait_ge(f_lg, bt * 2 + 1)
                dve.tensor_scalar(lgT[0:E0, :], psum[7][0:E0, :], gate_bc[:, 0:1], None, ALU.add).then_inc(f_lgs, 1)
                dve.wait_ge(f_lg, bt * 2 + 2)
                step(dve.tensor_copy(lg0[:, :, :], psum[7][:, :].rearrange("p (t q) -> p t q", t=TT)[:, :, 0:E0]))

                def best(scores, m, oh):
                    step(dve.tensor_reduce(m[:, :], scores, AX.X, ALU.max))
                    step(dve.tensor_tensor(tie[:, :, :], scores, b3(m[:, :]), ALU.is_equal))
                    step(dve.tensor_tensor(tie[:, :, :], tie[:, :, :], rev[:, :, 0:E0], ALU.mult))
                    step(dve.tensor_reduce(w1t[:, :], tie[:, :, :], AX.X, ALU.max))
                    step(dve.tensor_tensor(oh[:, :, :], tie[:, :, :], b3(w1t[:, :]), ALU.is_equal))

                best(lg0[:, :, :], m1, oh1)
                step(dve.scalar_tensor_tensor(lg0[:, :, :], oh1[:, :, :], -BIG, lg0[:, :, :], ALU.mult, ALU.add))
                best(lg0[:, :, :], m2, oh2)
                dve.tensor_tensor(dm[:, :], m2[:, :], m1[:, :], ALU.subtract).then_inc(f_dm, 1)
                if follow:
                    gate_mix(bt - 1, step)
                dve.wait_ge(f_th, bt + 1)
                step(dve.tensor_scalar(w2t[:, :], th[:, :], 0.5, 0.5, ALU.mult, ALU.add))
                step(dve.tensor_scalar(w1t[:, :], th[:, :], -0.5, 0.5, ALU.mult, ALU.add))
                step(dve.tensor_tensor(oh1[:, :, :], oh1[:, :, :], b3(w1t[:, :]), ALU.mult))
                step(dve.tensor_tensor(oh2[:, :, :], oh2[:, :, :], b3(w2t[:, :]), ALU.mult))
                dve.tensor_tensor(wf[:, :, :], oh1[:, :, :], oh2[:, :, :], ALU.add).then_inc(f_w, 1)
                if follow:
                    finish(bt - 1, step)
                dve.wait_ge(f_wT, bt + 1)
                dve.tensor_copy(wT[0:E0, :], psum[7][0:E0, :]).then_inc(f_wTs, 1)
                dve.wait_ge(f_dn, bt * CH + AC + NU)
                dve.tensor_tensor(abel[:, :, :], psum[4][:, :].rearrange("p (t d) -> p t d", t=TT),
                                  ab2_bc[:, :].unsqueeze(1).broadcast_to([P, TT, D]), ALU.add).then_inc(f_ab, 1)
                dve.wait_ge(f_b, bt + 1)
                dve.tensor_copy(acc[:, :, :], psum[7][:, :].rearrange("p (t d) -> p t d", t=TT)).then_inc(f_ba, 1)
                dve.wait_ge(f_ba, bt + 2)
                for e in range(E0):
                    dve.wait_ge(f_dn, bt * CH + AC + (e + 1) * EC + NU)
                    if e:
                        dve.wait_ge(f_ea, bt * E0 + e + 2)
                    for t in range(TT):
                        ins = dve.scalar_tensor_tensor(acc[:, t, :], psum[5 + e % 2][:, t * P:(t + 1) * P],
                                                       wf[:, t, e:e + 1], acc[:, t, :], ALU.mult, ALU.add)
                    ins.then_inc(f_ea, 1)
                dve.wait_ge(f_ea, bt * E0 + E0 + 2)
                step(dve.tensor_tensor(ta[:, :, :], abel[:, :, :],
                                       gc_bc[:, 0:1, :].broadcast_to([P, TT, D]), ALU.mult))
                step(dve.tensor_tensor(tb[:, :, :], acc[:, :, :],
                                       gc_bc[:, 1:2, :].broadcast_to([P, TT, D]), ALU.mult))
                step(dve.tensor_tensor(ta[:, :, :], ta[:, :, :], tb[:, :, :], ALU.add))
                step(dve.tensor_tensor(tb[:, :, :], acc[:, :, :], abel[:, :, :], ALU.subtract))
                dve.tensor_reduce(gz[:, :], ta[:, :, :], AX.X, ALU.add).then_inc(f_gz, 1)
                return k[0]

            first = batch_steps(0, 0, False)
            per = first + STEPS_G + STEPS_F - 1
            with dve.Fori(1, B) as bt:
                assert batch_steps(bt, bt * per + (first - per), True) == per
            step, _ = chain(first + (B - 1) * per)
            gate_mix(B - 1, step)
            finish(B - 1, step)

        early.close()
        NS = 4
        ST = HEADS * TT
        U_T, U_LG, U_V, U_LGT, U_OHT, U_B2, U_QK = 0, 1, 2, 4, 5, 6, 8
        U_S = U_QK + 2 * HEADS
        FFN = E1 * HC
        qh = sb("qh", [P, HEADS, T], F32R)
        ql = sb("ql", [P, HEADS, T], F32R)
        kk = sb("kk", [P, HEADS, HEADS, HT], F32R)
        vt = sb("vt", [P, TT, HEADS, VD])
        PB = 4
        pb = [sb(f"pb{i}", [P, T]) for i in range(PB)]
        vs = [sb(f"vs{i}", [P, D]) for i in range(PB)]
        nmx, zz, rz = (sb(n, [P, PB]) for n in ("nmx", "zz", "rz"))
        xs3 = sb("xs3", [P, TT, D])
        xd = sb("xd", [P, HEADS, 2, HT])
        x1T = xd[:, :, 0, :]
        oh, sc3, tie3 = (sb(n, [P, TT, E1]) for n in ("oh", "sc3", "tie3"))
        mm3, mt3 = (sb(n, [P, TT]) for n in ("mm3", "mt3"))
        ohT = sb("ohT", [E1, T])
        ya, s1, th3, ob = (sb(n, [P, TT, D]) for n in ("ya", "s1", "th3", "ob"))
        NH = 4
        hd = [sb(f"hd{i}", [P, T]) for i in range(NH)]
        bn3 = sb("bn3", [P, TT, 6])
        mv3 = sb("mv3", [P, TT, 2])
        ve3, r3 = (sb(n, [P, TT]) for n in ("ve3", "r3"))

        n_c = sem("n_c")
        n_v = sem("n_v")
        n_r = sem("n_r")
        n_xs = sem("n_xs")
        n_T = sem("n_T")
        n_xT = sem("n_xT")
        n_lg = sem("n_lg")
        n_lgs = sem("n_lgs")
        n_oh = sem("n_oh")
        n_V = sem("n_V")
        n_Vs = sem("n_Vs")
        n_qk = sem("n_qk")
        n_hi = sem("n_hi")
        n_lo = sem("n_lo")
        n_s = sem("n_s")
        n_mx = sem("n_mx")
        n_e = sem("n_e")
        n_rz = sem("n_rz")
        n_vs = sem("n_vs")
        n_av = sem("n_av")
        n_s1 = sem("n_s1")
        n_up = sem("n_up")
        n_h = sem("n_h")
        n_dn = sem("n_dn")
        n_y = sem("n_y")
        n_th = sem("n_th")
        n_o = sem("n_o")
        n_st = sem("n_st")

        def ring_free(eng, bt, use):
            u = use - NS
            if u < 0:
                eng.wait_ge(n_e, bt * ST + NS)
            elif u == U_T:
                eng.wait_ge(n_xT, bt + 1)
            elif u == U_LG:
                eng.wait_ge(n_lgs, bt * 4 + 1)
            elif u < U_LGT:
                eng.wait_ge(n_Vs, bt * 2 + u - U_V + 1)
            elif u <= U_B2:
                eng.wait_ge(n_lgs, bt * 4 + u - U_LGT + 2)
            elif u < U_QK:
                eng.wait_ge(n_Vs, bt * 2 + 2)
            elif u < U_S:
                eng.wait_ge(n_lo, bt * 2 * HEADS + u - U_QK + 1)
            else:
                eng.wait_ge(n_e, bt * ST + u - U_S + 1 + NS)

        @blk.gpsimd
        def _(pool):
            pool.wait_ge(f_x1, B)
            pool.wait_ge(f_dn, B * CH + NU)
            with pool.Fori(0, B) as bt:
                pool.wait_ge(n_v, bt + 1)
                pool.tensor_tensor(r3[:, :], ve3[:, :], half_neg[:, 0:TT], ALU.pow).then_inc(n_r, 1)
                for n in range(ST):
                    if n == 0:
                        pool.wait_ge(n_Vs, bt * 2 + 2)
                    pool.wait_ge(n_rz, bt * ST + n + 1)
                    pool.wait_ge(n_av, bt * ST + n + 1)
                    pool.tensor_tensor(vs[n % PB][:, :], vt[:, n % TT, :, :].rearrange("p j d -> p (j d)"),
                                       rz[:, n % PB:n % PB + 1].broadcast_to([P, D]), ALU.mult).then_inc(n_vs, 1)

        @blk.tensor
        def _(pe):
            pe.wait_ge(ld_late, N_LATE)
            pe.wait_ge(f_ea, B * E0 + 2)
            with pe.Fori(0, B) as bt:
                ring_free(pe, bt, U_T)
                pe.wait_ge(n_xs, bt + 1)
                for t in range(TT):
                    mm = pe.transpose(psum[U_T % NS][:, t * P:(t + 1) * P], xs3[:, t, :], ident[:, :])
                mm.then_inc(n_T, 1)
                pe.wait_ge(n_xT, bt + 1)
                ring_free(pe, bt, U_LG)
                pe.matmul(psum[U_LG % NS][0:E1, :], wg[:, :], x1T, start=True, stop=True).then_inc(n_lg, 1)
                for j in range(HEADS):
                    if j % 4 == 0:
                        ring_free(pe, bt, U_V + j // 4)
                    mm = pe.matmul(psum[(U_V + j // 4) % NS][:, j % 4 * P:(j % 4 + 1) * P],
                                   xd[:, j, :, :].rearrange("p a k -> p (a k)"),
                                   mv[:, :], start=True, stop=True)
                    if j % 4 == 3:
                        mm.then_inc(n_V, 1)
                pe.wait_ge(n_lgs, bt * 4 + 1)
                ring_free(pe, bt, U_LGT)
                for t in range(TT):
                    mm = pe.transpose(psum[U_LGT % NS][:, t * P:(t + 1) * P], lgT[:, t * P:(t + 1) * P], ident[:, :])
                mm.then_inc(n_lg, 1)
                pe.wait_ge(n_oh, bt + 1)
                ring_free(pe, bt, U_OHT)
                for t in range(TT):
                    mm = pe.transpose(psum[U_OHT % NS][0:E1, t * P:(t + 1) * P], oh[:, t, :], ident[:, :])
                mm.then_inc(n_lg, 1)
                pe.wait_ge(n_lgs, bt * 4 + 3)
                for t in range(TT):
                    mm = pe.matmul(psum[U_B2 % NS][:, t * P:(t + 1) * P], ohT[:, t * P:(t + 1) * P], b2_sb[:, :],
                                   start=True, stop=True)
                mm.then_inc(n_lg, 1)
                for u in range(2 * HEADS):
                    w = (mq_d, mk_d)[u % 2]
                    ring_free(pe, bt, U_QK + u)
                    pe.matmul(psum[(U_QK + u) % NS][:, :], w[:, u // 2, :, :].rearrange("p a k -> p (a k)"), x1T,
                              start=True, stop=True).then_inc(n_qk, 1)

                def score(n):
                    h, m = n // TT, n % TT
                    if n == 0:
                        pe.wait_ge(n_lo, (bt + 1) * 2 * HEADS)
                    ring_free(pe, bt, U_S + n)
                    keys = kk[:, h, 2 * m:2 * m + 2, :].rearrange("p a k -> p (a k)")
                    for i, q in enumerate((qh, ql)):
                        mm = pe.matmul(psum[(U_S + n) % NS][:, :], keys, q[:, :, h * HT:(h + 1) * HT],
                                       start=(i == 0), stop=(i == 1))
                    mm.then_inc(n_s, 1)

                def value(n):
                    h, m = n // TT, n % TT
                    pe.wait_ge(n_vs, bt * ST + n + 1 + PB)
                    if n % (4 * TT) == 0:
                        pe.wait_ge(n_s1, bt * (HEADS // 4) + h // 4 + 1)
                    for c in range(TT):
                        o = h % 4 * P + c * 2 * VD
                        mm = pe.matmul(psum[7][:, o:o + 2 * VD], pb[n % PB][:, c * P:(c + 1) * P],
                                       vs[n % PB][:, c * 2 * VD:(c + 1) * 2 * VD],
                                       start=(n % (4 * TT) == 0 and c == 0), stop=(m == TT - 1), skip_group_check=True)
                    mm.then_inc(n_av, 1)

                def up(n):
                    pe.wait_ge(n_h, bt * FFN + n + 1)
                    pe.matmul(psum[4 + n % 2][:, :], w_1[:, n // HC, n % HC * P:(n % HC + 1) * P], x1T,
                              start=True, stop=True).then_inc(n_up, 1)

                def down(n):
                    pe.wait_ge(n_h, bt * FFN + n + 1 + 2)
                    if n % HC == 0:
                        pe.wait_ge(n_y, bt * E1 + n // HC + 1)
                    for t in range(TT):
                        mm = pe.matmul(psum[6][:, t * P:(t + 1) * P], hd[n % NH][:, t * P:(t + 1) * P], w_2[:, n, :],
                                       start=(n % HC == 0 and t == 0), stop=(n % HC == HC - 1), skip_group_check=True)
                    mm.then_inc(n_dn, 1)

                for n in range(ST + 2):
                    if n < ST:
                        score(n)
                        up(n)
                    if 1 <= n <= FFN:
                        down(n - 1)
                    if n >= 2:
                        value(n - 2)

        @blk.scalar
        def _(act):
            act.sem_inc(n_e, NS)
            act.sem_inc(n_h, 2)
            act.wait_ge(f_x1, B)
            act.wait_ge(f_dn, B * CH + NU)
            with act.Fori(0, B) as bt:
                act.wait_ge(n_T, bt + 1)
                act.activation(xd[:, :, :, :], psum[U_T % NS][:, :].rearrange("p (j k) -> p j k", j=HEADS).unsqueeze(2)
                               .broadcast_to([P, HEADS, 2, HT]), ACT.Copy).then_inc(n_xT, 1)
                for u in range(2 * HEADS):
                    act.wait_ge(n_qk, bt * 2 * HEADS + u + 1)
                    bank = psum[(U_QK + u) % NS]
                    if u % 2 == 0:
                        ins = act.activation(qh[:, u // 2, :], bank[:, :], ACT.Copy, scale=SC1)
                    else:
                        ins = act.activation(kk[:, :, u // 2, :], bank[:, :].rearrange("p (h k) -> p h k", h=HEADS),
                                             ACT.Copy)
                    ins.then_inc(n_hi, 1)
                for n in range(ST):
                    act.wait_ge(n_mx, bt * ST + n + 1)
                    act.wait_ge(n_av, bt * ST + n + 1)
                    act.activation(pb[n % PB][:, :], psum[(U_S + n) % NS][:, :], ACT.Exp, bias=nmx[:, n % PB:n % PB + 1],
                                   scale=1.0, accum_out=zz[:, n % PB:n % PB + 1]).then_inc(n_e, 1)
                    act.wait_ge(n_up, bt * FFN + n + 1)
                    act.wait_ge(n_dn, bt * FFN + n + 1)
                    act.activation(hd[n % NH][:, :], psum[4 + n % 2][:, :], ACT.Relu, bias=col(ROW_B1 + n), scale=1.0)\
                       .then_inc(n_h, 1)
                act.wait_ge(n_y, bt * E1 + E1 + 1)
                act.activation(th3[:, :, :], ya[:, :, :], ACT.Tanh, scale=0.5).then_inc(n_th, 1)

        @blk.vector
        def _(dve):
            dve.sem_inc(n_av, PB)
            dve.sem_inc(n_s1, 1)
            dve.sem_inc(n_y, 1)
            dve.sem_inc(n_dn, NH)
            dve.wait_ge(f_dn, B * CH + NU)
            PER = 8
            with dve.Fori(0, B) as bt:
                count = [0]

                def step(ins):
                    ins.then_inc(n_c, 1)
                    count[0] += 1
                    dve.wait_ge(n_c, bt * PER + count[0])

                xb = lambda t: x_all[:, bass.ds(bt * TT + t, 1), :].rearrange("p a d -> p (a d)")
                for t in range(TT):
                    ins = dve.bn_stats(bn3[:, t, :], xb(t))
                step(ins)
                dve.memset(ve3[:, :], EPS)
                for t in range(TT):
                    ins = dve.bn_aggr(mv3[:, t, :], bn3[:, t, :])
                step(ins)
                dve.tensor_tensor(ve3[:, :], ve3[:, :], mv3[:, :, 1], ALU.add).then_inc(n_v, 1)
                dve.wait_ge(n_r, bt + 1)
                for t in range(TT):
                    ins = dve.tensor_scalar(xs3[:, t, :], xb(t), mv3[:, t, 0:1], r3[:, t:t + 1],
                                            ALU.subtract, ALU.mult)
                ins.then_inc(n_xs, 1)
                dve.wait_ge(n_lg, bt * 4 + 1)
                dve.tensor_scalar(lgT[0:E1, :], psum[U_LG % NS][0:E1, :], bg_c[:, 0:1], None, ALU.add).then_inc(n_lgs, 1)
                for i in range(2):
                    dve.wait_ge(n_V, bt * 2 + i + 1)
                    src = psum[(U_V + i) % NS][:, :].rearrange("p (j m r d) -> p m j r d", j=4, m=TT, r=2)
                    for r in range(2):
                        ins = dve.tensor_copy(vt[r * HT:(r + 1) * HT, :, 4 * i:4 * i + 4, :],
                                              src[r * HT:(r + 1) * HT, :, :, r, :])
                    ins.then_inc(n_Vs, 1)
                dve.wait_ge(n_lg, bt * 4 + 2)
                sc = psum[U_LGT % NS][:, :].rearrange("p (t q) -> p t q", t=TT)[:, :, 0:E1]
                b3 = lambda a: a.unsqueeze(2).broadcast_to([P, TT, E1])
                dve.tensor_copy(sc3[:, :, :], sc).then_inc(n_lgs, 1)
                dve.wait_ge(n_lgs, bt * 4 + 2)
                step(dve.tensor_reduce(mm3[:, :], sc3[:, :, :], AX.X, ALU.max))
                step(dve.tensor_tensor(tie3[:, :, :], sc3[:, :, :], b3(mm3[:, :]), ALU.is_equal))
                step(dve.tensor_tensor(tie3[:, :, :], tie3[:, :, :], rev[:, :, :], ALU.mult))
                step(dve.tensor_reduce(mt3[:, :], tie3[:, :, :], AX.X, ALU.max))
                dve.tensor_tensor(oh[:, :, :], tie3[:, :, :], b3(mt3[:, :]), ALU.is_equal).then_inc(n_oh, 1)
                dve.wait_ge(n_lg, bt * 4 + 3)
                dve.tensor_copy(ohT[:, :], psum[U_OHT % NS][0:E1, :]).then_inc(n_lgs, 1)
                dve.wait_ge(n_lg, bt * 4 + 4)
                dve.tensor_copy(ya[:, :, :], psum[U_B2 % NS][:, :].rearrange("p (t d) -> p t d", t=TT)).then_inc(n_lgs, 1)
                for u in range(2 * HEADS):
                    dve.wait_ge(n_hi, bt * 2 * HEADS + u + 1)
                    bank = psum[(U_QK + u) % NS]
                    if u % 2 == 0:
                        ins = dve.scalar_tensor_tensor(ql[:, u // 2, :], bank[:, :], SC1, qh[:, u // 2, :].bitcast(F32),
                                                       ALU.mult, ALU.subtract)
                    else:
                        low = kk[KS:P, :, u // 2, :]
                        ins = dve.tensor_tensor(low, bank[KS:P, :].rearrange("p (h k) -> p h k", h=HEADS), low.bitcast(F32), ALU.subtract)
                    ins.then_inc(n_lo, 1)

                def maxima(n):
                    dve.wait_ge(n_s, bt * ST + n + 1)
                    dve.wait_ge(n_e, bt * ST + n + 1)
                    dve.tensor_reduce(nmx[:, n % PB:n % PB + 1], psum[(U_S + n) % NS][:, :], AX.X, ALU.max,
                                      negate=True).then_inc(n_mx, 1)

                def inverse(n):
                    dve.wait_ge(n_e, bt * ST + n + 1 + NS)
                    dve.wait_ge(n_vs, bt * ST + n + 1)
                    dve.reciprocal(rz[:, n % PB:n % PB + 1], zz[:, n % PB:n % PB + 1]).then_inc(n_rz, 1)

                def take_expert(e):
                    dve.wait_ge(n_dn, bt * FFN + (e + 1) * HC + NH)
                    dve.wait_ge(n_y, bt * E1 + e + 1)
                    for t in range(TT):
                        ins = dve.scalar_tensor_tensor(ya[:, t, :], psum[6][:, t * P:(t + 1) * P], oh[:, t, e:e + 1],
                                                       ya[:, t, :], ALU.mult, ALU.add)
                    ins.then_inc(n_y, 1)

                def take_heads(g):
                    dve.wait_ge(n_av, bt * ST + (g + 1) * 4 * TT + PB)
                    src = psum[7][:, :].rearrange("p (a b c j d) -> p b a c j d", a=2, b=2, c=TT, j=2)
                    for half in range(2):
                        for j in range(2):
                            ins = dve.tensor_copy(
                                s1[half * HT:(half + 1) * HT, 2 * g:2 * g + 2, :]
                                .rearrange("p a (c j d) -> p a c j d", c=TT, j=2)[:, :, :, j, :],
                                src[j * HT:(j + 1) * HT, half, :, :, j, :])
                    ins.then_inc(n_s1, 1)

                for n in range(ST + 4):
                    if n < ST:
                        maxima(n)
                    if 1 <= n <= ST:
                        inverse(n - 1)
                    if n >= 5 and (n - 5) % HC == 0:
                        take_expert((n - 5) // HC)
                    if n == 4 * TT + 1:
                        take_heads(0)
                take_heads(1)
                dve.wait_ge(n_th, bt + 1)
                dve.wait_ge(n_s1, bt * 2 + 3)
                dve.wait_ge(n_st, bt * 16 + 16)
                step(dve.scalar_tensor_tensor(ya[:, :, :], th3[:, :, :], 1.0, ya[:, :, :], ALU.add, ALU.mult))
                step(dve.scalar_tensor_tensor(ob[:, :, :], ya[:, :, :], 0.5, s1[:, :, :], ALU.mult, ALU.mult))
                dve.tensor_tensor(ob[:, :, :], ob[:, :, :], x_all[:, bass.ds(bt * TT, TT), :], ALU.add).then_inc(n_o, 1)
                assert count[0] == PER

        @blk.sync
        def _(sp):
            sp.sem_inc(n_vs, PB)
            sp.sem_inc(n_st, 16)
            ov = out.rearrange("b (t p) d -> p (b t) d", p=P)
            with sp.Fori(0, B) as bt:
                sp.wait_ge(n_o, bt + 1)
                sp.dma_start(ov[:, bass.ds(bt * TT, TT), :], ob[:, :, :]).then_inc(n_st, 16)
            sp.wait_ge(n_st, 16 * B + 16)


_INS = ['L0_attn_x', 'L0_attn_W', 'L0_attn_b', 'L0_ffn_ln_g', 'L0_ffn_ln_b', 'L0_ffn_aw1', 'L0_ffn_ab1', 'L0_ffn_aw2',
        'L0_ffn_ab2', 'L0_ffn_gate_w', 'L0_ffn_gate_b', 'L0_ffn_ew1', 'L0_ffn_eb1', 'L0_ffn_ew2', 'L0_ffn_eb2',
        'L0_ffn_gens', 'L0_ffn_gc_w', 'L0_ffn_gc_b', 'L1_attn_Mq', 'L1_attn_Mk', 'L1_attn_Mv', 'L1_ffn_Wg', 'L1_ffn_bg',
        'L1_ffn_W1', 'L1_ffn_b1', 'L1_ffn_W2', 'L1_ffn_b2']
_OUTS = [((8, 512, 128), 'float32')]


def kernel(**inputs):
    import numpy as _np
    import concourse.bacc as _bacc
    from concourse import mybir as _mybir
    from concourse.bass_utils import run_bass_kernel_spmd as _run

    nc = _bacc.Bacc("TRN2", target_bir_lowering=False, num_devices=1)
    arrays, args = {}, []
    for name in _INS:
        a = _np.ascontiguousarray(inputs[name])
        arrays[f"in_{name}_dram"] = a
        args.append(nc.dram_tensor(f"in_{name}_dram", a.shape, _mybir.dt.from_np(a.dtype), kind="ExternalInput").ap())
    for i, (shape, dtype) in enumerate(_OUTS):
        dt = _mybir.dt.from_np(_np.dtype(dtype))
        args.append(nc.dram_tensor(f"out_{i}_dram", shape, dt, kind="ExternalOutput").ap())
    recurrent_d2_kernel(nc, *args)
    r = _run(nc, [arrays], core_ids=[0])
    got = tuple(r.results[0][f"out_{i}_dram"] for i in range(len(_OUTS)))
    return got[0]
```

```python
from contextlib import ExitStack

import concourse.bass as bass
from concourse import mybir

F32 = mybir.dt.float32
F32R = mybir.dt.float32r
ALU = mybir.AluOpType
ACT = mybir.ActivationFunctionType
AX = mybir.AxisListType

P = 128
EPS = 1e-5
BIG = 3.0e38
TAYLOR = 12
SQUARE = 4


def recurrent_d2_kernel(nc, x, W, b, ln_g, ln_b, aw1, ab1, aw2, ab2, gate_w, gate_b, ew1, eb1, ew2, eb2,
                        gens, gc_w, gc_b, Mq, Mk, Mv, Wg, bg, W1, b1, W2, b2, out):
    B, T, D = x.shape
    TT = T // P
    NT = B * TT
    AC = aw1.shape[1] // P
    E0, H0 = ew1.shape[0], ew1.shape[2]
    EC = H0 // P
    E1, H1 = W1.shape[0], W1.shape[2]
    HC = H1 // P
    G = gens.shape[0]
    HEADS = 8
    KS = Mq.shape[1] // HEADS
    HT = T // HEADS
    VD = D // HEADS
    SC0 = float(D) ** -0.5
    SC1 = float(KS) ** -0.5
    LOOPS = B // 2
    ROW_B, ROW_G, ROW_LB, ROW_AB1 = 0, 3, 4, 5
    ROW_EB1 = ROW_AB1 + AC
    ROW_B1 = ROW_EB1 + E0 * EC
    ROWS = ROW_B1 + E1 * HC

    with ExitStack() as ctx:
        def sb(name, shape, dt=F32):
            return ctx.enter_context(nc.sbuf_tensor(name, shape, dt))

        early = ctx.enter_context(ExitStack())

        def sbe(name, shape, dt=F32):
            return early.enter_context(nc.sbuf_tensor(name, shape, dt))

        def sem(name):
            return ctx.enter_context(nc.semaphore(name))

        x_all = sb("x_all", [P, NT, D])
        ident = sb("ident", [P, P])
        cols = sb("cols", [P, ROWS])
        mq_d = sb("mq_d", [P, HEADS, 2, KS])
        mk_d = sb("mk_d", [P, HEADS, 2, KS])
        mv = sb("mv", [P, D])
        wg = sb("wg", [P, E1])
        bg_c = sb("bg_c", [E1, 1])
        w_1 = sb("w_1", [P, E1, H1])
        xn_all = sb("xn_all", [P, NT, D])
        xn2T = sb("xn2T", [P, B * T])
        oh_all = sb("oh_all", [P, NT, E1])
        w_2 = sb("w_2", [P, E1 * HC, D])
        b2_sb = sb("b2_sb", [E1, D])
        rev = sb("rev", [P, TT, E1])
        half_neg = sb("half_neg", [P, NT])
        s_all = sbe("s_all", [P, NT, D])
        lgT = sbe("lgT", [P, T])
        lgT3 = sbe("lgT3", [P, T])
        cmask = sbe("cmask", [P, P])
        rows = sbe("rows", [ROWS, P])
        bqs = sbe("bqs", [P, 1])
        coef = sbe("coef", [P, TAYLOR])
        w_qkv = sbe("w_qkv", [P, 3 * D])
        bv_bc = sbe("bv_bc", [P, D])
        w_a1 = sbe("w_a1", [P, AC * P])
        w_a2 = sbe("w_a2", [P, AC, D])
        ab2_bc = sbe("ab2_bc", [P, D])
        w_gate = sbe("w_gate", [P, E0])
        gate_bc = sbe("gate_bc", [E0, 1])
        w_e1 = sbe("w_e1", [P, E0, H0])
        w_e2 = sbe("w_e2", [P, E0 * EC, D])
        w_e2T = sbe("w_e2T", [P, E0 * EC, D])
        eb2_sb = sbe("eb2_sb", [E0, D])
        eb2T = sbe("eb2T", [P, E0])
        eb2R = sbe("eb2R", [E0, D])
        gA = sbe("gA", [P, G, D])
        gAT = sbe("gAT", [P, G, D])
        gE = sbe("gE", [P, G, D])
        gET = sbe("gET", [P, G, D])
        rot = sbe("rot", [P, D])
        gc_bc = sbe("gc_bc", [P, 2, D])
        gcb_bc = sbe("gcb_bc", [P, 1])
        gcb_half = sbe("gcb_half", [P, 1])
        bn = sbe("bn", [P, NT, 6])
        mv_st = sbe("mv_st", [P, NT, 2])
        ve = sbe("ve", [P, NT])
        rs1 = sbe("rs1", [P, NT])
        rs2 = sbe("rs2", [P, NT])

        psum = [ctx.enter_context(nc.psum_tensor(f"bank{i}", [P, T], F32)) for i in range(8)]

        ld_x = [sem(f"ld_x{i}") for i in range(B)]
        ld_w = sem("ld_w")
        ld_late = sem("ld_late")
        cst = sem("cst")
        blk = ctx.enter_context(nc.Block())

        col = lambda i: cols[:, i:i + 1]
        batch = lambda t, n, i: t[:, bass.ds(i * n, n)]

        N_LD, N_LATE = 16 * 20, 16 * 10

        colsT = sem("colsT")
        cols_ok = sem("cols_ok")
        bias_ok = sem("bias_ok")
        bn_ok = sem("bn_ok")
        st_ok = sem("st_ok")
        st_pool = sem("st_pool")
        e_mm = sem("e_mm")
        e_ev = sem("e_ev")
        r_mm = sem("r_mm")
        r_ev = sem("r_ev")

        @blk.sync
        def _(sp):
            xv = x.rearrange("b (t p) d -> p b t d", p=P)
            for i in range(B):
                sp.dma_start(x_all[:, i * TT:(i + 1) * TT, :], xv[:, i]).then_inc(ld_x[i], 16)
            rw = lambda a, n: a.rearrange("(c p) -> c p", p=P) if n else a
            sp.dma_start(gA[:, :, :], gens.rearrange("g r c -> r g c")).then_inc(ld_w, 16)
            sp.dma_start(rows[ROW_B:ROW_B + 3, :], rw(b, 3)).then_inc(ld_w, 16)
            sp.dma_start(rows[ROW_G:ROW_G + 1, :], rw(ln_g, 1)).then_inc(ld_w, 16)
            sp.dma_start(rows[ROW_LB:ROW_LB + 1, :], rw(ln_b, 1)).then_inc(ld_w, 16)
            sp.dma_start(rows[ROW_AB1:ROW_AB1 + AC, :], rw(ab1, AC)).then_inc(ld_w, 16)
            sp.dma_start(rows[ROW_EB1:ROW_EB1 + E0 * EC, :],
                         eb1.rearrange("e (c p) -> (e c) p", p=P)).then_inc(ld_w, 16)
            sp.dma_start(rows[ROW_B1:ROWS, :], b1.rearrange("e (c p) -> (e c) p", p=P)).then_inc(ld_w, 16)
            sp.dma_start(w_qkv[:, :], W).then_inc(ld_w, 16)
            sp.dma_start(bv_bc[:, :], b[2 * D:3 * D].partition_broadcast(P)).then_inc(ld_w, 16)
            sp.dma_start(w_a1[:, :], aw1).then_inc(ld_w, 16)
            sp.dma_start(w_a2[:, :, :], aw2.rearrange("(c p) d -> p c d", p=P)).then_inc(ld_w, 16)
            sp.dma_start(ab2_bc[:, :], ab2.partition_broadcast(P)).then_inc(ld_w, 16)
            sp.dma_start(w_gate[:, :], gate_w).then_inc(ld_w, 16)
            sp.dma_start(gate_bc[:, :], gate_b.rearrange("(e a) -> e a", a=1)).then_inc(ld_w, 16)
            sp.dma_start(w_e1[:, :, :], ew1.rearrange("e d h -> d e h")).then_inc(ld_w, 16)
            sp.dma_start(w_e2[:, :, :], ew2.rearrange("e (c p) d -> p (e c) d", p=P)).then_inc(ld_w, 16)
            sp.dma_start(eb2_sb[:, :], eb2).then_inc(ld_w, 16)
            sp.dma_start(gc_bc[:, 0, :], gc_w[0:D, :].rearrange("d a -> (d a)").partition_broadcast(P)).then_inc(ld_w, 16)
            sp.dma_start(gc_bc[:, 1, :], gc_w[D:2 * D, :].rearrange("d a -> (d a)").partition_broadcast(P)).then_inc(ld_w, 16)
            sp.dma_start(gcb_bc[:, :], gc_b.partition_broadcast(P)).then_inc(ld_w, 16)
            for m, src in ((mq_d, Mq), (mk_d, Mk)):
                for c in range(2):
                    sp.dma_start(m[:, :, c, :], src.rearrange("d (r k) -> d r k", k=KS)).then_inc(ld_late, 16)
            sp.dma_start(mv[:, :], Mv).then_inc(ld_late, 16)
            sp.dma_start(wg[:, :], Wg).then_inc(ld_late, 16)
            sp.dma_start(bg_c[:, :], bg.rearrange("(e a) -> e a", a=1)).then_inc(ld_late, 16)
            sp.dma_start(w_1[:, :, :], W1.rearrange("e d h -> d e h")).then_inc(ld_late, 16)
            sp.dma_start(w_2[:, :, :], W2.rearrange("e (c p) d -> p (e c) d", p=P)).then_inc(ld_late, 16)
            sp.dma_start(b2_sb[:, :], b2).then_inc(ld_late, 16)

        @blk.gpsimd
        def _(pool):
            pool.memset(ident[:, :], 0.0).then_inc(cst, 1)
            pool.memset(cmask[:, :], 0.0).then_inc(cst, 1)
            pool.memset(half_neg[:, :], -0.5).then_inc(cst, 1)
            for e in range(E1):
                pool.memset(rev[:, :, e:e + 1], float(E1 - e)).then_inc(cst, 1)
            pool.memset(lgT[:, :], 0.0).then_inc(cst, 1)
            pool.memset(lgT3[:, :], 0.0).then_inc(cst, 1)
            pool.iota(coef[:, :], pattern=[[-1, TAYLOR]], base=TAYLOR, channel_multiplier=0,
                      allow_small_or_imprecise_dtypes=True).then_inc(cst, 1)
            pool.wait_ge(cst, 6 + E1)
            pool.affine_select(out=ident[:, :], in_=ident[:, :], compare_op=ALU.not_equal, fill=1.0,
                               base=0, pattern=[[-1, P]], channel_multiplier=1).then_inc(cst, 1)
            pool.affine_select(out=cmask[:, :], in_=cmask[:, :], compare_op=ALU.is_ge, fill=-9.0e15,
                               base=0, pattern=[[-1, P]], channel_multiplier=1).then_inc(cst, 1)
            pool.wait_ge(bn_ok, 1)
            n = [0]

            def step(ins):
                ins.then_inc(st_pool, 1)
                n[0] += 1
                pool.wait_ge(st_pool, n[0])

            var = mv_st[:, :, 1]
            step(pool.tensor_scalar(ve[:, :], var, EPS, None, ALU.add))
            step(pool.tensor_tensor(rs1[:, :], ve[:, :], half_neg[:, :], ALU.pow))
            step(pool.tensor_tensor(ve[:, :], rs1[:, :], rs1[:, :], ALU.mult))
            step(pool.tensor_tensor(ve[:, :], ve[:, :], var, ALU.mult))
            step(pool.tensor_scalar(ve[:, :], ve[:, :], EPS, None, ALU.add))
            pool.tensor_tensor(rs2[:, :], ve[:, :], half_neg[:, :], ALU.pow).then_inc(st_ok, 1)

        N_CST = 8 + E1

        @blk.tensor
        def _(pe):
            pe.wait_ge(cst, N_CST)
            pe.wait_ge(ld_w, N_LD)
            pe.transpose(psum[0][:, 0:ROWS], rows[:, :], ident[0:ROWS, 0:ROWS]).then_inc(colsT, 1)
            for g in range(G):
                mm = pe.transpose(psum[1][:, g * P:(g + 1) * P], gA[:, g, :], ident[:, :])
            mm.then_inc(e_mm, 1)
            for q in range(E0 * EC // 4):
                for i in range(4):
                    mm = pe.transpose(psum[5 + q][:, i * P:(i + 1) * P], w_e2[:, 4 * q + i, :], ident[:, :])
            mm.then_inc(r_mm, 1)
            pe.transpose(psum[2][:, 0:E0], eb2_sb[:, :], ident[0:E0, 0:E0]).then_inc(r_mm, 1)

        @blk.vector
        def _(dve):
            for i in range(B):
                dve.wait_ge(ld_x[i], 16)
                for t in range(i * TT, (i + 1) * TT):
                    dve.bn_stats(bn[:, t, :], x_all[:, t, :]).then_inc(bias_ok, 1)
            dve.wait_ge(bias_ok, NT)
            for t in range(NT):
                mm = dve.bn_aggr(mv_st[:, t, :], bn[:, t, :])
            mm.then_inc(bn_ok, 1)
            dve.wait_ge(colsT, 1)
            dve.tensor_copy(cols[:, :], psum[0][:, 0:ROWS]).then_inc(cols_ok, 1)
            dve.wait_ge(cols_ok, 1)
            dve.tensor_scalar(bqs[:, :], col(ROW_B), SC0, None, ALU.mult).then_inc(cols_ok, 1)
            dve.wait_ge(ld_w, N_LD)
            dve.tensor_scalar(gcb_half[:, :], gcb_bc[:, :], 0.5, None, ALU.mult).then_inc(cols_ok, 1)
            dve.wait_ge(e_mm, 1)
            dve.tensor_scalar(gAT[:, :, :], psum[1][:, :].rearrange("p (g d) -> p g d", g=G),
                              2.0 ** -SQUARE, None, ALU.mult).then_inc(cols_ok, 1)
            dve.wait_ge(cst, N_CST)
            dve.tensor_copy(gE[:, :, :], ident[:, :].unsqueeze(1).broadcast_to([P, G, D])).then_inc(cols_ok, 1)
            dve.reciprocal(coef[:, :], coef[:, :]).then_inc(cols_ok, 1)
            dve.wait_ge(cols_ok, 6)
            dve.engine_nop().then_inc(e_ev, 1)
            dve.wait_ge(r_mm, 1)
            for q in range(E0 * EC // 4):
                mm = dve.tensor_copy(w_e2T[:, 4 * q:4 * q + 4, :],
                                     psum[5 + q][:, :].rearrange("p (i d) -> p i d", i=4))
            mm.then_inc(r_ev, 1)
            dve.wait_ge(r_mm, 2)
            dve.tensor_copy(eb2T[:, :], psum[2][:, 0:E0]).then_inc(r_ev, 1)


        xs = [sbe(f"xs{i}", [P, TT, D]) for i in range(2)]
        xh = [sbe(f"xh{i}", [P, TT, D]) for i in range(2)]
        xT = [sbe(f"xT{i}", [P, T]) for i in range(2)]
        qT = [sbe(f"qT{i}", [P, T]) for i in range(2)]
        kT = [sbe(f"kT{i}", [P, T]) for i in range(2)]
        va = [sbe(f"va{i}", [P, TT, D]) for i in range(2)]
        pr = [sbe(f"pr{i}", [P, T]) for i in range(2)]
        prT = [sbe(f"prT{i}", [P, T]) for i in range(2)]
        VBANK = (7, 3)
        nm0 = sbe("nm0", [P, 2])
        z0 = sbe("z0", [P, 2])
        rz0 = sbe("rz0", [P, 2])
        nms0 = sbe("nms0", [P, 2])
        a_xs = sem("a_xs")
        a_xh = sem("a_xh")
        a_keep = sem("a_keep")
        a_T = sem("a_T")
        a_xT = sem("a_xT")
        a_x2T = sem("a_x2T")
        a_qkv = sem("a_qkv")
        a_q = sem("a_q")
        a_v = sem("a_v")
        a_s = sem("a_s")
        a_dm = sem("a_dm")
        a_mx = sem("a_mx")
        a_nm = sem("a_nm")
        a_p = sem("a_p")
        a_rz = sem("a_rz")
        a_pT = sem("a_pT")
        a_pTs = sem("a_pTs")
        a_o = sem("a_o")
        a_os = sem("a_os")

        @blk.gpsimd
        def _(pool):
            with pool.Fori(0, LOOPS) as i:
                for par in range(2):
                    bt = 2 * i + par
                    pool.wait_ge(a_T, bt * 2 + 2)
                    for t in range(TT):
                        pool.wait_ge(a_xs, bt * TT + t + 1)
                        pool.tensor_tensor(xh[par][:, t, :], xs[par][:, t, :],
                                           rs2[:, bass.ds(bt * TT + t, 1)].broadcast_to([P, D]), ALU.mult)\
                            .then_inc(a_xh, 1)
                    pool.tensor_copy(xn_all[:, bass.ds(bt * TT, TT), :], xs[par][:, :, :]).then_inc(a_keep, 1)

        ROUNDS = 2
        assert ROUNDS * (B - 2) == TAYLOR
        TURNED, SQUARED = TAYLOR, TAYLOR + 1
        e_done = lambda r: r + 1 if r <= SQUARED else SQUARED + 1 + 2 * (r - SQUARED)
        LAST = SQUARED + SQUARE + G - 1

        def phase1(eng, batch):
            with eng.Fori(0, LOOPS - 1) as i:
                for par in range(2):
                    batch(2 * i + par, par, True, {1: [(2 * i + par) * ROUNDS], 7: [(2 * i + par) * ROUNDS + 1]})
            batch(B - 2, 0, True, {1: [TURNED], 7: [SQUARED]})
            batch(B - 1, 1, False, {1: [SQUARED + 1], 3: [SQUARED + 2], 5: [SQUARED + 3], 7: [SQUARED + 4],
                                    8: [SQUARED + 5], 9: [SQUARED + 6]})

        @blk.tensor
        def _(pe):
            pe.wait_ge(r_ev, 2)
            pe.wait_ge(e_ev, 1)

            def turn_xs(bt, par):
                pe.wait_ge(a_xs, (bt + 1) * TT)
                pe.wait_ge(a_xT, bt + 1)
                for t in range(TT):
                    mm = pe.transpose(psum[0][:, t * P:(t + 1) * P], xs[par][:, t, :], ident[:, :])
                mm.then_inc(a_T, 1)

            def turn_xh(bt, par):
                pe.wait_ge(a_xh, (bt + 1) * TT)
                pe.wait_ge(a_x2T, bt + 1)
                for t in range(TT):
                    mm = pe.transpose(psum[1][:, t * P:(t + 1) * P], xh[par][:, t, :], ident[:, :])
                mm.then_inc(a_T, 1)

            def exp_round(r, bank):
                if not isinstance(r, int) or r < TURNED:
                    pe.wait_ge(e_ev, r + 1)
                    for g in range(G):
                        mm = pe.matmul(psum[bank][:, g * P:(g + 1) * P], gAT[:, g, :], gE[:, g, :],
                                       start=True, stop=True)
                elif r == TURNED:
                    pe.wait_ge(e_ev, e_done(r))
                    for g in range(G):
                        mm = pe.transpose(psum[bank][:, g * P:(g + 1) * P], gE[:, g, :], ident[:, :])
                elif r < SQUARED + SQUARE:
                    pe.wait_ge(e_ev, e_done(r))
                    for g in range(G):
                        pe.matmul(psum[0][:, g * P:(g + 1) * P], gET[:, g, :], gE[:, g, :], start=True, stop=True)
                    for g in range(G):
                        mm = pe.matmul(psum[1][:, g * P:(g + 1) * P], gE[:, g, :], gET[:, g, :], start=True, stop=True)
                else:
                    n = r - SQUARED - SQUARE
                    pe.wait_ge(e_ev, e_done(SQUARED + SQUARE))
                    if n:
                        pe.wait_ge(r_ev, 2 + n)
                    g = G - 2 - n
                    mm = pe.matmul(psum[0][:, 0:D], gET[:, g, :], gE[:, G - 1, :] if n == 0 else rot[:, :],
                                   start=True, stop=True)
                mm.then_inc(e_mm, 1)

            turn_xs(0, 0)
            turn_xh(0, 0)

            def batch(bt, par, more, rounds):
                def after(i):
                    for r in rounds.get(i, []):
                        if i == 1:
                            pe.wait_ge(a_xT, bt + 2)
                            pe.wait_ge(a_x2T, bt + 2)
                        elif more:
                            pe.wait_ge(a_xT, bt + 3)
                            pe.wait_ge(a_x2T, bt + 3)
                        exp_round(r, 0 if i == 1 else 1)

                pe.wait_ge(a_xT, bt + 2)
                pe.wait_ge(a_v, bt + 1)
                pe.matmul(psum[2][:, :], w_qkv[:, 0:D], xT[par][:, :], start=True, stop=True).then_inc(a_qkv, 1)
                pe.wait_ge(a_os, bt * TT + 2)
                pe.matmul(psum[3][:, :], w_qkv[:, D:2 * D], xT[par][:, :], start=True, stop=True).then_inc(a_qkv, 1)
                after(1)
                pe.wait_ge(a_q, bt * 2 + 3)
                for t in range(TT):
                    mm = pe.matmul(psum[2][:, t * P:(t + 1) * P], xT[par][:, t * P:(t + 1) * P],
                                   w_qkv[:, 2 * D:3 * D], start=True, stop=True)
                mm.then_inc(a_qkv, 1)
                pe.wait_ge(a_q, bt * 2 + 4)

                def scores(t):
                    pe.wait_ge(a_p, bt * TT + t + 1)
                    pe.matmul(psum[4 + t % 2][:, 0:(t + 1) * P], qT[par][:, t * P:(t + 1) * P],
                              kT[par][:, 0:(t + 1) * P], start=True, stop=True).then_inc(a_s, 1)

                def turn(t):
                    pe.wait_ge(a_p, bt * TT + t + 3)
                    pe.wait_ge(a_pTs, bt * TT + t + 1)
                    for c in range(t + 1):
                        mm = pe.transpose(psum[6][:, c * P:(c + 1) * P], pr[t % 2][:, c * P:(c + 1) * P],
                                          ident[:, :])
                    mm.then_inc(a_pT, 1)

                def values(t):
                    pe.wait_ge(a_pTs, bt * TT + t + 2)
                    if t == 0:
                        pe.wait_ge(a_v, bt + 2)
                    pe.wait_ge(a_os, bt * TT + t + 1)
                    for c in range(t + 1):
                        mm = pe.matmul(psum[VBANK[t % 2]][:, 0:P], prT[t % 2][:, c * P:(c + 1) * P],
                                       va[par][:, c, :], start=(c == 0), stop=(c == t))
                    mm.then_inc(a_o, 1)

                scores(0)
                scores(1)
                if more:
                    pe.wait_ge(e_ev, e_done(rounds[1][0] + 1) if isinstance(bt, int) else rounds[1][0] + 2)
                    turn_xs(bt + 1, 1 - par)
                after(3)
                turn(0)
                scores(2)
                if more:
                    turn_xh(bt + 1, 1 - par)
                turn(1)
                after(5)
                values(0)
                scores(3)
                after(7)
                turn(2)
                values(1)
                after(8)
                turn(3)
                values(2)
                after(9)
                values(3)

            phase1(pe, batch)
            pe.wait_ge(e_mm, 1 + LAST)
            pe.wait_ge(r_ev, 2 + G - 1)
            pe.wait_ge(a_p, B * TT + 2)
            pe.wait_ge(a_pTs, B * TT + 1)
            for q in range(E0 * EC // 4):
                for i in range(4):
                    mm = pe.matmul(psum[4 + q][:, i * P:(i + 1) * P], w_e2T[:, 4 * q + i, :], rot[:, :],
                                   start=True, stop=True)
                mm.then_inc(r_mm, 1)
            pe.matmul(psum[1][0:E0, 0:D], eb2T[:, :], rot[:, :], start=True, stop=True).then_inc(r_mm, 1)

        @blk.scalar
        def _(act):
            act.sem_inc(a_xT, 1)
            act.sem_inc(a_q, 2)
            act.sem_inc(a_p, 2)
            act.wait_ge(cols_ok, 2)

            def store_xT(bt, par):
                act.wait_ge(a_T, bt * 2 + 1 + 4)
                act.activation(xT[par][:, :], psum[0][:, :], ACT.Copy).then_inc(a_xT, 1)

            store_xT(0, 0)

            def batch(bt, par, more, rounds):
                act.wait_ge(a_qkv, bt * 3 + 1)
                act.activation(qT[par][:, :], psum[2][:, :], ACT.Identity, bias=bqs[:, 0:1], scale=SC0)\
                    .then_inc(a_q, 1)
                act.wait_ge(a_qkv, bt * 3 + 2)
                act.activation(kT[par][:, :], psum[3][:, :], ACT.Identity, bias=col(ROW_B + 1), scale=1.0)\
                    .then_inc(a_q, 1)
                for t in range(TT):
                    act.wait_ge(a_mx, bt * TT + t + 1)
                    act.wait_ge(a_pT, bt * TT + t + 1)
                    act.wait_ge(a_rz, bt * TT + t + 1)
                    act.activation(pr[t % 2][:, 0:(t + 1) * P], psum[4 + t % 2][:, 0:(t + 1) * P], ACT.Exp,
                                   bias=nm0[:, t % 2:t % 2 + 1], scale=1.0,
                                   accum_out=z0[:, t % 2:t % 2 + 1]).then_inc(a_p, 1)
                    if t == 1 and more:
                        store_xT(bt + 1, 1 - par)

            phase1(act, batch)

        @blk.vector
        def _(dve):
            dve.sem_inc(a_T, 4)
            dve.sem_inc(a_x2T, 1)
            dve.sem_inc(a_v, 1)
            dve.sem_inc(a_pT, 2)
            dve.sem_inc(a_rz, 2)
            dve.sem_inc(a_pTs, 1)
            dve.sem_inc(a_os, 2)
            dve.wait_ge(st_ok, 1)
            groups = lambda a: a.rearrange("p (g d) -> p g d", g=G)

            def norm(bt, par):
                dve.wait_ge(a_T, bt * 2 + 1)
                dve.wait_ge(a_keep, bt + 1)
                for t in range(TT):
                    g = bt * TT + t
                    dve.tensor_scalar(xs[par][:, t, :], x_all[:, bass.ds(g, 1), :].rearrange("p a d -> p (a d)"),
                                      mv_st[:, bass.ds(g, 1), 0], rs1[:, bass.ds(g, 1)],
                                      ALU.subtract, ALU.mult).then_inc(a_xs, 1)

            def store_x2T(bt):
                dve.wait_ge(a_T, bt * 2 + 2 + 4)
                dve.tensor_scalar(xn2T[:, bass.ds(bt * T, T)], psum[1][:, :], col(ROW_G), col(ROW_LB),
                                  ALU.mult, ALU.add).then_inc(a_x2T, 1)

            def store_round(r, bank):
                dve.wait_ge(e_mm, r + 2)
                if not isinstance(r, int) or r < TURNED:
                    dve.scalar_tensor_tensor(gE[:, :, :], groups(psum[bank][:, :]), coef[:, bass.ds(r, 1)],
                                             ident[:, :].unsqueeze(1).broadcast_to([P, G, D]),
                                             ALU.mult, ALU.add).then_inc(e_ev, 1)
                elif r == TURNED:
                    dve.tensor_copy(gET[:, :, :], groups(psum[bank][:, :])).then_inc(e_ev, 1)
                elif r < SQUARED + SQUARE:
                    dve.tensor_copy(gE[:, :, :], groups(psum[0][:, :])).then_inc(e_ev, 1)
                    dve.tensor_copy(gET[:, :, :], groups(psum[1][:, :])).then_inc(e_ev, 1)
                else:
                    dve.tensor_copy(rot[:, :], psum[0][:, 0:D]).then_inc(r_ev, 1)

            norm(0, 0)
            store_x2T(0)

            def batch(bt, par, more, rounds):
                def after(i):
                    for r in rounds.get(i, []):
                        store_round(r, 0 if i == 1 else 1)

                if more:
                    norm(bt + 1, 1 - par)
                after(1)
                dve.wait_ge(a_qkv, bt * 3 + 3)
                dve.tensor_tensor(va[par][:, :, :], psum[2][:, :].rearrange("p (t d) -> p t d", t=TT),
                                  bv_bc[:, :].unsqueeze(1).broadcast_to([P, TT, D]), ALU.add).then_inc(a_v, 1)

                def top(t):
                    s = psum[4 + t % 2]
                    dve.wait_ge(a_s, bt * TT + t + 1)
                    dve.tensor_tensor(s[:, t * P:(t + 1) * P], s[:, t * P:(t + 1) * P], cmask[:, :],
                                      ALU.add).then_inc(a_dm, 1)
                    dve.wait_ge(a_dm, bt * TT + t + 1)
                    dve.wait_ge(a_p, bt * TT + t + 1)
                    dve.tensor_reduce(nm0[:, t % 2:t % 2 + 1], s[:, 0:(t + 1) * P], AX.X, ALU.max,
                                      negate=True).then_inc(a_mx, 1)

                def store_turned(t):
                    dve.wait_ge(a_pT, bt * TT + t + 3)
                    dve.wait_ge(a_o, bt * TT + t + 1)
                    dve.wait_ge(a_os, bt * TT + t + 1)
                    dve.tensor_copy(prT[t % 2][:, 0:(t + 1) * P], psum[6][:, 0:(t + 1) * P]).then_inc(a_pTs, 1)
                    dve.reciprocal(rz0[:, t % 2:t % 2 + 1], z0[:, t % 2:t % 2 + 1]).then_inc(a_rz, 1)

                def store_values(t):
                    dve.wait_ge(a_rz, bt * TT + t + 3)
                    dve.wait_ge(a_o, bt * TT + t + 3)
                    dve.tensor_scalar(s_all[:, bass.ds(bt * TT + t, 1), :].rearrange("p a d -> p (a d)"),
                                      psum[VBANK[t % 2]][:, 0:P], rz0[:, t % 2:t % 2 + 1], None,
                                      ALU.mult).then_inc(a_os, 1)

                top(0)
                top(1)
                after(3)
                store_turned(0)
                top(2)
                if more:
                    store_x2T(bt + 1)
                store_turned(1)
                after(5)
                store_values(0)
                top(3)
                after(7)
                store_turned(2)
                store_values(1)
                after(8)
                store_turned(3)
                store_values(2)
                after(9)
                store_values(3)

            phase1(dve, batch)
            for q in range(E0 * EC // 4):
                dve.wait_ge(r_mm, 3 + q)
                dve.tensor_copy(w_e2[:, 4 * q:4 * q + 4, :],
                                psum[4 + q][:, :].rearrange("p (i d) -> p i d", i=4)).then_inc(r_ev, 1)
            dve.wait_ge(r_mm, 3 + E0 * EC // 4)
            dve.tensor_copy(eb2R[:, :], psum[1][0:E0, 0:D]).then_inc(r_ev, 1)

        @blk.sync
        def _(sp):
            sp.sem_inc(a_keep, 2)
            sp.sem_inc(a_o, 2)

        NU = 4
        CH = AC + E0 * EC
        NEXT = (10, 12, 14)
        hid = [sbe(f"hid{i}", [P, T]) for i in range(NU)]
        lg = sbe("lg", [P, TT, E1])
        lg0, oh1, oh2, tie, wf = (sbe(n, [P, TT, E0]) for n in ("lg0", "oh1", "oh2", "tie", "wf"))
        m1, m2, dm, th, w1t, w2t, gz, gt = (sbe(n, [P, TT]) for n in ("m1", "m2", "dm", "th", "w1t", "w2t", "gz", "gt"))
        wT = sbe("wT", [E1, T])
        acc, abel, ta, tb, tanh_r = (sbe(n, [P, TT, D]) for n in ("acc", "abel", "ta", "tb", "tanh_r"))
        mq_ok = sem("mq_ok")
        f_lg = sem("f_lg")
        f_lgs = sem("f_lgs")
        f_c = sem("f_c")
        f_dm = sem("f_dm")
        f_th = sem("f_th")
        f_w = sem("f_w")
        f_wT = sem("f_wT")
        f_wTs = sem("f_wTs")
        f_b = sem("f_b")
        f_ba = sem("f_ba")
        f_up = sem("f_up")
        f_h = sem("f_h")
        f_dn = sem("f_dn")
        f_ab = sem("f_ab")
        f_ea = sem("f_ea")
        f_gz = sem("f_gz")
        f_gt = sem("f_gt")
        f_r = sem("f_r")
        f_tr = sem("f_tr")
        f_x1 = sem("f_x1")
        f_v3 = sem("f_v3")
        f_r3 = sem("f_r3")
        f_xs3 = sem("f_xs3")
        f_k3 = sem("f_k3")
        f_T3 = sem("f_T3")
        f_Ts3 = sem("f_Ts3")
        f_lg3 = sem("f_lg3")
        f_lgs3 = sem("f_lgs3")
        f_s3 = sem("f_s3")
        f_oh3 = sem("f_oh3")
        xs3 = sbe("xs3", [P, TT, D])
        sc3, tie3 = (sbe(n, [P, TT, E1]) for n in ("sc3", "tie3"))
        mm3, mt3, ve3, r3 = (sbe(n, [P, TT]) for n in ("mm3", "mt3", "ve3", "r3"))
        bn3 = sbe("bn3", [P, TT, 6])
        mv3 = sbe("mv3", [P, TT, 2])

        @blk.gpsimd
        def _(pool):
            pool.wait_ge(ld_late, N_LATE)
            pool.tensor_scalar(mq_d[:, :, :, :], mq_d[:, :, :, :], SC1, None, ALU.mult).then_inc(mq_ok, 1)
            with pool.Fori(0, B) as bt:
                pool.wait_ge(f_v3, bt + 1)
                pool.tensor_tensor(r3[:, :], ve3[:, :], half_neg[:, 0:TT], ALU.pow).then_inc(f_r3, 1)
                pool.wait_ge(f_xs3, bt + 1)
                pool.tensor_copy(xn_all[:, bass.ds(bt * TT, TT), :], xs3[:, :, :]).then_inc(f_k3, 1)

        @blk.tensor
        def _(pe):
            pe.wait_ge(a_os, B * TT + 2)
            pe.wait_ge(r_ev, 2 + G - 1 + E0 * EC // 4 + 1)
            pe.wait_ge(a_x2T, B + 1)
            pe.wait_ge(ld_late, N_LATE)

            def next_T(bt):
                pe.wait_ge(f_xs3, bt + 1)
                pe.wait_ge(f_ba, bt + 2)
                for t in range(TT):
                    mm = pe.transpose(psum[7][:, t * P:(t + 1) * P], xs3[:, t, :], ident[:, :])
                mm.then_inc(f_T3, 1)

            def next_scores(bt):
                pe.wait_ge(f_Ts3, bt + 1)
                pe.matmul(psum[7][0:E1, :], wg[:, :], xn2T[:, bass.ds(bt * T, T)], start=True, stop=True)\
                  .then_inc(f_lg3, 1)

            def next_turn(bt):
                pe.wait_ge(f_lgs3, bt + 1)
                for t in range(TT):
                    mm = pe.transpose(psum[7][:, t * P:(t + 1) * P], lgT3[:, t * P:(t + 1) * P], ident[:, :])
                mm.then_inc(f_lg3, 1)

            def batch_products(bt, follow):
                xb = xn2T[:, bass.ds(bt * T, T)]

                def up(n):
                    pe.wait_ge(f_h, bt * CH + n + 1)
                    w = w_a1[:, n * P:(n + 1) * P] if n < AC else \
                        w_e1[:, (n - AC) // EC, (n - AC) % EC * P:((n - AC) % EC + 1) * P]
                    pe.matmul(psum[n % NU][:, :], w, xb, start=True, stop=True).then_inc(f_up, 1)

                def down(n):
                    pe.wait_ge(f_h, bt * CH + n + 1 + NU)
                    if n < AC:
                        dst, w, first, last = psum[4], w_a2[:, n, :], n == 0, n == AC - 1
                        if first:
                            pe.wait_ge(f_ab, bt + 1)
                    else:
                        e, c = (n - AC) // EC, (n - AC) % EC
                        dst, w, first, last = psum[5 + e % 2], w_e2[:, n - AC, :], c == 0, c == EC - 1
                        if first:
                            pe.wait_ge(f_ea, bt * E0 + e + 1)
                    for t in range(TT):
                        mm = pe.matmul(dst[:, t * P:(t + 1) * P], hid[n % NU][:, t * P:(t + 1) * P], w,
                                       start=(first and t == 0), stop=last, skip_group_check=True)
                    mm.then_inc(f_dn, 1)

                pe.wait_ge(f_ba, bt + 1)
                pe.wait_ge(f_s3, bt + 1)
                pe.matmul(psum[7][0:E0, :], w_gate[:, :], xb, start=True, stop=True).then_inc(f_lg, 1)
                up(0)
                up(1)
                for n in range(CH):
                    if n + 2 < CH:
                        up(n + 2)
                    down(n)
                    if n == 1:
                        pe.wait_ge(f_lgs, bt + 1)
                        for t in range(TT):
                            mm = pe.transpose(psum[7][:, t * P:(t + 1) * P], lgT[:, t * P:(t + 1) * P], ident[:, :])
                        mm.then_inc(f_lg, 1)
                    if n == 7:
                        pe.wait_ge(f_w, bt + 1)
                        for t in range(TT):
                            mm = pe.transpose(psum[7][0:E0, t * P:(t + 1) * P], wf[:, t, :], ident[:, :])
                        mm.then_inc(f_wT, 1)
                    if n == 9:
                        pe.wait_ge(f_wTs, bt + 1)
                        for t in range(TT):
                            mm = pe.matmul(psum[7][:, t * P:(t + 1) * P], wT[0:E0, t * P:(t + 1) * P], eb2R[:, :],
                                           start=True, stop=True)
                        mm.then_inc(f_b, 1)
                    if follow and n in NEXT:
                        if n == NEXT[0]:
                            pe.wait_ge(f_ba, bt + 2)
                        (next_T, next_scores, next_turn)[NEXT.index(n)](bt - 1)

            batch_products(0, False)
            with pe.Fori(1, B) as bt:
                batch_products(bt, True)
            next_T(B - 1)
            next_scores(B - 1)
            next_turn(B - 1)

        @blk.scalar
        def _(act):
            act.sem_inc(f_h, NU)
            act.wait_ge(cols_ok, 3)

            def gate_tanh(bt):
                act.wait_ge(f_gz, bt + 1)
                act.activation(gt[:, :], gz[:, :], ACT.Tanh, bias=gcb_half[:, 0:1], scale=0.5).then_inc(f_gt, 1)

            def silu_tanh(bt):
                act.wait_ge(f_r, bt + 1)
                act.activation(tanh_r[:, :, :], ta[:, :, :], ACT.Tanh, scale=0.5).then_inc(f_tr, 1)

            def next_store(bt):
                act.wait_ge(f_T3, bt + 2)
                act.activation(xn2T[:, bass.ds(bt * T, T)], psum[7][:, :], ACT.Copy).then_inc(f_Ts3, 1)

            def chunks(bt, follow):
                for n in range(CH):
                    act.wait_ge(f_up, bt * CH + n + 1)
                    act.wait_ge(f_dn, bt * CH + n + 1)
                    act.activation(hid[n % NU][:, :], psum[n % NU][:, :], ACT.Gelu,
                                   bias=col((ROW_AB1 if n < AC else ROW_EB1 - AC) + n), scale=1.0).then_inc(f_h, 1)
                    if n == 0 and follow:
                        gate_tanh(bt - 1)
                    if n == 4:
                        act.wait_ge(f_dm, bt + 1)
                        act.activation(th[:, :], dm[:, :], ACT.Tanh, scale=0.5).then_inc(f_th, 1)
                    if n == 6 and follow:
                        silu_tanh(bt - 1)
                    if n == NEXT[0] + 2 and follow:
                        next_store(bt - 1)

            chunks(0, False)
            with act.Fori(1, B) as bt:
                chunks(bt, True)
            gate_tanh(B - 1)
            silu_tanh(B - 1)
            next_store(B - 1)

        @blk.vector
        def _(dve):
            dve.sem_inc(f_dn, NU)
            dve.sem_inc(f_T3, 1)
            dve.sem_inc(f_k3, 1)
            dve.sem_inc(f_ab, 1)
            dve.sem_inc(f_ba, 1)
            dve.sem_inc(f_ea, 2)
            dve.sem_inc(f_s3, 2)
            dve.wait_ge(a_keep, B + 2)
            b3 = lambda a: a.unsqueeze(2).broadcast_to([P, TT, E0])
            FOLLOW = TT + 1 + 2 + 2 + 4

            def chain(base):
                k = [0]

                def step(ins, last=False):
                    ins.then_inc(f_c, 1)
                    k[0] += 1
                    dve.wait_ge(f_c, base + k[0])
                return step, k

            def gate_mix(bt, step):
                dve.wait_ge(f_gt, bt + 1)
                step(dve.tensor_scalar(gt[:, :], gt[:, :], 0.5, 0.5, ALU.mult, ALU.add))
                for t in range(TT):
                    step(dve.scalar_tensor_tensor(ta[:, t, :], tb[:, t, :], gt[:, t:t + 1], abel[:, t, :],
                                                  ALU.mult, ALU.add))
                dve.tensor_tensor(ta[:, :, :], ta[:, :, :], xn_all[:, bass.ds(bt * TT, TT), :], ALU.add)\
                   .then_inc(f_r, 1)

            def finish(bt, step):
                dve.wait_ge(f_tr, bt + 1)
                step(dve.scalar_tensor_tensor(ta[:, :, :], tanh_r[:, :, :], 1.0, ta[:, :, :], ALU.add, ALU.mult))
                step(dve.scalar_tensor_tensor(ta[:, :, :], ta[:, :, :], 0.5, s_all[:, bass.ds(bt * TT, TT), :],
                                              ALU.mult, ALU.mult))
                xb = x_all[:, bass.ds(bt * TT, TT), :]
                dve.tensor_tensor(xb, xb, ta[:, :, :], ALU.add).then_inc(f_x1, 1)
                dve.wait_ge(f_x1, bt + 1)
                xt = lambda t: x_all[:, bass.ds(bt * TT + t, 1), :].rearrange("p a d -> p (a d)")
                dve.memset(ve3[:, 0:TT // 2], EPS)
                for t in range(TT):
                    ins = dve.bn_stats(bn3[:, t, :], xt(t))
                step(ins)
                dve.memset(ve3[:, TT // 2:TT], EPS)
                for t in range(TT):
                    ins = dve.bn_aggr(mv3[:, t, :], bn3[:, t, :])
                step(ins)
                dve.tensor_tensor(ve3[:, :], ve3[:, :], mv3[:, :, 1], ALU.add).then_inc(f_v3, 1)

            def next_norm(bt):
                xt = lambda t: x_all[:, bass.ds(bt * TT + t, 1), :].rearrange("p a d -> p (a d)")
                dve.wait_ge(f_T3, bt + 1)
                dve.wait_ge(f_k3, bt + 1)
                dve.wait_ge(f_r3, bt + 1)
                for t in range(TT):
                    ins = dve.tensor_scalar(xs3[:, t, :], xt(t), mv3[:, t, 0:1], r3[:, t:t + 1],
                                            ALU.subtract, ALU.mult)
                ins.then_inc(f_xs3, 1)

            def next_scores(bt):
                dve.wait_ge(f_lg3, bt * 2 + 1)
                dve.tensor_scalar(lgT3[0:E1, :], psum[7][0:E1, :], bg_c[:, 0:1], None, ALU.add).then_inc(f_lgs3, 1)

            def next_route(bt, step):
                d3 = lambda a: a.unsqueeze(2).broadcast_to([P, TT, E1])
                dve.wait_ge(f_lg3, bt * 2 + 2)
                dve.tensor_copy(sc3[:, :, :], psum[7][:, :].rearrange("p (t q) -> p t q", t=TT)[:, :, 0:E1])\
                   .then_inc(f_s3, 1)
                dve.wait_ge(f_s3, bt + 3)
                step(dve.tensor_reduce(mm3[:, :], sc3[:, :, :], AX.X, ALU.max))
                step(dve.tensor_tensor(tie3[:, :, :], sc3[:, :, :], d3(mm3[:, :]), ALU.is_equal))
                step(dve.tensor_tensor(tie3[:, :, :], tie3[:, :, :], rev[:, :, :], ALU.mult))
                step(dve.tensor_reduce(mt3[:, :], tie3[:, :, :], AX.X, ALU.max))
                dve.tensor_tensor(oh_all[:, bass.ds(bt * TT, TT), :], tie3[:, :, :], d3(mt3[:, :]), ALU.is_equal)\
                   .then_inc(f_oh3, 1)

            def batch_steps(bt, base, follow):
                step, k = chain(base)
                dve.wait_ge(f_lg, bt * 2 + 1)
                dve.tensor_scalar(lgT[0:E0, :], psum[7][0:E0, :], gate_bc[:, 0:1], None, ALU.add).then_inc(f_lgs, 1)
                dve.wait_ge(f_lg, bt * 2 + 2)
                step(dve.tensor_copy(lg0[:, :, :], psum[7][:, :].rearrange("p (t q) -> p t q", t=TT)[:, :, 0:E0]))

                def best(scores, m, oh):
                    step(dve.tensor_reduce(m[:, :], scores, AX.X, ALU.max))
                    step(dve.tensor_tensor(tie[:, :, :], scores, b3(m[:, :]), ALU.is_equal))
                    step(dve.tensor_tensor(tie[:, :, :], tie[:, :, :], rev[:, :, 0:E0], ALU.mult))
                    step(dve.tensor_reduce(w1t[:, :], tie[:, :, :], AX.X, ALU.max))
                    step(dve.tensor_tensor(oh[:, :, :], tie[:, :, :], b3(w1t[:, :]), ALU.is_equal))

                best(lg0[:, :, :], m1, oh1)
                step(dve.scalar_tensor_tensor(lg0[:, :, :], oh1[:, :, :], -BIG, lg0[:, :, :], ALU.mult, ALU.add))
                best(lg0[:, :, :], m2, oh2)
                dve.tensor_tensor(dm[:, :], m2[:, :], m1[:, :], ALU.subtract).then_inc(f_dm, 1)
                if follow:
                    gate_mix(bt - 1, step)
                dve.wait_ge(f_th, bt + 1)
                step(dve.tensor_scalar(w2t[:, :], th[:, :], 0.5, 0.5, ALU.mult, ALU.add))
                step(dve.tensor_scalar(w1t[:, :], th[:, :], -0.5, 0.5, ALU.mult, ALU.add))
                step(dve.tensor_tensor(oh1[:, :, :], oh1[:, :, :], b3(w1t[:, :]), ALU.mult))
                step(dve.tensor_tensor(oh2[:, :, :], oh2[:, :, :], b3(w2t[:, :]), ALU.mult))
                dve.tensor_tensor(wf[:, :, :], oh1[:, :, :], oh2[:, :, :], ALU.add).then_inc(f_w, 1)
                if follow:
                    finish(bt - 1, step)
                dve.wait_ge(f_wT, bt + 1)
                dve.tensor_copy(wT[0:E0, :], psum[7][0:E0, :]).then_inc(f_wTs, 1)
                if follow:
                    next_norm(bt - 1)

                def take_expert(e):
                    dve.wait_ge(f_dn, bt * CH + AC + (e + 1) * EC + NU)
                    if e:
                        dve.wait_ge(f_ea, bt * E0 + e + 2)
                    for t in range(TT):
                        y = psum[5 + e % 2][:, t * P:(t + 1) * P]
                        if e:
                            ins = dve.scalar_tensor_tensor(acc[:, t, :], y, wf[:, t, e:e + 1], acc[:, t, :],
                                                           ALU.mult, ALU.add)
                        else:
                            ins = dve.tensor_scalar(acc[:, t, :], y, wf[:, t, 0:1], None, ALU.mult)
                    ins.then_inc(f_ea, 1)

                take_expert(0)
                dve.wait_ge(f_dn, bt * CH + AC + NU)
                dve.tensor_tensor(abel[:, :, :], psum[4][:, :].rearrange("p (t d) -> p t d", t=TT),
                                  ab2_bc[:, :].unsqueeze(1).broadcast_to([P, TT, D]), ALU.add).then_inc(f_ab, 1)
                take_expert(1)
                dve.wait_ge(f_b, bt + 1)
                dve.wait_ge(f_ea, bt * E0 + 4)
                dve.tensor_tensor(acc[:, :, :], acc[:, :, :], psum[7][:, :].rearrange("p (t d) -> p t d", t=TT),
                                  ALU.add).then_inc(f_ba, 1)
                dve.wait_ge(f_ba, bt + 2)
                take_expert(2)
                take_expert(3)
                if follow:
                    next_scores(bt - 1)
                take_expert(4)
                if follow:
                    next_route(bt - 1, step)
                take_expert(5)
                dve.wait_ge(f_ea, bt * E0 + E0 + 2)
                step(dve.tensor_tensor(ta[:, :, :], abel[:, :, :],
                                       gc_bc[:, 0:1, :].broadcast_to([P, TT, D]), ALU.mult))
                step(dve.tensor_tensor(tb[:, :, :], acc[:, :, :],
                                       gc_bc[:, 1:2, :].broadcast_to([P, TT, D]), ALU.mult))
                step(dve.tensor_tensor(ta[:, :, :], ta[:, :, :], tb[:, :, :], ALU.add))
                step(dve.tensor_tensor(tb[:, :, :], acc[:, :, :], abel[:, :, :], ALU.subtract))
                dve.tensor_reduce(gz[:, :], ta[:, :, :], AX.X, ALU.add).then_inc(f_gz, 1)
                return k[0]

            first = batch_steps(0, 0, False)
            per = first + FOLLOW
            with dve.Fori(1, B) as bt:
                assert batch_steps(bt, bt * per + (first - per), True) == per
            step, _ = chain(first + (B - 1) * per)
            gate_mix(B - 1, step)
            finish(B - 1, step)
            next_norm(B - 1)
            next_scores(B - 1)
            next_route(B - 1, step)

        early.close()
        NB = -(-(NT + E1 - 1) // 3) * 3
        BB = NB // 3
        x_sorted = nc.dram_tensor("x_sorted", [NB * P, D], F32).ap()
        y_sorted = nc.dram_tensor("y_sorted", [NB * P, D], F32).ap()
        b1_bc = sb("b1_bc", [P, E1, H1])
        b2_bc = sb("b2_bc", [P, E1, D])
        zero = sb("zero", [P, D])
        tri = sb("tri", [P, P])
        ones = sb("ones", [P, P])
        thr = sb("thr", [P, NT])
        blk_no = sb("blk_no", [P, NB])
        cnt = sb("cnt", [P, E1])
        nblk, end, beg = (sb(n, [P, E1]) for n in ("nblk", "end", "beg"))
        slot_f = sb("slot_f", [P, NT])
        slot = sb("slot", [P, NT], mybir.dt.uint32)
        ex_f = sb("ex_f", [P, NB])
        ex = sb("ex", [P, NB], mybir.dt.int32)
        ld_b = sem("ld_b")
        t_cst = sem("t_cst")
        t_z = sem("t_z")
        t_mm = sem("t_mm")
        t_c = sem("t_c")
        t_slot = sem("t_slot")
        t_ex = sem("t_ex")
        t_sc = sem("t_sc")

        NS = 3
        ST = HEADS * TT
        SH = ST // 2
        HH = HEADS // 2
        TH = T // 2
        LAG = 4
        PB = 8
        hi = [sb(f"hi{i}", [P, 2, HH, HEADS, HT], F32R) for i in range(2)]
        ql = [sb(f"ql{i}", [P, HH, HEADS, HT], F32R) for i in range(2)]
        vt = sb("vt", [P, TT, HEADS, VD])
        vt_next = sb("vt_next", [P, TT, HEADS, VD])
        spare = sb("spare", [P, 1])
        oT = sb("oT", [P, T])
        pb = [sb(f"pb{i}", [P, T]) for i in range(PB)]
        view = lambda i, a, n: pb[i][:, a * n * E1:(a + 1) * n * E1]
        run, off = (view(PB - 1, a, NT).rearrange("p (e t) -> p e t", e=E1) for a in range(2))
        gtk, reset = (view(PB - 2, a, NT).rearrange("p (e t) -> p e t", e=E1) for a in range(2))
        leb = view(PB - 3, 0, NB).rearrange("p (k e) -> p k e", e=E1)
        vs = [sb(f"vs{i}", [P, D]) for i in range(PB)]
        nmx, zz, rz = (sb(n, [P, PB]) for n in ("nmx", "zz", "rz"))
        xd = sb("xd", [P, HEADS, 2, HT])
        s1 = sb("s1", [P, NT, D])
        part = lambda a, n: xn_all[:, a:a + n, :]
        row = lambda a, n=1: part(a, n).rearrange("p a d -> p (a d)")
        xg = [row(0), row(1)]
        xgT = row(2)
        ys = [row(3), row(4)]
        hs, hT = row(5, HC), row(5 + HC, HC)
        yg, th3, ob = (part(5 + 2 * HC + i * TT, TT) for i in range(3))
        slot_b = sb("slot_b", [P, TT], mybir.dt.uint32)

        n_xd = sem("n_xd")
        n_V = sem("n_V")
        n_Vs = sem("n_Vs")
        n_vt = sem("n_vt")
        n_qk = sem("n_qk")
        n_hi = sem("n_hi")
        n_lo = sem("n_lo")
        n_s = sem("n_s")
        n_mx = sem("n_mx")
        n_e = sem("n_e")
        n_rz = sem("n_rz")
        n_vs = sem("n_vs")
        n_av = sem("n_av")
        n_oT = sem("n_oT")
        n_T = sem("n_T")
        n_s1 = sem("n_s1")
        m_ld = [sem(f"m_ld{i}") for i in range(2)]
        m_T = sem("m_T")
        m_Ts = sem("m_Ts")
        m_up = sem("m_up")
        m_hs = sem("m_hs")
        m_hT = sem("m_hT")
        m_h = sem("m_h")
        m_dn = sem("m_dn")
        m_y = sem("m_y")
        m_st = [sem(f"m_st{i}") for i in range(2)]
        g_sl = sem("g_sl")
        g_y = sem("g_y")
        g_th = sem("g_th")
        g_c = sem("g_c")
        g_o = sem("g_o")
        g_st = sem("g_st")

        PAIR, HEADS_T, V_NEXT = range(3)
        SIDE = [[(0, PAIR), (2, PAIR), (4, PAIR), (5, HEADS_T), (6, PAIR), (8, PAIR), (10, PAIR), (12, PAIR),
                 (13, PAIR)],
                [(0, PAIR), (2, PAIR), (4, PAIR), (5, HEADS_T), (6, PAIR), (8, PAIR), (9, V_NEXT), (10, PAIR),
                 (11, V_NEXT), (12, PAIR), (13, PAIR)]]
        SIDE_USES = []
        side = {}
        for hb in range(2):
            for i, what in SIDE[hb]:
                num = sum(1 for w, _ in SIDE_USES if w == what)
                side[hb * SH + i] = (what, num, len(SIDE_USES))
                SIDE_USES.append((what, num))
        side_bank = lambda place: psum[(3, 5)[place % 2]]
        PAIRS = 2 * HEADS

        def side_free(eng, bt, place, last):
            q = place - 2
            what, num = SIDE_USES[q]
            if last and q >= 0 and what != HEADS_T and (num >= HEADS or what == V_NEXT):
                eng.wait_ge(n_lo, PAIRS * B)
            elif what == PAIR:
                eng.wait_ge(n_lo, bt * PAIRS + HEADS + num + 1 - (PAIRS if q < 0 else 0))
            elif what == V_NEXT:
                eng.wait_ge(n_Vs, bt * 2 + 2 + num + 1)
            else:
                eng.wait_ge(n_s1, bt * 2 + num + 1)

        NONE, BLOCKS, SUMS = range(3)
        GATHER_AT = (1, SH + 1)
        SUM_AT = (9, SH + 9)
        TURNS = 2 * ST
        AT = [2 + j * (TURNS - 7) // (BB - 1) for j in range(BB)]
        XT, UP, HTR, DN = range(4)
        turns = {}
        for j in range(BB):
            turns.setdefault(AT[j] - 2, []).append((j, XT))
            turns.setdefault(AT[j], []).append((j, UP))
            turns.setdefault((AT + [TURNS - 2])[j + 1] + 1, []).append((j, DN))
            turns.setdefault(AT[j] + 2, []).append((j, HTR))

        def uses(j):
            return j // 2, (BB + 1) // 2 if j % 2 == 0 else BB // 2

        def layer1(eng, body):
            body(0, NONE, False)
            eng.wait_ge(t_ex, 1)
            with eng.Fori(1, 4) as bt:
                body(bt, BLOCKS, False)
            with eng.Fori(4, B - 1) as bt:
                body(bt, SUMS, False)
            body(B - 1, SUMS, True)

        def half_tokens(bt, p):
            return bass.ds(bt * T + TH * (1 + p // HEADS), TH)

        @blk.gpsimd
        def _(pool):
            pool.wait_ge(f_x1, B)
            pool.wait_ge(f_dn, B * CH + NU)
            pool.wait_ge(f_s3, B + 2)
            pool.memset(zero[:, :], 0.0).then_inc(t_z, 1)
            pool.memset(ones[:, :], 1.0).then_inc(t_cst, 1)
            pool.memset(reset[:, :, :], 1.0).then_inc(t_cst, 1)
            pool.iota(thr[:, :], pattern=[[P, NT]], base=0, channel_multiplier=0,
                      allow_small_or_imprecise_dtypes=True).then_inc(t_cst, 1)
            pool.iota(blk_no[:, :], pattern=[[1, NB]], base=0, channel_multiplier=0,
                      allow_small_or_imprecise_dtypes=True).then_inc(t_cst, 1)
            pool.wait_ge(t_cst, 4)
            pool.memset(reset[:, :, 0:1], 0.0).then_inc(t_cst, 1)
            pool.affine_select(out=tri[:, :], in_=ones[:, :], compare_op=ALU.is_gt, fill=0.0, base=0,
                               pattern=[[1, P]], channel_multiplier=-1).then_inc(t_cst, 1)

            def body(bt, kind, last):
                for n in range(ST):
                    if n == 0:
                        pool.wait_ge(n_Vs, bt * 2 + 2)
                        pool.wait_ge(n_vs, bt * ST + PB)
                        pool.tensor_tensor(spare[:, :], ones[:, 0:1], ones[:, 0:1], ALU.mult)
                        pool.tensor_copy(vt[:, :, :, :], vt_next[:, :, :, :]).then_inc(n_vt, 1)
                        pool.wait_ge(n_vt, bt + 1)
                    if kind == SUMS and n in (1, ST // 2 + 1):
                        pool.wait_ge(g_sl, (bt - 4) * 2 + n // (ST // 2) + 1)
                    pool.wait_ge(n_rz, bt * ST + n + 1)
                    pool.wait_ge(n_av, bt * ST + n + 1)
                    pool.tensor_tensor(vs[n % PB][:, :], vt[:, n % TT, :, :].rearrange("p j d -> p (j d)"),
                                       rz[:, n % PB:n % PB + 1].broadcast_to([P, D]), ALU.mult).then_inc(n_vs, 1)
                    if kind == NONE:
                        if n == 0:
                            pool.wait_ge(t_slot, 1)
                            pool.wait_ge(t_z, 1 + 16)
                        pool.indirect_dma_start(
                            out=x_sorted, out_offset=bass.IndirectOffsetOnAxis(ap=slot[:, n:n + 1], axis=0),
                            in_=xn_all[:, n, :], in_offset=None).then_inc(t_sc, 16)
                    if kind == SUMS and n in (0, ST // 2):
                        k = (bt - 4) * 2 + n // (ST // 2)
                        if n == 0:
                            for par in range(2):
                                pool.wait_ge(m_st[par], 16 * 3 * uses(par)[1] + 16)
                        pool.wait_ge(g_o, k + 1)
                        pool.tensor_copy(slot_b[:, :], slot[:, bass.ds(k * TT, TT)]).then_inc(g_sl, 1)
                    t = n % SH - GATHER_AT[0]
                    if kind == SUMS and 0 <= t < TT:
                        pool.indirect_dma_start(
                            out=yg[:, t, :], out_offset=None, in_=y_sorted,
                            in_offset=bass.IndirectOffsetOnAxis(ap=slot_b[:, t:t + 1], axis=0)).then_inc(g_y, 16)

            layer1(pool, body)

        @blk.tensor
        def _(pe):
            pe.wait_ge(t_cst, 6)
            pe.wait_ge(f_s3, B + 2)
            pe.wait_ge(f_oh3, B)
            for i, w in enumerate((tri, ones)):
                mm = pe.matmul(psum[4][:, i * E1 * NT:(i + 1) * E1 * NT], w[:, :], oh_all[:, :, :].rearrange("p t e -> p e t"),
                               start=True, stop=True)
            mm.then_inc(t_mm, 1)

            def pair(bank, g, tokens):
                for i, w in enumerate((mq_d, mk_d)):
                    mm = pe.matmul(bank[:, i * TH:(i + 1) * TH], w[:, g, :, :].rearrange("p a k -> p (a k)"),
                                   xn2T[:, tokens], start=True, stop=True)
                mm.then_inc(n_qk, 1)

            def v_part(bank, v):
                for j in range(HH):
                    mm = pe.matmul(bank[:, j * P:(j + 1) * P], xd[:, v * HH + j, :, :].rearrange("p a k -> p (a k)"),
                                   mv[:, :], start=True, stop=True)
                mm.then_inc(n_V, 1)

            def turn_heads(bank, t):
                pe.wait_ge(n_oT, t + 1)
                for h in range(HH):
                    mm = pe.transpose(bank[:, h * P:(h + 1) * P], oT[:, h * P:(h + 1) * P], ident[:, :])
                mm.then_inc(n_T, 1)

            def value(bt, n):
                h, m = n % ST // TT, n % TT
                pe.wait_ge(n_vs, bt * ST + n + 1 + PB)
                if n % SH == 0:
                    pe.wait_ge(n_oT, bt * 2 + n // SH + 1)
                for c in range(TT):
                    mm = pe.matmul(psum[7][c * 2 * VD:(c + 1) * 2 * VD, h % HH * P:(h % HH + 1) * P],
                                   vs[n % PB][:, c * 2 * VD:(c + 1) * 2 * VD], pb[n % PB][:, c * P:(c + 1) * P],
                                   start=(n % SH == 0), stop=(m == TT - 1), skip_group_check=True)
                mm.then_inc(n_av, 1)

            pe.wait_ge(n_xd, 1)
            pe.wait_ge(mq_ok, 1)
            for v in range(2):
                v_part(side_bank(v), v)
            for g in range(HEADS):
                if g < 2:
                    pe.wait_ge(n_Vs, g + 1)
                else:
                    pe.wait_ge(n_lo, g - 1)
                pair(side_bank(g), g, bass.ds(0, TH))

            def body(bt, kind, last):
                def score(n):
                    h, m = n // TT, n % TT
                    if n % SH == 0:
                        pe.wait_ge(n_lo, bt * PAIRS + HEADS * (n // SH + 1))
                    before = n - NS if n >= NS else max(range(n, ST, NS)) - ST
                    pe.wait_ge(n_e, bt * ST + before + 1 + NS)
                    par, h = h // HH, h % HH
                    keys = hi[par][:, 1, h, 2 * m:2 * m + 2, :].rearrange("p a k -> p (a k)")
                    for i, q in enumerate((hi[par][:, 0, h, :, :], ql[par][:, h, :, :])):
                        mm = pe.matmul(psum[n % NS][:, :], keys, q.rearrange("p g k -> p (g k)"),
                                       start=(i == 0), stop=(i == 1))
                    mm.then_inc(n_s, 1)

                def beside(n):
                    what, num, place = side[n]
                    if what == PAIR and not (last and num >= HEADS):
                        side_free(pe, bt, place, last)
                        pair(side_bank(place), num % HEADS, half_tokens(bt, num))
                    elif what == V_NEXT and not last:
                        side_free(pe, bt, place, last)
                        pe.wait_ge(n_xd, bt + 2)
                        v_part(side_bank(place), num)
                    elif what == HEADS_T and not (kind == NONE and num == 0):
                        side_free(pe, bt, place, last)
                        turn_heads(side_bank(place), bt * 2 + num)

                def block(j, stage):
                    k = (bt - 1) * BB + j
                    if stage == XT:
                        n, per = uses(j)
                        pe.wait_ge(m_ld[j % 2], 16 * (n + 1) + 16 * per * (bt - 1))
                        pe.wait_ge(m_y, k + (2 if j == 0 else 1))
                        pe.transpose(psum[6][:, 0:P], xg[j % 2][:, :], ident[:, :]).then_inc(m_T, 1)
                    elif stage == UP:
                        e = pe.value_load(ex[0:1, bass.ds(k, 1)], min_val=0, max_val=E1 - 1)
                        pe.wait_ge(m_Ts, k + 1)
                        pe.wait_ge(m_h, k + 1)
                        pe.matmul(psum[4][:, :], xgT[:, :], w_1[:, bass.ds(e, 1), :].rearrange("p a h -> p (a h)"),
                                  start=True, stop=True).then_inc(m_up, 1)
                    elif stage == HTR:
                        pe.wait_ge(m_hs, k + 2)
                        for c in range(HC):
                            mm = pe.transpose(psum[4][:, c * P:(c + 1) * P], hs[:, c * P:(c + 1) * P], ident[:, :])
                        mm.then_inc(m_hT, 1)
                    else:
                        e = pe.value_load(ex[0:1, bass.ds(k, 1)], min_val=0, max_val=E1 - 1)
                        pe.wait_ge(m_h, k + 2)
                        if j == BB - 1:
                            pe.wait_ge(m_y, k + 2)
                        else:
                            pe.wait_ge(m_Ts, k + 2)
                        for c in range(HC):
                            mm = pe.matmul(psum[6][:, 0:D], hT[:, c * P:(c + 1) * P],
                                           w_2[:, bass.ds(e * HC + c, 1), :].rearrange("p a d -> p (a d)"),
                                           start=(c == 0), stop=(c == HC - 1))
                        mm.then_inc(m_dn, 1)

                for n in range(ST):
                    score(n)
                    if n in side:
                        beside(n)
                    for half in range(2):
                        for j, stage in turns.get(2 * n + half, []) if kind == BLOCKS else []:
                            block(j, stage)
                        if half == 0 and not (kind == NONE and n < LAG):
                            value(bt, n - LAG)

            layer1(pe, body)
            for n in range(-LAG, 0):
                value(B, n)
            pe.wait_ge(n_s1, B * 2)
            pe.wait_ge(n_lo, B * PAIRS)
            turn_heads(side_bank(0), B * 2)

        @blk.scalar
        def _(act):
            act.sem_inc(n_e, NS)
            act.sem_inc(n_oT, 1)
            act.sem_inc(m_y, 2)
            act.sem_inc(m_h, 1)
            act.sem_inc(m_dn, 1)
            act.wait_ge(f_x1, B)
            act.wait_ge(f_dn, B * CH + NU)
            act.wait_ge(f_s3, B + 2)

            def tokens_twice(bt):
                act.wait_ge(n_V, bt * 2)
                act.activation(xd[:, :, :, :], xn2T[:, bass.ds(bt * T, T)].rearrange("p (j k) -> p j k", j=HEADS)
                               .unsqueeze(2).broadcast_to([P, HEADS, 2, HT]), ACT.Copy).then_inc(n_xd, 1)

            def round_pair(bank, par, g, done):
                act.wait_ge(n_qk, done + 1)
                act.activation(hi[par][:, :, :, g, :], bank[:, :].rearrange("p (s h k) -> p s h k", s=2, h=HH),
                               ACT.Copy).then_inc(n_hi, 1)

            def take_values(t):
                act.wait_ge(n_av, t * SH + PB)
                act.wait_ge(n_T, t)
                act.activation(oT[:, :], psum[7][:, :], ACT.Copy).then_inc(n_oT, 1)

            act.activation(xd[:, :, :, :], xn2T[:, 0:T].rearrange("p (j k) -> p j k", j=HEADS)
                           .unsqueeze(2).broadcast_to([P, HEADS, 2, HT]), ACT.Copy).then_inc(n_xd, 1)
            for g in range(HEADS):
                round_pair(side_bank(g), 0, g, g)

            def body(bt, kind, last):
                def block(j, stage):
                    k = (bt - 1) * BB + j
                    if stage == XT:
                        act.wait_ge(m_T, k + 1 + 1)
                        act.wait_ge(m_up, k + 1)
                        act.activation(xgT[:, :], psum[6][:, 0:P], ACT.Copy).then_inc(m_Ts, 1)
                    elif stage == HTR:
                        act.wait_ge(m_hT, k + 1 + 1)
                        act.wait_ge(m_dn, k + 1)
                        act.activation(hT[:, :], psum[4][:, :], ACT.Relu).then_inc(m_h, 1)

                def tanh_y(k):
                    act.wait_ge(g_y, (k + 1) * 16 * TT)
                    act.wait_ge(g_o, k + 1)
                    act.activation(th3[:, :, :], yg[:, :, :], ACT.Tanh, scale=0.5).then_inc(g_th, 1)

                for n in range(ST):
                    act.wait_ge(n_mx, bt * ST + n + 1)
                    act.wait_ge(n_av, bt * ST + n + 1)
                    act.activation(pb[n % PB][:, :], psum[n % NS][:, :], ACT.Exp,
                                   bias=nmx[:, n % PB:n % PB + 1], scale=1.0,
                                   accum_out=zz[:, n % PB:n % PB + 1]).then_inc(n_e, 1)
                    what, num, place = side.get(n, (None, 0, 0))
                    if what == PAIR and not (last and num >= HEADS):
                        round_pair(side_bank(place), (1 + num // HEADS) % 2, num % HEADS, bt * PAIRS + HEADS + num)
                    if n % SH == LAG - 1 and not (kind == NONE and n < SH):
                        take_values(bt * 2 + n // SH)
                    if n == SH // 2 and not last:
                        tokens_twice(bt + 1)
                    for half in range(2):
                        for j, stage in turns.get(2 * n + half, []) if kind == BLOCKS else []:
                            block(j, stage)
                    if kind == SUMS and n in SUM_AT:
                        tanh_y((bt - 4) * 2 + n // SH)

            layer1(act, body)
            take_values(B * 2)

        @blk.vector
        def _(dve):
            dve.sem_inc(n_av, PB)
            dve.sem_inc(n_s1, 1)
            dve.sem_inc(n_T, 1)
            dve.sem_inc(m_hs, 1)
            dve.sem_inc(g_o, 1)
            dve.wait_ge(f_dn, B * CH + NU)
            dve.wait_ge(f_k3, B + 1)
            dve.wait_ge(t_cst, 6)
            dve.wait_ge(f_oh3, B)
            made = [0]

            def then(ins):
                ins.then_inc(t_c, 1)
                made[0] += 1
                dve.wait_ge(t_c, made[0])

            per_e = lambda a: a.unsqueeze(2).broadcast_to([P, E1, NT])
            et = lambda a: a[:, :, :].rearrange("p e t -> p (e t)")
            dve.wait_ge(t_mm, 1)
            pre = psum[4][:, 0:E1 * NT]
            tot = psum[4][:, E1 * NT:2 * E1 * NT]

            def counts():
                then(dve.tensor_tensor_scan(et(run), et(reset), tot, 0.0, ALU.mult, ALU.add))
                then(dve.tensor_tensor(et(off), et(run), tot, ALU.subtract))
                then(dve.tensor_tensor(et(off), et(off), pre, ALU.add))
                then(dve.tensor_copy(cnt[:, :], run[:, :, NT - 1]))
                then(dve.tensor_tensor(gtk[:, :, :], per_e(cnt[:, :]),
                                       thr[:, :].unsqueeze(1).broadcast_to([P, E1, NT]), ALU.is_gt))

            def first_blocks():
                then(dve.tensor_reduce(nblk[:, :], gtk[:, :, :], AX.X, ALU.add))
                then(dve.tensor_tensor_scan(end[:, :], ones[:, 0:E1], nblk[:, :], 0.0, ALU.mult, ALU.add))
                then(dve.tensor_tensor(beg[:, :], end[:, :], nblk[:, :], ALU.subtract))
                then(dve.tensor_scalar(beg[:, :], beg[:, :], float(P), None, ALU.mult))

            def slots():
                then(dve.tensor_tensor(off[:, :, :], off[:, :, :], per_e(beg[:, :]), ALU.add))
                then(dve.tensor_tensor(off[:, :, :], off[:, :, :], oh_all[:, :, :].rearrange("p t e -> p e t"),
                                       ALU.mult))
                then(dve.tensor_reduce(slot_f[:, :], off[:, :, :].rearrange("p e t -> p t e"), AX.X, ALU.add))
                dve.tensor_copy(slot[:, :], slot_f[:, :]).then_inc(t_slot, 1)

            def block_experts():
                then(dve.tensor_tensor(leb[:, :, :], end[:, :].unsqueeze(1).broadcast_to([P, NB, E1]),
                                       blk_no[:, :].unsqueeze(2).broadcast_to([P, NB, E1]), ALU.is_le))
                then(dve.tensor_reduce(ex_f[:, :], leb[:, :, :], AX.X, ALU.add))
                then(dve.tensor_scalar(ex_f[:, :], ex_f[:, :], float(E1 - 1), None, ALU.min))
                dve.tensor_copy(ex[:, :], ex_f[:, :]).then_inc(t_ex, 1)

            def store_v(bank, v, done):
                dve.wait_ge(n_V, done + 1)
                src = bank[:, :].rearrange("p (j m r d) -> p m j r d", j=HH, m=TT, r=2)
                for r in range(2):
                    ins = dve.tensor_copy(vt_next[r * HT:(r + 1) * HT, :, v * HH:(v + 1) * HH, :],
                                          src[r * HT:(r + 1) * HT, :, :, r, :])
                ins.then_inc(n_Vs, 1)

            def rest_of_pair(bank, par, g, done):
                dve.wait_ge(n_hi, done + 1)
                parts = bank[:, :].rearrange("p (s h k) -> p s h k", s=2, h=HH)
                dve.tensor_tensor(ql[par][:, :, g, :], parts[:, 0], hi[par][:, 0, :, g, :].bitcast(F32), ALU.subtract)
                low = hi[par][KS:P, 1, :, g, :]
                dve.tensor_tensor(low, parts[KS:P, 1], low.bitcast(F32), ALU.subtract).then_inc(n_lo, 1)

            def take_heads(bank, t):
                dve.wait_ge(n_T, t + 1)
                src = bank[:, :].rearrange("p (a b c j d) -> p b a c j d", a=2, b=2, c=TT, j=2)
                for half in range(2):
                    for j in range(2):
                        ins = dve.tensor_copy(
                            s1[half * HT:(half + 1) * HT, bass.ds(t * 2 - 2, 2), :]
                            .rearrange("p a (c j d) -> p a c j d", c=TT, j=2)[:, :, :, j, :],
                            src[j * HT:(j + 1) * HT, half, :, :, j, :])
                ins.then_inc(n_s1, 1)

            for v in range(2):
                store_v(side_bank(v), v, v)
            for g in range(HEADS):
                rest_of_pair(side_bank(g), 0, g, g)
                if g in (1, 3, 5, 7):
                    (counts, first_blocks, slots, block_experts)[g // 2]()
            dve.wait_ge(ld_b, 32)

            def sum_up(k, part):
                rows = bass.ds(k * TT, TT)
                if part == 0:
                    dve.wait_ge(g_th, k + 1)
                    dve.wait_ge(n_s1, k * 2 + 3)
                    dve.wait_ge(g_st, k * 16 + 16)
                    dve.scalar_tensor_tensor(ob[:, :, :], th3[:, :, :], 1.0, yg[:, :, :], ALU.add, ALU.mult)\
                       .then_inc(g_c, 1)
                elif part == 1:
                    dve.wait_ge(g_c, k * 2 + 1)
                    dve.scalar_tensor_tensor(ob[:, :, :], ob[:, :, :], 0.5, s1[:, rows, :], ALU.mult, ALU.mult)\
                       .then_inc(g_c, 1)
                else:
                    dve.wait_ge(g_c, k * 2 + 2)
                    dve.tensor_tensor(ob[:, :, :], ob[:, :, :], x_all[:, rows, :], ALU.add).then_inc(g_o, 1)

            def body(bt, kind, last):
                def maxima(n):
                    dve.wait_ge(n_s, bt * ST + n + 1)
                    dve.wait_ge(n_e, bt * ST + n + 1)
                    dve.tensor_reduce(nmx[:, n % PB:n % PB + 1], psum[n % NS][:, :], AX.X, ALU.max,
                                      negate=True).then_inc(n_mx, 1)

                def inverse(n):
                    dve.wait_ge(n_e, bt * ST + n + 1 + NS)
                    dve.wait_ge(n_vs, bt * ST + n + 1)
                    dve.reciprocal(rz[:, n % PB:n % PB + 1], zz[:, n % PB:n % PB + 1]).then_inc(n_rz, 1)

                def block(j, stage):
                    k = (bt - 1) * BB + j
                    if stage == UP:
                        e = dve.value_load(ex[0:1, bass.ds(k, 1)], min_val=0, max_val=E1 - 1)
                        dve.wait_ge(m_up, k + 1 + 1)
                        dve.wait_ge(m_hT, k + 1)
                        dve.tensor_tensor(hs[:, :], psum[4][:, :], b1_bc[:, bass.ds(e, 1), :].rearrange("p a h -> p (a h)"),
                                          ALU.add).then_inc(m_hs, 1)
                    elif stage == DN:
                        e = dve.value_load(ex[0:1, bass.ds(k, 1)], min_val=0, max_val=E1 - 1)
                        n, per = uses(j)
                        dve.wait_ge(m_st[j % 2], 16 * (n + 1) + 16 * per * (bt - 1))
                        dve.wait_ge(m_dn, k + 1 + 1)
                        dve.tensor_tensor(ys[j % 2][:, :], psum[6][:, 0:D],
                                          b2_bc[:, bass.ds(e, 1), :].rearrange("p a d -> p (a d)"), ALU.add)\
                           .then_inc(m_y, 1)

                for n in range(ST):
                    maxima(n)
                    if n or not kind == NONE:
                        inverse(n - 1)
                    what, num, place = side.get(n - 1, (None, 0, 0))
                    if what == PAIR and not (last and num >= HEADS):
                        rest_of_pair(side_bank(place), (1 + num // HEADS) % 2, num % HEADS, bt * PAIRS + HEADS + num)
                    what, num, place = side.get(n, (None, 0, 0))
                    if what == V_NEXT and not last:
                        if num == 0:
                            dve.wait_ge(n_vt, bt + 1)
                        store_v(side_bank(place), num, bt * 2 + 2 + num)
                    elif what == HEADS_T and not (kind == NONE and num == 0):
                        take_heads(side_bank(place), bt * 2 + num)
                    for half in range(2):
                        for j, stage in turns.get(2 * n + half, []) if kind == BLOCKS else []:
                            block(j, stage)
                    if kind == SUMS and 0 <= n % SH - SUM_AT[0] < 3 and not (last and n > SH):
                        sum_up((bt - 4) * 2 + n // SH, n % SH - SUM_AT[0])

            layer1(dve, body)
            dve.wait_ge(n_e, B * ST + NS)
            dve.wait_ge(n_vs, B * ST)
            dve.reciprocal(rz[:, PB - 1:PB], zz[:, PB - 1:PB]).then_inc(n_rz, 1)
            take_heads(side_bank(0), B * 2)
            for part in range(3):
                sum_up(B - 1, part)

        @blk.sync
        def _(sp):
            sp.sem_inc(n_vs, PB)
            sp.sem_inc(g_st, 16)
            for par in range(2):
                sp.sem_inc(m_st[par], 16)
            for s_ in (m_T, m_up, m_hT):
                sp.sem_inc(s_, 1)
            sp.wait_ge(f_x1, B)
            sp.wait_ge(f_dn, B * CH + NU)
            sp.wait_ge(f_k3, B + 1)
            sp.wait_ge(f_s3, B + 2)
            sp.dma_start(b1_bc[:, :, :], b1.rearrange("e h -> (e h)").partition_broadcast(P)).then_inc(ld_b, 16)
            sp.dma_start(b2_bc[:, :, :], b2.rearrange("e d -> (e d)").partition_broadcast(P)).then_inc(ld_b, 16)
            sp.wait_ge(t_z, 1)
            sp.dma_start(x_sorted.rearrange("(k p) d -> p k d", p=P), zero[:, :].unsqueeze(1).broadcast_to([P, NB, D]))\
              .then_inc(t_z, 16)
            sp.wait_ge(t_sc, 16 * NT)
            xs_v = x_sorted.rearrange("(k p) d -> p k d", p=P)
            ys_v = y_sorted.rearrange("(k p) d -> p k d", p=P)
            flat = lambda a: a.rearrange("p a d -> p (a d)")
            with sp.Fori(1, 4) as bt:
                def load(j):
                    k = (bt - 1) * BB + j
                    sp.wait_ge(m_T, k + (1 if j == 0 else 0))
                    sp.dma_start(xg[j % 2][:, :], flat(xs_v[:, bass.ds(k, 1), :])).then_inc(m_ld[j % 2], 16)

                load(0)
                load(1)
                for j in range(BB):
                    k = (bt - 1) * BB + j
                    if j + 2 < BB:
                        load(j + 2)
                    sp.wait_ge(m_y, k + 1 + 2)
                    sp.dma_start(flat(ys_v[:, bass.ds(k, 1), :]), ys[j % 2][:, :]).then_inc(m_st[j % 2], 16)
            ov = out.rearrange("b (t p) d -> p (b t) d", p=P)
            with sp.Fori(0, B) as k:
                sp.wait_ge(g_o, k + 2)
                sp.dma_start(ov[:, bass.ds(k * TT, TT), :], ob[:, :, :]).then_inc(g_st, 16)
            sp.wait_ge(g_st, 16 * B + 16)


_INS = ['L0_attn_x', 'L0_attn_W', 'L0_attn_b', 'L0_ffn_ln_g', 'L0_ffn_ln_b', 'L0_ffn_aw1', 'L0_ffn_ab1', 'L0_ffn_aw2',
        'L0_ffn_ab2', 'L0_ffn_gate_w', 'L0_ffn_gate_b', 'L0_ffn_ew1', 'L0_ffn_eb1', 'L0_ffn_ew2', 'L0_ffn_eb2',
        'L0_ffn_gens', 'L0_ffn_gc_w', 'L0_ffn_gc_b', 'L1_attn_Mq', 'L1_attn_Mk', 'L1_attn_Mv', 'L1_ffn_Wg', 'L1_ffn_bg',
        'L1_ffn_W1', 'L1_ffn_b1', 'L1_ffn_W2', 'L1_ffn_b2']
_OUTS = [((8, 512, 128), 'float32')]


def kernel(**inputs):
    import numpy as _np
    import concourse.bacc as _bacc
    from concourse import mybir as _mybir
    from concourse.bass_utils import run_bass_kernel_spmd as _run

    nc = _bacc.Bacc("TRN2", target_bir_lowering=False, num_devices=1)
    arrays, args = {}, []
    for name in _INS:
        a = _np.ascontiguousarray(inputs[name])
        arrays[f"in_{name}_dram"] = a
        args.append(nc.dram_tensor(f"in_{name}_dram", a.shape, _mybir.dt.from_np(a.dtype), kind="ExternalInput").ap())
    for i, (shape, dtype) in enumerate(_OUTS):
        dt = _mybir.dt.from_np(_np.dtype(dtype))
        args.append(nc.dram_tensor(f"out_{i}_dram", shape, dt, kind="ExternalOutput").ap())
    recurrent_d2_kernel(nc, *args)
    r = _run(nc, [arrays], core_ids=[0])
    got = tuple(r.results[0][f"out_{i}_dram"] for i in range(len(_OUTS)))
    return got[0]
```

```python
from contextlib import ExitStack

import concourse.bass as bass
from concourse import mybir

F32 = mybir.dt.float32
F32R = mybir.dt.float32r
ALU = mybir.AluOpType
ACT = mybir.ActivationFunctionType
AX = mybir.AxisListType

P = 128
EPS = 1e-5
BIG = 3.0e38
TAYLOR = 12
SQUARE = 4


def recurrent_d2_kernel(nc, x, W, b, ln_g, ln_b, aw1, ab1, aw2, ab2, gate_w, gate_b, ew1, eb1, ew2, eb2,
                        gens, gc_w, gc_b, Mq, Mk, Mv, Wg, bg, W1, b1, W2, b2, out):
    B, T, D = x.shape
    TT = T // P
    NT = B * TT
    AC = aw1.shape[1] // P
    E0, H0 = ew1.shape[0], ew1.shape[2]
    EC = H0 // P
    E1, H1 = W1.shape[0], W1.shape[2]
    HC = H1 // P
    G = gens.shape[0]
    HEADS = 8
    KS = Mq.shape[1] // HEADS
    HT = T // HEADS
    VD = D // HEADS
    SC0 = float(D) ** -0.5
    SC1 = float(KS) ** -0.5
    LOOPS = B // 2
    ROW_B, ROW_G, ROW_LB, ROW_AB1 = 0, 3, 4, 5
    ROW_EB1 = ROW_AB1 + AC
    ROW_B1 = ROW_EB1 + E0 * EC
    ROWS = ROW_B1 + E1 * HC

    with ExitStack() as ctx:
        def sb(name, shape, dt=F32):
            return ctx.enter_context(nc.sbuf_tensor(name, shape, dt))

        early = ctx.enter_context(ExitStack())

        def sbe(name, shape, dt=F32):
            return early.enter_context(nc.sbuf_tensor(name, shape, dt))

        def sem(name):
            return ctx.enter_context(nc.semaphore(name))

        x_all = sb("x_all", [P, NT, D])
        ident = sb("ident", [P, P])
        cols = sb("cols", [P, ROWS])
        mq_hi, mk_hi, mq_lo, mk_lo = (sb(n, [P, HEADS, 2, KS], F32R) for n in ("mq_hi", "mk_hi", "mq_lo", "mk_lo"))
        mv = sb("mv", [P, D])
        wg = sb("wg", [P, E1])
        bg_c = sb("bg_c", [E1, 1])
        w_1 = sb("w_1", [P, E1, H1])
        xn_all = sb("xn_all", [P, NT, D])
        xn2T = sb("xn2T", [P, B * T])
        oh_all = sb("oh_all", [P, NT, E1])
        w_2 = sb("w_2", [P, E1 * HC, D])
        b2_sb = sb("b2_sb", [E1, D])
        rev = sb("rev", [P, TT, E1])
        half_neg = sb("half_neg", [P, NT])
        s_all = sbe("s_all", [P, NT, D])
        lgT = sbe("lgT", [P, T])
        lgT3 = sbe("lgT3", [P, T])
        cmask = sbe("cmask", [P, P])
        rows = sbe("rows", [ROWS, P])
        bqs = sbe("bqs", [P, 1])
        coef = sbe("coef", [P, TAYLOR])
        w_qkv = sbe("w_qkv", [P, 3 * D])
        bv_bc = sbe("bv_bc", [P, D])
        m_raw = sbe("m_raw", [P, 2, HEADS, 2, KS])
        w_u1_hi, w_u1_lo = (sbe(n, [P, AC * P + E0 * H0], F32R) for n in ("w_u1_hi", "w_u1_lo"))
        w_a2 = sbe("w_a2", [P, AC, D])
        ab2_bc = sbe("ab2_bc", [P, D])
        w_gate = sbe("w_gate", [P, E0])
        gate_bc = sbe("gate_bc", [E0, 1])
        w_e2 = sbe("w_e2", [P, E0 * EC, D])
        w_e2T = sbe("w_e2T", [P, E0 * EC, D])
        eb2_sb = sbe("eb2_sb", [E0, D])
        eb2T = sbe("eb2T", [P, E0])
        eb2R = sbe("eb2R", [E0, D])
        gA = sbe("gA", [P, G, D])
        gAT = sbe("gAT", [P, G, D])
        gE = sbe("gE", [P, G, D])
        gET = sbe("gET", [P, G, D])
        rot = sbe("rot", [P, D])
        gc_bc = sbe("gc_bc", [P, 2, D])
        gcb_bc = sbe("gcb_bc", [P, 1])
        gcb_half = sbe("gcb_half", [P, 1])
        bn = sbe("bn", [P, NT, 6])
        mv_st = sbe("mv_st", [P, NT, 2])
        ve = sbe("ve", [P, NT])
        rs1 = sbe("rs1", [P, NT])
        rs2 = sbe("rs2", [P, NT])

        raw = early.enter_context(ExitStack())
        w_u1 = raw.enter_context(nc.sbuf_tensor("w_u1", [P, AC * P + E0 * H0], F32))

        psum = [ctx.enter_context(nc.psum_tensor(f"bank{i}", [P, T], F32)) for i in range(8)]

        ld_x = [sem(f"ld_x{i}") for i in range(B)]
        ld_w = sem("ld_w")
        ld_late = sem("ld_late")
        cst = sem("cst")
        blk = ctx.enter_context(nc.Block())

        col = lambda i: cols[:, i:i + 1]
        batch = lambda t, n, i: t[:, bass.ds(i * n, n)]

        N_LD, N_LATE = 16 * 20, 16 * 10

        u1_hi = sem("u1_hi")
        u1_lo = sem("u1_lo")
        colsT = sem("colsT")
        cols_ok = sem("cols_ok")
        bias_ok = sem("bias_ok")
        bn_ok = sem("bn_ok")
        st_ok = sem("st_ok")
        st_pool = sem("st_pool")
        e_mm = sem("e_mm")
        e_ev = sem("e_ev")
        r_mm = sem("r_mm")
        r_ev = sem("r_ev")

        @blk.sync
        def _(sp):
            xv = x.rearrange("b (t p) d -> p b t d", p=P)
            for i in range(B):
                sp.dma_start(x_all[:, i * TT:(i + 1) * TT, :], xv[:, i]).then_inc(ld_x[i], 16)
            rw = lambda a, n: a.rearrange("(c p) -> c p", p=P) if n else a
            sp.dma_start(gA[:, :, :], gens.rearrange("g r c -> r g c")).then_inc(ld_w, 16)
            sp.dma_start(rows[ROW_B:ROW_B + 3, :], rw(b, 3)).then_inc(ld_w, 16)
            sp.dma_start(rows[ROW_G:ROW_G + 1, :], rw(ln_g, 1)).then_inc(ld_w, 16)
            sp.dma_start(rows[ROW_LB:ROW_LB + 1, :], rw(ln_b, 1)).then_inc(ld_w, 16)
            sp.dma_start(rows[ROW_AB1:ROW_AB1 + AC, :], rw(ab1, AC)).then_inc(ld_w, 16)
            sp.dma_start(rows[ROW_EB1:ROW_EB1 + E0 * EC, :],
                         eb1.rearrange("e (c p) -> (e c) p", p=P)).then_inc(ld_w, 16)
            sp.dma_start(rows[ROW_B1:ROWS, :], b1.rearrange("e (c p) -> (e c) p", p=P)).then_inc(ld_w, 16)
            sp.dma_start(w_qkv[:, :], W).then_inc(ld_w, 16)
            sp.dma_start(bv_bc[:, :], b[2 * D:3 * D].partition_broadcast(P)).then_inc(ld_w, 16)
            sp.dma_start(w_u1[:, 0:AC * P], aw1).then_inc(ld_w, 16)
            sp.dma_start(w_a2[:, :, :], aw2.rearrange("(c p) d -> p c d", p=P)).then_inc(ld_w, 16)
            sp.dma_start(ab2_bc[:, :], ab2.partition_broadcast(P)).then_inc(ld_w, 16)
            sp.dma_start(w_gate[:, :], gate_w).then_inc(ld_w, 16)
            sp.dma_start(gate_bc[:, :], gate_b.rearrange("(e a) -> e a", a=1)).then_inc(ld_w, 16)
            sp.dma_start(w_u1[:, AC * P:].rearrange("p (e h) -> p e h", e=E0),
                         ew1.rearrange("e d h -> d e h")).then_inc(ld_w, 16)
            sp.dma_start(w_e2[:, :, :], ew2.rearrange("e (c p) d -> p (e c) d", p=P)).then_inc(ld_w, 16)
            sp.dma_start(eb2_sb[:, :], eb2).then_inc(ld_w, 16)
            sp.dma_start(gc_bc[:, 0, :], gc_w[0:D, :].rearrange("d a -> (d a)").partition_broadcast(P)).then_inc(ld_w, 16)
            sp.dma_start(gc_bc[:, 1, :], gc_w[D:2 * D, :].rearrange("d a -> (d a)").partition_broadcast(P)).then_inc(ld_w, 16)
            sp.dma_start(gcb_bc[:, :], gc_b.partition_broadcast(P)).then_inc(ld_w, 16)
            for m, src in enumerate((Mq, Mk)):
                for c in range(2):
                    sp.dma_start(m_raw[:, m, :, c, :], src.rearrange("d (r k) -> d r k", k=KS)).then_inc(ld_late, 16)
            sp.dma_start(mv[:, :], Mv).then_inc(ld_late, 16)
            sp.dma_start(wg[:, :], Wg).then_inc(ld_late, 16)
            sp.dma_start(bg_c[:, :], bg.rearrange("(e a) -> e a", a=1)).then_inc(ld_late, 16)
            sp.dma_start(w_1[:, :, :], W1.rearrange("e d h -> d e h")).then_inc(ld_late, 16)
            sp.dma_start(w_2[:, :, :], W2.rearrange("e (c p) d -> p (e c) d", p=P)).then_inc(ld_late, 16)
            sp.dma_start(b2_sb[:, :], b2).then_inc(ld_late, 16)

        @blk.gpsimd
        def _(pool):
            pool.memset(ident[:, :], 0.0).then_inc(cst, 1)
            pool.memset(cmask[:, :], 0.0).then_inc(cst, 1)
            pool.memset(half_neg[:, :], -0.5).then_inc(cst, 1)
            for e in range(E1):
                pool.memset(rev[:, :, e:e + 1], float(E1 - e)).then_inc(cst, 1)
            pool.memset(lgT[:, :], 0.0).then_inc(cst, 1)
            pool.memset(lgT3[:, :], 0.0).then_inc(cst, 1)
            pool.iota(coef[:, :], pattern=[[-1, TAYLOR]], base=TAYLOR, channel_multiplier=0,
                      allow_small_or_imprecise_dtypes=True).then_inc(cst, 1)
            pool.wait_ge(cst, 6 + E1)
            pool.affine_select(out=ident[:, :], in_=ident[:, :], compare_op=ALU.not_equal, fill=1.0,
                               base=0, pattern=[[-1, P]], channel_multiplier=1).then_inc(cst, 1)
            pool.affine_select(out=cmask[:, :], in_=cmask[:, :], compare_op=ALU.is_ge, fill=-9.0e15,
                               base=0, pattern=[[-1, P]], channel_multiplier=1).then_inc(cst, 1)
            pool.wait_ge(bn_ok, 1)
            n = [0]

            def step(ins):
                ins.then_inc(st_pool, 1)
                n[0] += 1
                pool.wait_ge(st_pool, n[0])

            var = mv_st[:, :, 1]
            step(pool.tensor_scalar(ve[:, :], var, EPS, None, ALU.add))
            step(pool.tensor_tensor(rs1[:, :], ve[:, :], half_neg[:, :], ALU.pow))
            step(pool.tensor_tensor(ve[:, :], rs1[:, :], rs1[:, :], ALU.mult))
            step(pool.tensor_tensor(ve[:, :], ve[:, :], var, ALU.mult))
            step(pool.tensor_scalar(ve[:, :], ve[:, :], EPS, None, ALU.add))
            pool.tensor_tensor(rs2[:, :], ve[:, :], half_neg[:, :], ALU.pow).then_inc(st_ok, 1)

        N_CST = 8 + E1

        @blk.tensor
        def _(pe):
            pe.wait_ge(cst, N_CST)
            pe.wait_ge(ld_w, N_LD)
            pe.transpose(psum[0][:, 0:ROWS], rows[:, :], ident[0:ROWS, 0:ROWS]).then_inc(colsT, 1)
            for g in range(G):
                mm = pe.transpose(psum[1][:, g * P:(g + 1) * P], gA[:, g, :], ident[:, :])
            mm.then_inc(e_mm, 1)
            for q in range(E0 * EC // 4):
                for i in range(4):
                    mm = pe.transpose(psum[5 + q][:, i * P:(i + 1) * P], w_e2[:, 4 * q + i, :], ident[:, :])
            mm.then_inc(r_mm, 1)
            pe.transpose(psum[2][:, 0:E0], eb2_sb[:, :], ident[0:E0, 0:E0]).then_inc(r_mm, 1)

        @blk.scalar
        def _(act):
            act.wait_ge(ld_w, N_LD)
            act.activation(w_u1_hi[:, :], w_u1[:, :], ACT.Copy).then_inc(u1_hi, 1)

        @blk.vector
        def _(dve):
            for i in range(B):
                dve.wait_ge(ld_x[i], 16)
                for t in range(i * TT, (i + 1) * TT):
                    dve.bn_stats(bn[:, t, :], x_all[:, t, :]).then_inc(bias_ok, 1)
            dve.wait_ge(bias_ok, NT)
            for t in range(NT):
                mm = dve.bn_aggr(mv_st[:, t, :], bn[:, t, :])
            mm.then_inc(bn_ok, 1)
            dve.wait_ge(colsT, 1)
            dve.tensor_copy(cols[:, :], psum[0][:, 0:ROWS]).then_inc(cols_ok, 1)
            dve.wait_ge(cols_ok, 1)
            dve.tensor_scalar(bqs[:, :], col(ROW_B), SC0, None, ALU.mult).then_inc(cols_ok, 1)
            dve.wait_ge(ld_w, N_LD)
            dve.tensor_scalar(gcb_half[:, :], gcb_bc[:, :], 0.5, None, ALU.mult).then_inc(cols_ok, 1)
            dve.wait_ge(e_mm, 1)
            dve.tensor_scalar(gAT[:, :, :], psum[1][:, :].rearrange("p (g d) -> p g d", g=G),
                              2.0 ** -SQUARE, None, ALU.mult).then_inc(cols_ok, 1)
            dve.wait_ge(cst, N_CST)
            dve.tensor_copy(gE[:, :, :], ident[:, :].unsqueeze(1).broadcast_to([P, G, D])).then_inc(cols_ok, 1)
            dve.reciprocal(coef[:, :], coef[:, :]).then_inc(cols_ok, 1)
            dve.wait_ge(cols_ok, 6)
            dve.engine_nop().then_inc(e_ev, 1)
            dve.wait_ge(r_mm, 1)
            for q in range(E0 * EC // 4):
                mm = dve.tensor_copy(w_e2T[:, 4 * q:4 * q + 4, :],
                                     psum[5 + q][:, :].rearrange("p (i d) -> p i d", i=4))
            mm.then_inc(r_ev, 1)
            dve.wait_ge(r_mm, 2)
            dve.tensor_copy(eb2T[:, :], psum[2][:, 0:E0]).then_inc(r_ev, 1)
            dve.wait_ge(u1_hi, 1)
            dve.tensor_tensor(w_u1_lo[:, :], w_u1[:, :], w_u1_hi[:, :].bitcast(F32),
                              ALU.subtract).then_inc(u1_lo, 1)


        raw.close()
        first = early.enter_context(ExitStack())

        def sbf(name, shape, dt=F32):
            return first.enter_context(nc.sbuf_tensor(name, shape, dt))

        xs = [sbf(f"xs{i}", [P, TT, D]) for i in range(2)]
        xh = [sbf(f"xh{i}", [P, TT, D]) for i in range(2)]
        xT = [sbf(f"xT{i}", [P, T]) for i in range(2)]
        qT = [sbf(f"qT{i}", [P, T]) for i in range(2)]
        kT = [sbf(f"kT{i}", [P, T]) for i in range(2)]
        va = [sbf(f"va{i}", [P, TT, D]) for i in range(2)]
        pr = [sbf(f"pr{i}", [P, T]) for i in range(2)]
        prT = [sbf(f"prT{i}", [P, T]) for i in range(2)]
        VBANK = (7, 3)
        nm0 = sbf("nm0", [P, 2])
        z0 = sbf("z0", [P, 2])
        rz0 = sbf("rz0", [P, 2])
        a_xs = sem("a_xs")
        a_xh = sem("a_xh")
        a_keep = sem("a_keep")
        a_T = sem("a_T")
        a_xT = sem("a_xT")
        a_x2T = sem("a_x2T")
        a_qkv = sem("a_qkv")
        a_q = sem("a_q")
        a_v = sem("a_v")
        a_s = sem("a_s")
        a_dm = sem("a_dm")
        a_mx = sem("a_mx")
        a_p = sem("a_p")
        a_rz = sem("a_rz")
        a_pT = sem("a_pT")
        a_pTs = sem("a_pTs")
        a_o = sem("a_o")
        a_os = sem("a_os")

        @blk.gpsimd
        def _(pool):
            with pool.Fori(0, LOOPS) as i:
                for par in range(2):
                    bt = 2 * i + par
                    pool.wait_ge(a_T, bt * 2 + 2)
                    for t in range(TT):
                        pool.wait_ge(a_xs, bt * TT + t + 1)
                        pool.tensor_tensor(xh[par][:, t, :], xs[par][:, t, :],
                                           rs2[:, bass.ds(bt * TT + t, 1)].broadcast_to([P, D]), ALU.mult)\
                            .then_inc(a_xh, 1)
                    pool.tensor_copy(xn_all[:, bass.ds(bt * TT, TT), :], xs[par][:, :, :]).then_inc(a_keep, 1)

        ROUNDS = 2
        assert ROUNDS * (B - 2) == TAYLOR
        TURNED, SQUARED = TAYLOR, TAYLOR + 1
        e_done = lambda r: r + 1 if r <= SQUARED else SQUARED + 1 + 2 * (r - SQUARED)
        LAST = SQUARED + SQUARE + G - 1

        def phase1(eng, batch):
            with eng.Fori(0, LOOPS - 1) as i:
                for par in range(2):
                    batch(2 * i + par, par, True, {1: [(2 * i + par) * ROUNDS], 8: [(2 * i + par) * ROUNDS + 1]})
            batch(B - 2, 0, True, {1: [TURNED], 8: [SQUARED]})
            batch(B - 1, 1, False, {1: [SQUARED + 1], 3: [SQUARED + 2], 5: [SQUARED + 3], 7: [SQUARED + 4],
                                    8: [SQUARED + 5], 9: [SQUARED + 6]})

        @blk.tensor
        def _(pe):
            pe.wait_ge(r_ev, 2)
            pe.wait_ge(e_ev, 1)

            def turn_xs(bt, par):
                pe.wait_ge(a_xs, (bt + 1) * TT)
                pe.wait_ge(a_xT, bt + 1)
                for t in range(TT):
                    mm = pe.transpose(psum[0][:, t * P:(t + 1) * P], xs[par][:, t, :], ident[:, :])
                mm.then_inc(a_T, 1)

            def turn_xh(bt, par):
                pe.wait_ge(a_xh, (bt + 1) * TT)
                pe.wait_ge(a_x2T, bt + 1)
                for t in range(TT):
                    mm = pe.transpose(psum[1][:, t * P:(t + 1) * P], xh[par][:, t, :], ident[:, :])
                mm.then_inc(a_T, 1)

            def exp_round(r, bank):
                if not isinstance(r, int) or r < TURNED:
                    pe.wait_ge(e_ev, r + 1)
                    for g in range(G):
                        mm = pe.matmul(psum[bank][:, g * P:(g + 1) * P], gAT[:, g, :], gE[:, g, :],
                                       start=True, stop=True)
                elif r == TURNED:
                    pe.wait_ge(e_ev, e_done(r))
                    for g in range(G):
                        mm = pe.transpose(psum[bank][:, g * P:(g + 1) * P], gE[:, g, :], ident[:, :])
                elif r < SQUARED + SQUARE:
                    pe.wait_ge(e_ev, e_done(r))
                    for g in range(G):
                        pe.matmul(psum[0][:, g * P:(g + 1) * P], gET[:, g, :], gE[:, g, :], start=True, stop=True)
                    for g in range(G):
                        mm = pe.matmul(psum[1][:, g * P:(g + 1) * P], gE[:, g, :], gET[:, g, :], start=True, stop=True)
                else:
                    n = r - SQUARED - SQUARE
                    pe.wait_ge(e_ev, e_done(SQUARED + SQUARE))
                    if n:
                        pe.wait_ge(r_ev, 2 + n)
                    g = G - 2 - n
                    mm = pe.matmul(psum[0][:, 0:D], gET[:, g, :], gE[:, G - 1, :] if n == 0 else rot[:, :],
                                   start=True, stop=True)
                mm.then_inc(e_mm, 1)

            turn_xs(0, 0)
            turn_xh(0, 0)

            def batch(bt, par, more, rounds):
                def after(i):
                    for r in rounds.get(i, []):
                        if i == 1:
                            pe.wait_ge(a_xT, bt + 2)
                            pe.wait_ge(a_x2T, bt + 2)
                        elif more:
                            pe.wait_ge(a_xT, bt + 3)
                            pe.wait_ge(a_x2T, bt + 3)
                        exp_round(r, 0 if i == 1 else 1)

                pe.wait_ge(a_xT, bt + 2)
                pe.wait_ge(a_v, bt + 1)
                pe.matmul(psum[2][:, :], w_qkv[:, 0:D], xT[par][:, :], start=True, stop=True).then_inc(a_qkv, 1)
                pe.wait_ge(a_os, bt * TT + 2)
                pe.matmul(psum[3][:, :], w_qkv[:, D:2 * D], xT[par][:, :], start=True, stop=True).then_inc(a_qkv, 1)
                after(1)
                pe.wait_ge(a_q, bt * 2 + 3)
                for t in range(TT):
                    mm = pe.matmul(psum[2][:, t * P:(t + 1) * P], xT[par][:, t * P:(t + 1) * P],
                                   w_qkv[:, 2 * D:3 * D], start=True, stop=True)
                mm.then_inc(a_qkv, 1)
                pe.wait_ge(a_q, bt * 2 + 4)

                def scores(t):
                    pe.wait_ge(a_p, bt * TT + t + 1)
                    pe.matmul(psum[4 + t % 2][:, 0:(t + 1) * P], qT[par][:, t * P:(t + 1) * P],
                              kT[par][:, 0:(t + 1) * P], start=True, stop=True).then_inc(a_s, 1)

                def turn(t):
                    pe.wait_ge(a_p, bt * TT + t + 3)
                    pe.wait_ge(a_pTs, bt * TT + t + 1)
                    for c in range(t + 1):
                        mm = pe.transpose(psum[6][:, c * P:(c + 1) * P], pr[t % 2][:, c * P:(c + 1) * P],
                                          ident[:, :])
                    mm.then_inc(a_pT, 1)

                def values(t):
                    pe.wait_ge(a_pTs, bt * TT + t + 2)
                    if t == 0:
                        pe.wait_ge(a_v, bt + 2)
                    pe.wait_ge(a_os, bt * TT + t + 1)
                    for c in range(t + 1):
                        mm = pe.matmul(psum[VBANK[t % 2]][:, 0:P], prT[t % 2][:, c * P:(c + 1) * P],
                                       va[par][:, c, :], start=(c == 0), stop=(c == t))
                    mm.then_inc(a_o, 1)

                scores(0)
                scores(1)
                if more:
                    pe.wait_ge(e_ev, e_done(rounds[1][0] + 1) if isinstance(bt, int) else rounds[1][0] + 2)
                    turn_xs(bt + 1, 1 - par)
                after(3)
                turn(0)
                scores(2)
                if more:
                    turn_xh(bt + 1, 1 - par)
                turn(1)
                after(5)
                values(0)
                scores(3)
                after(7)
                turn(2)
                values(1)
                after(8)
                turn(3)
                values(2)
                after(9)
                values(3)

            phase1(pe, batch)
            pe.wait_ge(e_mm, 1 + LAST)
            pe.wait_ge(r_ev, 2 + G - 1)
            pe.wait_ge(a_p, B * TT + 2)
            pe.wait_ge(a_pTs, B * TT + 1)
            for q in range(E0 * EC // 4):
                for i in range(4):
                    mm = pe.matmul(psum[4 + q][:, i * P:(i + 1) * P], w_e2T[:, 4 * q + i, :], rot[:, :],
                                   start=True, stop=True)
                mm.then_inc(r_mm, 1)
            pe.matmul(psum[1][0:E0, 0:D], eb2T[:, :], rot[:, :], start=True, stop=True).then_inc(r_mm, 1)

        @blk.scalar
        def _(act):
            act.sem_inc(a_xT, 1)
            act.sem_inc(a_q, 2)
            act.sem_inc(a_p, 2)
            act.wait_ge(cols_ok, 2)

            def store_xT(bt, par):
                act.wait_ge(a_T, bt * 2 + 1 + 4)
                act.activation(xT[par][:, :], psum[0][:, :], ACT.Copy).then_inc(a_xT, 1)

            store_xT(0, 0)

            def batch(bt, par, more, rounds):
                act.wait_ge(a_qkv, bt * 3 + 1)
                act.activation(qT[par][:, :], psum[2][:, :], ACT.Identity, bias=bqs[:, 0:1], scale=SC0)\
                    .then_inc(a_q, 1)
                act.wait_ge(a_qkv, bt * 3 + 2)
                act.activation(kT[par][:, :], psum[3][:, :], ACT.Identity, bias=col(ROW_B + 1), scale=1.0)\
                    .then_inc(a_q, 1)
                for t in range(TT):
                    act.wait_ge(a_mx, bt * TT + t + 1)
                    act.wait_ge(a_pT, bt * TT + t + 1)
                    act.wait_ge(a_rz, bt * TT + t + 1)
                    act.activation(pr[t % 2][:, 0:(t + 1) * P], psum[4 + t % 2][:, 0:(t + 1) * P], ACT.Exp,
                                   bias=nm0[:, t % 2:t % 2 + 1], scale=1.0,
                                   accum_out=z0[:, t % 2:t % 2 + 1]).then_inc(a_p, 1)
                    if t == 1 and more:
                        store_xT(bt + 1, 1 - par)

            phase1(act, batch)

        @blk.vector
        def _(dve):
            dve.sem_inc(a_T, 4)
            dve.sem_inc(a_x2T, 1)
            dve.sem_inc(a_v, 1)
            dve.sem_inc(a_pT, 2)
            dve.sem_inc(a_rz, 2)
            dve.sem_inc(a_pTs, 1)
            dve.sem_inc(a_os, 2)
            dve.wait_ge(st_ok, 1)
            groups = lambda a: a.rearrange("p (g d) -> p g d", g=G)

            def norm(bt, par):
                dve.wait_ge(a_T, bt * 2 + 1)
                dve.wait_ge(a_keep, bt + 1)
                for t in range(TT):
                    g = bt * TT + t
                    dve.tensor_scalar(xs[par][:, t, :], x_all[:, bass.ds(g, 1), :].rearrange("p a d -> p (a d)"),
                                      mv_st[:, bass.ds(g, 1), 0], rs1[:, bass.ds(g, 1)],
                                      ALU.subtract, ALU.mult).then_inc(a_xs, 1)

            def store_x2T(bt):
                dve.wait_ge(a_T, bt * 2 + 2 + 4)
                dve.tensor_scalar(xn2T[:, bass.ds(bt * T, T)], psum[1][:, :], col(ROW_G), col(ROW_LB),
                                  ALU.mult, ALU.add).then_inc(a_x2T, 1)

            def store_round(r, bank):
                dve.wait_ge(e_mm, r + 2)
                if not isinstance(r, int) or r < TURNED:
                    dve.scalar_tensor_tensor(gE[:, :, :], groups(psum[bank][:, :]), coef[:, bass.ds(r, 1)],
                                             ident[:, :].unsqueeze(1).broadcast_to([P, G, D]),
                                             ALU.mult, ALU.add).then_inc(e_ev, 1)
                elif r == TURNED:
                    dve.tensor_copy(gET[:, :, :], groups(psum[bank][:, :])).then_inc(e_ev, 1)
                elif r < SQUARED + SQUARE:
                    dve.tensor_copy(gE[:, :, :], groups(psum[0][:, :])).then_inc(e_ev, 1)
                    dve.tensor_copy(gET[:, :, :], groups(psum[1][:, :])).then_inc(e_ev, 1)
                else:
                    dve.tensor_copy(rot[:, :], psum[0][:, 0:D]).then_inc(r_ev, 1)

            dve.wait_ge(u1_lo, 1)
            norm(0, 0)
            store_x2T(0)

            def batch(bt, par, more, rounds):
                def after(i):
                    for r in rounds.get(i, []):
                        store_round(r, 0 if i == 1 else 1)

                if more:
                    norm(bt + 1, 1 - par)
                after(1)
                dve.wait_ge(a_qkv, bt * 3 + 3)
                dve.tensor_tensor(va[par][:, :, :], psum[2][:, :].rearrange("p (t d) -> p t d", t=TT),
                                  bv_bc[:, :].unsqueeze(1).broadcast_to([P, TT, D]), ALU.add).then_inc(a_v, 1)

                def top(t):
                    s = psum[4 + t % 2]
                    dve.wait_ge(a_s, bt * TT + t + 1)
                    dve.tensor_tensor(s[:, t * P:(t + 1) * P], s[:, t * P:(t + 1) * P], cmask[:, :],
                                      ALU.add).then_inc(a_dm, 1)
                    dve.wait_ge(a_dm, bt * TT + t + 1)
                    dve.wait_ge(a_p, bt * TT + t + 1)
                    dve.tensor_reduce(nm0[:, t % 2:t % 2 + 1], s[:, 0:(t + 1) * P], AX.X, ALU.max,
                                      negate=True).then_inc(a_mx, 1)

                def store_turned(t):
                    dve.wait_ge(a_pT, bt * TT + t + 3)
                    dve.wait_ge(a_o, bt * TT + t + 1)
                    dve.wait_ge(a_os, bt * TT + t + 1)
                    dve.tensor_copy(prT[t % 2][:, 0:(t + 1) * P], psum[6][:, 0:(t + 1) * P]).then_inc(a_pTs, 1)
                    dve.reciprocal(rz0[:, t % 2:t % 2 + 1], z0[:, t % 2:t % 2 + 1]).then_inc(a_rz, 1)

                def store_values(t):
                    dve.wait_ge(a_rz, bt * TT + t + 3)
                    dve.wait_ge(a_o, bt * TT + t + 3)
                    dve.tensor_scalar(s_all[:, bass.ds(bt * TT + t, 1), :].rearrange("p a d -> p (a d)"),
                                      psum[VBANK[t % 2]][:, 0:P], rz0[:, t % 2:t % 2 + 1], None,
                                      ALU.mult).then_inc(a_os, 1)

                top(0)
                top(1)
                after(3)
                store_turned(0)
                top(2)
                if more:
                    store_x2T(bt + 1)
                store_turned(1)
                after(5)
                store_values(0)
                top(3)
                after(7)
                store_turned(2)
                store_values(1)
                after(8)
                store_turned(3)
                store_values(2)
                after(9)
                store_values(3)

            phase1(dve, batch)
            for q in range(E0 * EC // 4):
                dve.wait_ge(r_mm, 3 + q)
                dve.tensor_copy(w_e2[:, 4 * q:4 * q + 4, :],
                                psum[4 + q][:, :].rearrange("p (i d) -> p i d", i=4)).then_inc(r_ev, 1)
            dve.wait_ge(r_mm, 3 + E0 * EC // 4)
            dve.tensor_copy(eb2R[:, :], psum[1][0:E0, 0:D]).then_inc(r_ev, 1)

        @blk.sync
        def _(sp):
            sp.sem_inc(a_keep, 2)
            sp.sem_inc(a_o, 2)

        first.close()
        NU = 4
        CH = AC + E0 * EC
        NEXT = (10, 12, 14)
        hid = [sbe(f"hid{i}", [P, T]) for i in range(NU)]
        lg0, oh1, oh2, tie, wf = (sbe(n, [P, TT, E0]) for n in ("lg0", "oh1", "oh2", "tie", "wf"))
        m1, m2, dm, th, w1t, w2t, gz, gt = (sbe(n, [P, TT]) for n in ("m1", "m2", "dm", "th", "w1t", "w2t", "gz", "gt"))
        wT = sbe("wT", [E1, T])
        acc, abel, ta, tb, tanh_r = (sbe(n, [P, TT, D]) for n in ("acc", "abel", "ta", "tb", "tanh_r"))
        mq_ok = sem("mq_ok")
        m_hi = sem("m_hi")
        m_lo = sem("m_lo")
        f_xh = sem("f_xh")
        f_xl = sem("f_xl")
        f_lg = sem("f_lg")
        f_lgs = sem("f_lgs")
        f_c = sem("f_c")
        f_dm = sem("f_dm")
        f_th = sem("f_th")
        f_w = sem("f_w")
        f_wT = sem("f_wT")
        f_wTs = sem("f_wTs")
        f_b = sem("f_b")
        f_ba = sem("f_ba")
        f_up = sem("f_up")
        f_h = sem("f_h")
        f_dn = sem("f_dn")
        f_ab = sem("f_ab")
        f_ea = sem("f_ea")
        f_gz = sem("f_gz")
        f_gt = sem("f_gt")
        f_r = sem("f_r")
        f_tr = sem("f_tr")
        f_x1 = sem("f_x1")
        f_v3 = sem("f_v3")
        f_r3 = sem("f_r3")
        f_xs3 = sem("f_xs3")
        f_k3 = sem("f_k3")
        f_T3 = sem("f_T3")
        f_Ts3 = sem("f_Ts3")
        f_lg3 = sem("f_lg3")
        f_lgs3 = sem("f_lgs3")
        f_s3 = sem("f_s3")
        f_oh3 = sem("f_oh3")
        xb_hi, xb_lo = (sbe(n, [P, T], F32R) for n in ("xb_hi", "xb_lo"))
        xs3 = sbe("xs3", [P, TT, D])
        sc3, tie3 = (sbe(n, [P, TT, E1]) for n in ("sc3", "tie3"))
        mm3, mt3, ve3, r3 = (sbe(n, [P, TT]) for n in ("mm3", "mt3", "ve3", "r3"))
        bn3 = sbe("bn3", [P, TT, 6])
        mv3 = sbe("mv3", [P, TT, 2])

        @blk.gpsimd
        def _(pool):
            pool.wait_ge(ld_late, N_LATE)
            pool.tensor_scalar(m_raw[:, 0], m_raw[:, 0], SC1, None, ALU.mult).then_inc(mq_ok, 1)
            pool.wait_ge(mq_ok, 1)
            for m, (hi_, lo_) in enumerate(((mq_hi, mq_lo), (mk_hi, mk_lo))):
                pool.tensor_copy(hi_[:, :, :, :], m_raw[:, m]).then_inc(m_hi, 1)
            pool.wait_ge(m_hi, 2)
            for m, (hi_, lo_) in enumerate(((mq_hi, mq_lo), (mk_hi, mk_lo))):
                pool.tensor_tensor(lo_[:, :, :, :], m_raw[:, m], hi_[:, :, :, :].bitcast(F32), ALU.subtract)\
                    .then_inc(m_lo, 1)
            with pool.Fori(0, B) as bt:
                pool.wait_ge(f_v3, bt + 1)
                pool.tensor_tensor(r3[:, :], ve3[:, :], half_neg[:, 0:TT], ALU.pow).then_inc(f_r3, 1)
                pool.wait_ge(f_xs3, bt + 1)
                pool.tensor_copy(xn_all[:, bass.ds(bt * TT, TT), :], xs3[:, :, :]).then_inc(f_k3, 1)

        @blk.tensor
        def _(pe):
            pe.wait_ge(a_os, B * TT + 2)
            pe.wait_ge(r_ev, 2 + G - 1 + E0 * EC // 4 + 1)
            pe.wait_ge(a_x2T, B + 1)
            pe.wait_ge(ld_late, N_LATE)

            def next_T(bt):
                pe.wait_ge(f_xs3, bt + 1)
                pe.wait_ge(f_ba, bt + 2)
                for t in range(TT):
                    mm = pe.transpose(psum[7][:, t * P:(t + 1) * P], xs3[:, t, :], ident[:, :])
                mm.then_inc(f_T3, 1)

            def next_scores(bt):
                pe.wait_ge(f_Ts3, bt + 1)
                pe.matmul(psum[7][0:E1, :], wg[:, :], xn2T[:, bass.ds(bt * T, T)], start=True, stop=True)\
                  .then_inc(f_lg3, 1)

            def next_turn(bt):
                pe.wait_ge(f_lgs3, bt + 1)
                for t in range(TT):
                    mm = pe.transpose(psum[7][:, t * P:(t + 1) * P], lgT3[:, t * P:(t + 1) * P], ident[:, :])
                mm.then_inc(f_lg3, 1)

            def batch_products(bt, follow):
                xb = xn2T[:, bass.ds(bt * T, T)]

                def up(n):
                    pe.wait_ge(f_h, bt * CH + n + 1)
                    if n == 0:
                        pe.wait_ge(f_xl, bt + 1)
                    for i, (w, x_) in enumerate(((w_u1_hi, xb_hi), (w_u1_hi, xb_lo), (w_u1_lo, xb_hi))):
                        mm = pe.matmul(psum[n % NU][:, :], w[:, n * P:(n + 1) * P], x_[:, :],
                                       start=(i == 0), stop=(i == 2))
                    mm.then_inc(f_up, 1)

                def down(n):
                    pe.wait_ge(f_h, bt * CH + n + 1 + NU)
                    if n < AC:
                        dst, w, first, last = psum[4], w_a2[:, n, :], n == 0, n == AC - 1
                        if first:
                            pe.wait_ge(f_ab, bt + 1)
                    else:
                        e, c = (n - AC) // EC, (n - AC) % EC
                        dst, w, first, last = psum[5 + e % 2], w_e2[:, n - AC, :], c == 0, c == EC - 1
                        if first:
                            pe.wait_ge(f_ea, bt * E0 + e + 1)
                    for t in range(TT):
                        mm = pe.matmul(dst[:, t * P:(t + 1) * P], hid[n % NU][:, t * P:(t + 1) * P], w,
                                       start=(first and t == 0), stop=last, skip_group_check=True)
                    mm.then_inc(f_dn, 1)

                pe.wait_ge(f_ba, bt + 1)
                pe.wait_ge(f_s3, bt + 1)
                pe.matmul(psum[7][0:E0, :], w_gate[:, :], xb, start=True, stop=True).then_inc(f_lg, 1)
                up(0)
                up(1)
                for n in range(CH):
                    if n + 2 < CH:
                        up(n + 2)
                    down(n)
                    if n == 1:
                        pe.wait_ge(f_lgs, bt + 1)
                        for t in range(TT):
                            mm = pe.transpose(psum[7][:, t * P:(t + 1) * P], lgT[:, t * P:(t + 1) * P], ident[:, :])
                        mm.then_inc(f_lg, 1)
                    if n == 7:
                        pe.wait_ge(f_w, bt + 1)
                        for t in range(TT):
                            mm = pe.transpose(psum[7][0:E0, t * P:(t + 1) * P], wf[:, t, :], ident[:, :])
                        mm.then_inc(f_wT, 1)
                    if n == 9:
                        pe.wait_ge(f_wTs, bt + 1)
                        for t in range(TT):
                            mm = pe.matmul(psum[7][:, t * P:(t + 1) * P], wT[0:E0, t * P:(t + 1) * P], eb2R[:, :],
                                           start=True, stop=True)
                        mm.then_inc(f_b, 1)
                    if follow and n in NEXT:
                        if n == NEXT[0]:
                            pe.wait_ge(f_ba, bt + 2)
                        (next_T, next_scores, next_turn)[NEXT.index(n)](bt - 1)

            batch_products(0, False)
            with pe.Fori(1, B) as bt:
                batch_products(bt, True)
            next_T(B - 1)
            next_scores(B - 1)
            next_turn(B - 1)

        @blk.scalar
        def _(act):
            act.sem_inc(f_h, NU)
            act.wait_ge(cols_ok, 3)

            def round_x(bt):
                act.wait_ge(f_up, bt * CH)
                act.activation(xb_hi[:, :], xn2T[:, bass.ds(bt * T, T)], ACT.Copy).then_inc(f_xh, 1)

            act.wait_ge(a_os, B * TT + 2)
            act.wait_ge(a_keep, B + 2)
            act.activation(xb_hi[:, :], xn2T[:, 0:T], ACT.Copy).then_inc(f_xh, 1)

            def gate_tanh(bt):
                act.wait_ge(f_gz, bt + 1)
                act.activation(gt[:, :], gz[:, :], ACT.Tanh, bias=gcb_half[:, 0:1], scale=0.5).then_inc(f_gt, 1)

            def silu_tanh(bt):
                act.wait_ge(f_r, bt + 1)
                act.activation(tanh_r[:, :, :], ta[:, :, :], ACT.Tanh, scale=0.5).then_inc(f_tr, 1)

            def next_store(bt):
                act.wait_ge(f_T3, bt + 2)
                act.activation(xn2T[:, bass.ds(bt * T, T)], psum[7][:, :], ACT.Copy).then_inc(f_Ts3, 1)

            def chunks(bt, follow, more=True):
                for n in range(CH):
                    act.wait_ge(f_up, bt * CH + n + 1)
                    act.wait_ge(f_dn, bt * CH + n + 1)
                    act.activation(hid[n % NU][:, :], psum[n % NU][:, :], ACT.Gelu,
                                   bias=col((ROW_AB1 if n < AC else ROW_EB1 - AC) + n), scale=1.0).then_inc(f_h, 1)
                    if n == 3 and follow:
                        gate_tanh(bt - 1)
                    if n == 4:
                        act.wait_ge(f_dm, bt + 1)
                        act.activation(th[:, :], dm[:, :], ACT.Tanh, scale=0.5).then_inc(f_th, 1)
                    if n == 6 and follow:
                        silu_tanh(bt - 1)
                    if n == NEXT[0] + 2 and follow:
                        next_store(bt - 1)
                if more:
                    round_x(bt + 1)

            chunks(0, False)
            with act.Fori(1, B - 1) as bt:
                chunks(bt, True)
            chunks(B - 1, True, False)
            gate_tanh(B - 1)
            silu_tanh(B - 1)
            next_store(B - 1)

        @blk.vector
        def _(dve):
            dve.sem_inc(f_dn, NU)
            dve.sem_inc(f_T3, 1)
            dve.sem_inc(f_k3, 1)
            dve.sem_inc(f_ab, 1)
            dve.sem_inc(f_ba, 1)
            dve.sem_inc(f_ea, 2)
            dve.sem_inc(f_s3, 2)
            dve.wait_ge(a_keep, B + 2)
            b3 = lambda a: a.unsqueeze(2).broadcast_to([P, TT, E0])
            FOLLOW = TT + 1 + 2 + 2 + 4

            def chain(base):
                k = [0]

                def step(ins, last=False):
                    ins.then_inc(f_c, 1)
                    k[0] += 1
                    dve.wait_ge(f_c, base + k[0])
                return step, k

            def gate_mix(bt, step):
                dve.wait_ge(f_gt, bt + 1)
                step(dve.tensor_scalar(gt[:, :], gt[:, :], 0.5, 0.5, ALU.mult, ALU.add))
                for t in range(TT):
                    step(dve.scalar_tensor_tensor(ta[:, t, :], tb[:, t, :], gt[:, t:t + 1], abel[:, t, :],
                                                  ALU.mult, ALU.add))
                dve.tensor_tensor(ta[:, :, :], ta[:, :, :], xn_all[:, bass.ds(bt * TT, TT), :], ALU.add)\
                   .then_inc(f_r, 1)

            def finish(bt, step):
                dve.wait_ge(f_tr, bt + 1)
                step(dve.scalar_tensor_tensor(ta[:, :, :], tanh_r[:, :, :], 1.0, ta[:, :, :], ALU.add, ALU.mult))
                step(dve.scalar_tensor_tensor(ta[:, :, :], ta[:, :, :], 0.5, s_all[:, bass.ds(bt * TT, TT), :],
                                              ALU.mult, ALU.mult))
                xb = x_all[:, bass.ds(bt * TT, TT), :]
                dve.tensor_tensor(xb, xb, ta[:, :, :], ALU.add).then_inc(f_x1, 1)

            def next_stats(bt, step):
                dve.wait_ge(f_x1, bt + 1)
                xt = lambda t: x_all[:, bass.ds(bt * TT + t, 1), :].rearrange("p a d -> p (a d)")
                dve.memset(ve3[:, 0:TT // 2], EPS)
                for t in range(TT):
                    ins = dve.bn_stats(bn3[:, t, :], xt(t))
                step(ins)
                dve.memset(ve3[:, TT // 2:TT], EPS)
                for t in range(TT):
                    ins = dve.bn_aggr(mv3[:, t, :], bn3[:, t, :])
                step(ins)
                dve.tensor_tensor(ve3[:, :], ve3[:, :], mv3[:, :, 1], ALU.add).then_inc(f_v3, 1)

            def next_norm(bt):
                xt = lambda t: x_all[:, bass.ds(bt * TT + t, 1), :].rearrange("p a d -> p (a d)")
                dve.wait_ge(f_T3, bt + 1)
                dve.wait_ge(f_k3, bt + 1)
                dve.wait_ge(f_r3, bt + 1)
                for t in range(TT):
                    ins = dve.tensor_scalar(xs3[:, t, :], xt(t), mv3[:, t, 0:1], r3[:, t:t + 1],
                                            ALU.subtract, ALU.mult)
                ins.then_inc(f_xs3, 1)

            def next_scores(bt):
                dve.wait_ge(f_lg3, bt * 2 + 1)
                dve.tensor_scalar(lgT3[0:E1, :], psum[7][0:E1, :], bg_c[:, 0:1], None, ALU.add).then_inc(f_lgs3, 1)

            def next_route(bt, step):
                d3 = lambda a: a.unsqueeze(2).broadcast_to([P, TT, E1])
                dve.wait_ge(f_lg3, bt * 2 + 2)
                dve.tensor_copy(sc3[:, :, :], psum[7][:, :].rearrange("p (t q) -> p t q", t=TT)[:, :, 0:E1])\
                   .then_inc(f_s3, 1)
                dve.wait_ge(f_s3, bt + 3)
                step(dve.tensor_reduce(mm3[:, :], sc3[:, :, :], AX.X, ALU.max))
                step(dve.tensor_tensor(tie3[:, :, :], sc3[:, :, :], d3(mm3[:, :]), ALU.is_equal))
                step(dve.tensor_tensor(tie3[:, :, :], tie3[:, :, :], rev[:, :, :], ALU.mult))
                step(dve.tensor_reduce(mt3[:, :], tie3[:, :, :], AX.X, ALU.max))
                dve.tensor_tensor(oh_all[:, bass.ds(bt * TT, TT), :], tie3[:, :, :], d3(mt3[:, :]), ALU.is_equal)\
                   .then_inc(f_oh3, 1)

            def rest_of_x(bt):
                dve.wait_ge(f_xh, bt + 1)
                dve.tensor_tensor(xb_lo[:, :], xn2T[:, bass.ds(bt * T, T)], xb_hi[:, :].bitcast(F32),
                                  ALU.subtract).then_inc(f_xl, 1)

            rest_of_x(0)

            def batch_steps(bt, base, follow, more=True):
                step, k = chain(base)
                dve.wait_ge(f_lg, bt * 2 + 1)
                dve.tensor_scalar(lgT[0:E0, :], psum[7][0:E0, :], gate_bc[:, 0:1], None, ALU.add).then_inc(f_lgs, 1)
                dve.wait_ge(f_lg, bt * 2 + 2)
                step(dve.tensor_copy(lg0[:, :, :], psum[7][:, :].rearrange("p (t q) -> p t q", t=TT)[:, :, 0:E0]))

                def best(scores, m, oh):
                    step(dve.tensor_reduce(m[:, :], scores, AX.X, ALU.max))
                    step(dve.tensor_tensor(tie[:, :, :], scores, b3(m[:, :]), ALU.is_equal))
                    step(dve.tensor_tensor(tie[:, :, :], tie[:, :, :], rev[:, :, 0:E0], ALU.mult))
                    step(dve.tensor_reduce(w1t[:, :], tie[:, :, :], AX.X, ALU.max))
                    step(dve.tensor_tensor(oh[:, :, :], tie[:, :, :], b3(w1t[:, :]), ALU.is_equal))

                best(lg0[:, :, :], m1, oh1)
                step(dve.scalar_tensor_tensor(lg0[:, :, :], oh1[:, :, :], -BIG, lg0[:, :, :], ALU.mult, ALU.add))
                best(lg0[:, :, :], m2, oh2)
                dve.tensor_tensor(dm[:, :], m2[:, :], m1[:, :], ALU.subtract).then_inc(f_dm, 1)
                if follow:
                    gate_mix(bt - 1, step)
                dve.wait_ge(f_th, bt + 1)
                step(dve.tensor_scalar(w2t[:, :], th[:, :], 0.5, 0.5, ALU.mult, ALU.add))
                step(dve.tensor_scalar(w1t[:, :], th[:, :], -0.5, 0.5, ALU.mult, ALU.add))
                step(dve.tensor_tensor(oh1[:, :, :], oh1[:, :, :], b3(w1t[:, :]), ALU.mult))
                step(dve.tensor_tensor(oh2[:, :, :], oh2[:, :, :], b3(w2t[:, :]), ALU.mult))
                dve.tensor_tensor(wf[:, :, :], oh1[:, :, :], oh2[:, :, :], ALU.add).then_inc(f_w, 1)
                if follow:
                    finish(bt - 1, step)

                def take_expert(e):
                    dve.wait_ge(f_dn, bt * CH + AC + (e + 1) * EC + NU)
                    if e:
                        dve.wait_ge(f_ea, bt * E0 + e + 2)
                    for t in range(TT):
                        y = psum[5 + e % 2][:, t * P:(t + 1) * P]
                        if e:
                            ins = dve.scalar_tensor_tensor(acc[:, t, :], y, wf[:, t, e:e + 1], acc[:, t, :],
                                                           ALU.mult, ALU.add)
                        else:
                            ins = dve.tensor_scalar(acc[:, t, :], y, wf[:, t, 0:1], None, ALU.mult)
                    ins.then_inc(f_ea, 1)

                dve.wait_ge(f_w, bt + 1)
                take_expert(0)
                if follow:
                    next_stats(bt - 1, step)
                dve.wait_ge(f_wT, bt + 1)
                dve.tensor_copy(wT[0:E0, :], psum[7][0:E0, :]).then_inc(f_wTs, 1)
                if follow:
                    next_norm(bt - 1)
                dve.wait_ge(f_dn, bt * CH + AC + NU)
                dve.tensor_tensor(abel[:, :, :], psum[4][:, :].rearrange("p (t d) -> p t d", t=TT),
                                  ab2_bc[:, :].unsqueeze(1).broadcast_to([P, TT, D]), ALU.add).then_inc(f_ab, 1)
                take_expert(1)
                dve.wait_ge(f_b, bt + 1)
                dve.wait_ge(f_ea, bt * E0 + 4)
                dve.tensor_tensor(acc[:, :, :], acc[:, :, :], psum[7][:, :].rearrange("p (t d) -> p t d", t=TT),
                                  ALU.add).then_inc(f_ba, 1)
                dve.wait_ge(f_ba, bt + 2)
                take_expert(2)
                take_expert(3)
                if follow:
                    next_scores(bt - 1)
                take_expert(4)
                if follow:
                    next_route(bt - 1, step)
                if more:
                    rest_of_x(bt + 1)
                take_expert(5)
                dve.wait_ge(f_ea, bt * E0 + E0 + 2)
                step(dve.tensor_tensor(ta[:, :, :], abel[:, :, :],
                                       gc_bc[:, 0:1, :].broadcast_to([P, TT, D]), ALU.mult))
                step(dve.tensor_tensor(tb[:, :, :], acc[:, :, :],
                                       gc_bc[:, 1:2, :].broadcast_to([P, TT, D]), ALU.mult))
                step(dve.tensor_tensor(ta[:, :, :], ta[:, :, :], tb[:, :, :], ALU.add))
                step(dve.tensor_tensor(tb[:, :, :], acc[:, :, :], abel[:, :, :], ALU.subtract))
                dve.tensor_reduce(gz[:, :], ta[:, :, :], AX.X, ALU.add).then_inc(f_gz, 1)
                return k[0]

            first = batch_steps(0, 0, False)
            per = first + FOLLOW
            with dve.Fori(1, B - 1) as bt:
                assert batch_steps(bt, bt * per + (first - per), True) == per
            batch_steps(B - 1, (B - 1) * per + (first - per), True, False)
            step, _ = chain(first + (B - 1) * per)
            gate_mix(B - 1, step)
            finish(B - 1, step)
            next_stats(B - 1, step)
            next_norm(B - 1)
            next_scores(B - 1)
            next_route(B - 1, step)

        early.close()
        NB = NT + E1 - 1
        x_sorted = nc.dram_tensor("x_sorted", [NB * P, D], F32).ap()
        y_sorted = nc.dram_tensor("y_sorted", [NB * P, D], F32).ap()
        b2_bc = sb("b2_bc", [P, E1, D])
        zero = sb("zero", [P, D])
        tri = sb("tri", [P, P])
        ones = sb("ones", [P, P])
        thr = sb("thr", [P, NT])
        blk_no = sb("blk_no", [P, NB])
        cnt = sb("cnt", [P, E1])
        nblk, end, beg = (sb(n, [P, E1]) for n in ("nblk", "end", "beg"))
        slot_f = sb("slot_f", [P, NT])
        slot = sb("slot", [P, NT], mybir.dt.uint32)
        ex_f = sb("ex_f", [P, NB])
        ex = sb("ex", [P, NB], mybir.dt.int32)
        ld_b = sem("ld_b")
        t_cst = sem("t_cst")
        t_z = sem("t_z")
        t_mm = sem("t_mm")
        t_c = sem("t_c")
        t_slot = sem("t_slot")
        t_ex = sem("t_ex")
        t_sc = sem("t_sc")

        NS = 3
        ST = HEADS * TT
        SH = ST // 2
        HH = HEADS // 2
        TH = T // 2
        LO_LAG = 2
        LAG = 5
        PB = 8
        hi = [sb(f"hi{i}", [P, 2, HH, HEADS, HT], F32R) for i in range(2)]
        ql = [sb(f"ql{i}", [P, HH, HEADS, HT], F32R) for i in range(2)]
        xp_hi, xp_lo = ([sb(f"{n}{i}", [P, TH], F32R) for i in range(2)] for n in ("xp_hi", "xp_lo"))
        vt = sb("vt", [P, TT, HEADS, VD])
        vt_next = sb("vt_next", [P, TT, HEADS, VD])
        oT = sb("oT", [P, T])
        pb = [sb(f"pb{i}", [P, T]) for i in range(PB)]
        view = lambda i, a, n: pb[i][:, a * n * E1:(a + 1) * n * E1]
        run, off = (view(PB - 1, a, NT).rearrange("p (e t) -> p e t", e=E1) for a in range(2))
        gtk, reset = (view(PB - 2, a, NT).rearrange("p (e t) -> p e t", e=E1) for a in range(2))
        leb = view(PB - 3, 0, NB).rearrange("p (k e) -> p k e", e=E1)
        vs = [sb(f"vs{i}", [P, D]) for i in range(PB)]
        nmx, zz, rz = (sb(n, [P, PB]) for n in ("nmx", "zz", "rz"))
        xd = sb("xd", [P, HEADS, 2, HT])
        s1 = sb("s1", [P, NT, D])
        part = lambda a, n: xn_all[:, a:a + n, :]
        row = lambda a, n=1: part(a, n).rearrange("p a d -> p (a d)")
        xg, xgT, ys = ([row(a), row(a + 1)] for a in (0, 2, 4))
        hs, hT = ([row(a, HC), row(a + HC, HC)] for a in (6, 6 + 2 * HC))
        yg, th3, ob = (part(i * TT, TT) for i in range(3))
        slot_b = sb("slot_b", [P, TT], mybir.dt.uint32)

        n_xd = sem("n_xd")
        n_V = sem("n_V")
        n_Vs = sem("n_Vs")
        n_vt = sem("n_vt")
        n_qk = sem("n_qk")
        n_xh = sem("n_xh")
        n_xl = sem("n_xl")
        n_hi = sem("n_hi")
        n_lo = sem("n_lo")
        n_s = sem("n_s")
        n_mx = sem("n_mx")
        n_e = sem("n_e")
        n_rz = sem("n_rz")
        n_vs = sem("n_vs")
        n_av = sem("n_av")
        n_oT = sem("n_oT")
        n_T = sem("n_T")
        n_s1 = sem("n_s1")
        m_ld = [sem(f"m_ld{i}") for i in range(2)]
        m_T = sem("m_T")
        m_Ts = sem("m_Ts")
        m_up = sem("m_up")
        m_hs = sem("m_hs")
        m_hT = sem("m_hT")
        m_h = sem("m_h")
        m_dn = sem("m_dn")
        m_y = sem("m_y")
        m_st = [sem(f"m_st{i}") for i in range(2)]
        g_sl = sem("g_sl")
        g_y = sem("g_y")
        g_th = sem("g_th")
        g_c = sem("g_c")
        g_o = sem("g_o")
        g_st = sem("g_st")

        PAIR_AT, HEADS_AT, V_AT = (0, 1, 3, 5, 7, 9, 11, 12), 7, (SH + 10, SH + 14)
        pair_of = {hb * SH + i: hb * HEADS + g for hb in range(2) for g, i in enumerate(PAIR_AT)}
        PAIRS = 2 * HEADS
        pair_bank = lambda p: psum[(3, 5)[p % 2]]
        SCORE, HEADS_T, V_NEXT = range(3)
        RING = []
        for n in range(ST):
            RING.append((SCORE, n))
            if n % SH == HEADS_AT:
                RING.append((HEADS_T, n // SH))
            if n in V_AT:
                RING.append((V_NEXT, V_AT.index(n)))
        assert len(RING) % NS == 0
        ring_bank = lambda what, num: psum[RING.index((what, num)) % NS]

        def made(what, num, first, last):
            return not (what == HEADS_T and num == 0 and first or what == V_NEXT and last)

        def ring_free(eng, bt, what, num, kind, last):
            q = RING.index((what, num)) - NS
            while q >= 0 and not made(*RING[q], kind == FIRST, last):
                q -= NS
            what, num = RING[q]
            b = -1 if q < 0 else 0
            if what == SCORE:
                eng.wait_ge(n_e, bt * ST + b * ST + num + 1 + NS)
            elif what == V_NEXT:
                eng.wait_ge(n_Vs, bt * 2 + b * 2 + 2 + num + 1)
            else:
                eng.wait_ge(n_s1, bt * 2 + b * 2 + num + 1)

        FIRST, PLAIN, SUMS = range(3)
        BEFORE = 2
        GATHER_AT = (3, SH + 3)
        SUM_AT = (10, SH + 10)
        LOAD = -2
        XT, UP, HTR, DN = range(4)

        def blocks(eng, make):
            def step(i, par):
                for d in (LOAD, HTR, UP, XT, DN):
                    if not isinstance(i, int) or 0 <= i - d < NB:
                        make(d, i - d, (par - d) % 2)

            make(LOAD, 0, 0)
            make(LOAD, 1, 1)
            for i in range(4):
                step(i, i % 2)
            with eng.Fori(2, NB // 2 - 1) as half:
                for par in range(2):
                    step(half * 2 + par, par)
            for i in range(NB // 2 * 2 - 2, NB + DN):
                step(i, i % 2)

        def layer1(eng, body, make=None, enter=None, leave=None):
            body(0, FIRST, False)
            for bt in range(1, BEFORE):
                body(bt, PLAIN, False)
            if make:
                eng.wait_ge(t_ex, 1)
                if enter:
                    enter()
                blocks(eng, make)
                if leave:
                    leave()
            with eng.Fori(BEFORE, 4) as bt:
                body(bt, PLAIN, False)
            with eng.Fori(4, B - 1) as bt:
                body(bt, SUMS, False)
            body(B - 1, SUMS, True)

        def half_tokens(half):
            return bass.ds(half * TH, TH)

        SPLIT_AT = 4

        @blk.gpsimd
        def _(pool):
            pool.wait_ge(f_x1, B)
            pool.wait_ge(f_dn, B * CH + NU)
            pool.wait_ge(f_s3, B + 2)
            pool.memset(zero[:, :], 0.0).then_inc(t_z, 1)
            pool.memset(ones[:, :], 1.0).then_inc(t_cst, 1)
            pool.memset(reset[:, :, :], 1.0).then_inc(t_cst, 1)
            pool.iota(thr[:, :], pattern=[[P, NT]], base=0, channel_multiplier=0,
                      allow_small_or_imprecise_dtypes=True).then_inc(t_cst, 1)
            pool.iota(blk_no[:, :], pattern=[[1, NB]], base=0, channel_multiplier=0,
                      allow_small_or_imprecise_dtypes=True).then_inc(t_cst, 1)
            pool.wait_ge(t_cst, 4)
            pool.memset(reset[:, :, 0:1], 0.0).then_inc(t_cst, 1)
            pool.affine_select(out=tri[:, :], in_=ones[:, :], compare_op=ALU.is_gt, fill=0.0, base=0,
                               pattern=[[1, P]], channel_multiplier=-1).then_inc(t_cst, 1)

            def sum_up(k, part):
                rows = bass.ds(k * TT, TT)
                if part == 0:
                    pool.wait_ge(g_th, k * 2 + 2)
                    pool.wait_ge(g_st, k * 16 + 16)
                    pool.tensor_tensor(ob[:, :, :], th3[:, :, :], yg[:, :, :], ALU.mult).then_inc(g_c, 1)
                elif part == 1:
                    pool.wait_ge(n_s1, k * 2 + 3)
                    pool.wait_ge(g_c, k * 2 + 1)
                    pool.tensor_tensor(ob[:, :, :], ob[:, :, :], s1[:, rows, :], ALU.mult).then_inc(g_c, 1)
                else:
                    pool.wait_ge(g_c, k * 2 + 2)
                    pool.tensor_tensor(ob[:, :, :], ob[:, :, :], x_all[:, rows, :], ALU.add).then_inc(g_o, 1)

            def body(bt, kind, last):
                for n in range(ST):
                    if isinstance(bt, int) and bt < BEFORE:
                        if bt == 0 and n == 0:
                            pool.wait_ge(t_slot, 1)
                            pool.wait_ge(t_z, 1 + 16)
                        now = bt * ST + n
                        for g in range(min(now * 3 // 4, NT), min((now + 1) * 3 // 4, NT)):
                            pool.indirect_dma_start(
                                out=x_sorted, out_offset=bass.IndirectOffsetOnAxis(ap=slot[:, g:g + 1], axis=0),
                                in_=xn_all[:, g, :], in_offset=None).then_inc(t_sc, 16)
                    if n == 0:
                        pool.wait_ge(n_vt, bt + 1)
                    if kind == SUMS and n in (1, ST // 2 + 1):
                        pool.wait_ge(g_sl, (bt - 4) * 2 + n // (ST // 2) + 1)
                    pool.wait_ge(n_rz, bt * ST + n + 1)
                    pool.wait_ge(n_av, bt * ST + n + 1)
                    pool.tensor_tensor(vs[n % PB][:, :], vt[:, n % TT, :, :].rearrange("p j d -> p (j d)"),
                                       rz[:, n % PB:n % PB + 1].broadcast_to([P, D]), ALU.mult).then_inc(n_vs, 1)
                    if kind == SUMS and n in (0, ST // 2):
                        k = (bt - 4) * 2 + n // (ST // 2)
                        if n == 0:
                            for par in range(2):
                                pool.wait_ge(m_st[par], 16 * ((NB + 1 - par) // 2) + 16)
                        pool.wait_ge(g_o, k + 1)
                        pool.tensor_copy(slot_b[:, :], slot[:, bass.ds(k * TT, TT)]).then_inc(g_sl, 1)
                    t = n % SH - GATHER_AT[0]
                    if kind == SUMS and 0 <= t < TT:
                        pool.indirect_dma_start(
                            out=yg[:, t, :], out_offset=None, in_=y_sorted,
                            in_offset=bass.IndirectOffsetOnAxis(ap=slot_b[:, t:t + 1], axis=0)).then_inc(g_y, 16)

                    if kind == SUMS and 0 <= n % SH - SUM_AT[0] - 1 < 3 and not (last and n > SH):
                        sum_up((bt - 4) * 2 + n // SH, n % SH - SUM_AT[0] - 1)

            layer1(pool, body)
            for part in range(3):
                sum_up(B - 1, part)

        @blk.tensor
        def _(pe):
            pe.wait_ge(t_cst, 6)
            pe.wait_ge(f_s3, B + 2)
            pe.wait_ge(f_oh3, B)
            for i, w in enumerate((tri, ones)):
                mm = pe.matmul(psum[4][:, i * E1 * NT:(i + 1) * E1 * NT], w[:, :], oh_all[:, :, :].rearrange("p t e -> p e t"),
                               start=True, stop=True)
            mm.then_inc(t_mm, 1)

            def pair(bank, g, par):
                for i, (w_hi, w_lo) in enumerate(((mq_hi, mq_lo), (mk_hi, mk_lo))):
                    for j, (w, x_) in enumerate(((w_hi, xp_hi), (w_hi, xp_lo), (w_lo, xp_hi))):
                        mm = pe.matmul(bank[:, i * TH:(i + 1) * TH], w[:, g, :, :].rearrange("p a k -> p (a k)"),
                                       x_[par][:, :], start=(j == 0), stop=(j == 2))
                mm.then_inc(n_qk, 1)

            def v_part(bank, v):
                for j in range(HH):
                    mm = pe.matmul(bank[:, j * P:(j + 1) * P], xd[:, v * HH + j, :, :].rearrange("p a k -> p (a k)"),
                                   mv[:, :], start=True, stop=True)
                mm.then_inc(n_V, 1)

            def turn_heads(bank, t):
                pe.wait_ge(n_oT, t + 1)
                for h in range(HH):
                    mm = pe.transpose(bank[:, h * P:(h + 1) * P], oT[:, h * P:(h + 1) * P], ident[:, :])
                mm.then_inc(n_T, 1)

            def value(bt, n):
                h, m = n % ST // TT, n % TT
                pe.wait_ge(n_vs, bt * ST + n + 1 + PB)
                if n % SH == 0:
                    pe.wait_ge(n_oT, bt * 2 + n // SH + 1)
                for c in range(TT):
                    mm = pe.matmul(psum[7][c * 2 * VD:(c + 1) * 2 * VD, h % HH * P:(h % HH + 1) * P],
                                   vs[n % PB][:, c * 2 * VD:(c + 1) * 2 * VD], pb[n % PB][:, c * P:(c + 1) * P],
                                   start=(n % SH == 0), stop=(m == TT - 1), skip_group_check=True)
                mm.then_inc(n_av, 1)

            pe.wait_ge(n_xd, 1)
            pe.wait_ge(m_lo, 2)
            for v in range(2):
                v_part(pair_bank(v), v)
            pe.wait_ge(n_xl, 1)
            for g in range(HEADS):
                if g < 2:
                    pe.wait_ge(n_Vs, g + 1)
                else:
                    pe.wait_ge(n_lo, g - 1)
                pair(pair_bank(g), g, 0)

            def body(bt, kind, last):
                def score(n):
                    h, m = n // TT, n % TT
                    if n % SH == 0:
                        pe.wait_ge(n_lo, bt * PAIRS + HEADS * (n // SH + 1))
                    ring_free(pe, bt, SCORE, n, kind, last)
                    bank = ring_bank(SCORE, n)
                    par, h = h // HH, h % HH
                    keys = hi[par][:, 1, h, 2 * m:2 * m + 2, :].rearrange("p a k -> p (a k)")
                    for i, q in enumerate((hi[par][:, 0, h, :, :], ql[par][:, h, :, :])):
                        mm = pe.matmul(bank[:, :], keys, q.rearrange("p g k -> p (g k)"),
                                       start=(i == 0), stop=(i == 1))
                    mm.then_inc(n_s, 1)

                def next_pair(p):
                    if p % HEADS == 0:
                        pe.wait_ge(n_xl, bt * 2 + p // HEADS + 2)
                    pe.wait_ge(n_lo, bt * PAIRS + HEADS + p - 1)
                    pair(pair_bank(p), p % HEADS, 1 - p // HEADS)

                def next_v(v):
                    ring_free(pe, bt, V_NEXT, v, kind, last)
                    pe.wait_ge(n_xd, bt + 2)
                    v_part(ring_bank(V_NEXT, v), v)

                def heads_back(hb):
                    ring_free(pe, bt, HEADS_T, hb, kind, last)
                    turn_heads(ring_bank(HEADS_T, hb), bt * 2 + hb)

                for n in range(ST):
                    first = n % SH == 0
                    with_value = not (kind == FIRST and n < LAG)
                    if not first:
                        score(n)
                    if with_value and n % SH != LAG:
                        value(bt, n - LAG)
                    if n in pair_of and not (last and n >= SH):
                        next_pair(pair_of[n])
                    if first:
                        score(n)
                    if n in V_AT and not last:
                        next_v(V_AT.index(n))
                    if n % SH == HEADS_AT and not (kind == FIRST and n < SH):
                        heads_back(n // SH)
                    if with_value and n % SH == LAG:
                        value(bt, n - LAG)

            def expert(k):
                return pe.value_load(ex[0:1, bass.ds(k, 1)], min_val=0, max_val=E1 - 1)

            early_read = {}

            def make(stage, k, par):
                if stage == XT:
                    pe.wait_ge(m_ld[par], (k - par + 2) * 8)
                    pe.transpose(psum[3][:, 0:P], xg[par][:, :], ident[:, :]).then_inc(m_T, 1)
                elif stage == UP:
                    e = early_read.pop(UP) if UP in early_read else expert(k)
                    pe.wait_ge(m_Ts, k + 1)
                    pe.matmul(psum[(0, 1)[par]][:, :], xgT[par][:, :],
                              w_1[:, bass.ds(e, 1), :].rearrange("p a h -> p (a h)"),
                              start=True, stop=True).then_inc(m_up, 1)
                elif stage == HTR:
                    if not isinstance(k, int) or k + 1 < NB:
                        early_read[UP] = expert(k + 1)
                    pe.wait_ge(m_hs, k + 1)
                    for c in range(HC):
                        mm = pe.transpose(psum[(2, 4)[par]][:, c * P:(c + 1) * P], hs[par][:, c * P:(c + 1) * P],
                                          ident[:, :])
                    mm.then_inc(m_hT, 1)
                elif stage == DN:
                    e = expert(k)
                    pe.wait_ge(m_h, k + 1)
                    pe.wait_ge(m_y, k + 1)
                    for c in range(HC):
                        mm = pe.matmul(psum[(5, 6)[par]][:, 0:D], hT[par][:, c * P:(c + 1) * P],
                                       w_2[:, bass.ds(e * HC + c, 1), :].rearrange("p a d -> p (a d)"),
                                       start=(c == 0), stop=(c == HC - 1))
                    mm.then_inc(m_dn, 1)

            def enter():
                pe.wait_ge(n_lo, BEFORE * PAIRS + HEADS)
                pe.wait_ge(n_e, BEFORE * ST + NS)

            def leave():
                pe.wait_ge(m_y, NB + 2)

            layer1(pe, body, make, enter, leave)
            for n in range(-LAG, 0):
                value(B, n)
            pe.wait_ge(n_s1, B * 2)
            pe.wait_ge(n_lo, B * PAIRS)
            turn_heads(pair_bank(0), B * 2)

        @blk.scalar
        def _(act):
            act.sem_inc(n_e, NS)
            act.sem_inc(n_oT, 1)
            act.sem_inc(m_y, 2)
            act.sem_inc(m_dn, 2)
            act.wait_ge(f_x1, B)
            act.wait_ge(f_dn, B * CH + NU)
            act.wait_ge(f_s3, B + 2)

            def tokens_twice(bt):
                act.wait_ge(n_V, bt * 2)
                act.activation(xd[:, :, :, :], xn2T[:, bass.ds(bt * T, T)].rearrange("p (j k) -> p j k", j=HEADS)
                               .unsqueeze(2).broadcast_to([P, HEADS, 2, HT]), ACT.Copy).then_inc(n_xd, 1)

            def round_pair(bank, par, g, done):
                act.wait_ge(n_qk, done + 1)
                act.activation(hi[par][:, :, :, g, :], bank[:, :].rearrange("p (s h k) -> p s h k", s=2, h=HH),
                               ACT.Copy).then_inc(n_hi, 1)

            def take_values(t):
                act.wait_ge(n_av, t * SH + PB)
                act.wait_ge(n_T, t)
                act.activation(oT[:, :], psum[7][:, :], ACT.Copy).then_inc(n_oT, 1)

            act.activation(xd[:, :, :, :], xn2T[:, 0:T].rearrange("p (j k) -> p j k", j=HEADS)
                           .unsqueeze(2).broadcast_to([P, HEADS, 2, HT]), ACT.Copy).then_inc(n_xd, 1)
            def round_tokens(half, par):
                act.activation(xp_hi[par][:, :], xn2T[:, half_tokens(half)], ACT.Copy).then_inc(n_xh, 1)

            for half in range(2):
                round_tokens(half, half)
            for g in range(HEADS):
                round_pair(pair_bank(g), 0, g, g)

            def body(bt, kind, last):
                def tanh_y(k):
                    act.wait_ge(g_y, (k + 1) * 16 * TT)
                    act.wait_ge(g_o, k + 1)
                    act.activation(th3[:, :, :], yg[:, :, :], ACT.Tanh, scale=0.5).then_inc(g_th, 1)
                    act.wait_ge(g_th, k * 2 + 1)
                    act.activation(th3[:, :, :], th3[:, :, :], ACT.Copy, bias=0.5, scale=0.5).then_inc(g_th, 1)

                for n in range(ST):
                    if n % SH == LAG - 1 and not (kind == FIRST and n < SH):
                        take_values(bt * 2 + n // SH)
                    act.wait_ge(n_mx, bt * ST + n + 1)
                    act.wait_ge(n_av, bt * ST + n + 1)
                    act.activation(pb[n % PB][:, :], ring_bank(SCORE, n)[:, :], ACT.Exp,
                                   bias=nmx[:, n % PB:n % PB + 1], scale=1.0,
                                   accum_out=zz[:, n % PB:n % PB + 1]).then_inc(n_e, 1)
                    if n in pair_of and not (last and n >= SH):
                        p = pair_of[n]
                        round_pair(pair_bank(p), 1 - p // HEADS, p % HEADS, bt * PAIRS + HEADS + p)
                    if n == 2:
                        act.wait_ge(n_Vs, bt * 2 + 2)
                        act.wait_ge(n_vs, bt * ST + PB)
                        act.activation(vt[:, :, :, :], vt_next[:, :, :, :], ACT.Copy).then_inc(n_vt, 1)
                    if n == SH // 2 and not last:
                        tokens_twice(bt + 1)
                    if n % SH == SPLIT_AT and not last:
                        round_tokens(bt * 2 + n // SH + 2, n // SH)
                    if kind == SUMS and n in SUM_AT:
                        tanh_y((bt - 4) * 2 + n // SH)

            def make(stage, k, par):
                if stage == XT:
                    act.wait_ge(m_T, k + 3)
                    act.wait_ge(m_up, k + 1)
                    act.activation(xgT[par][:, :], psum[3][:, 0:P], ACT.Copy).then_inc(m_Ts, 1)
                elif stage == HTR:
                    e = act.value_load(ex[0:1, bass.ds(k, 1)], min_val=0, max_val=E1 - 1)
                    act.wait_ge(m_hT, k + 3)
                    act.wait_ge(m_dn, k + 1)
                    for c in range(HC):
                        ins = act.activation(hT[par][:, c * P:(c + 1) * P], psum[(2, 4)[par]][:, c * P:(c + 1) * P],
                                             ACT.Relu, bias=cols[:, bass.ds(e * HC + (ROW_B1 + c), 1)], scale=1.0)
                    ins.then_inc(m_h, 1)

            layer1(act, body, make)
            take_values(B * 2)

        @blk.vector
        def _(dve):
            dve.sem_inc(n_av, PB)
            dve.sem_inc(n_s1, 1)
            dve.sem_inc(n_T, 1)
            dve.sem_inc(g_o, 1)
            dve.wait_ge(f_dn, B * CH + NU)
            dve.wait_ge(f_k3, B + 1)
            dve.wait_ge(t_cst, 6)
            dve.wait_ge(f_oh3, B)
            made = [0]

            def then(ins):
                ins.then_inc(t_c, 1)
                made[0] += 1
                dve.wait_ge(t_c, made[0])

            per_e = lambda a: a.unsqueeze(2).broadcast_to([P, E1, NT])
            et = lambda a: a[:, :, :].rearrange("p e t -> p (e t)")
            dve.wait_ge(t_mm, 1)
            pre = psum[4][:, 0:E1 * NT]
            tot = psum[4][:, E1 * NT:2 * E1 * NT]

            def counts():
                then(dve.tensor_tensor_scan(et(run), et(reset), tot, 0.0, ALU.mult, ALU.add))
                then(dve.tensor_tensor(et(off), et(run), tot, ALU.subtract))
                then(dve.tensor_tensor(et(off), et(off), pre, ALU.add))
                then(dve.tensor_copy(cnt[:, :], run[:, :, NT - 1]))
                then(dve.tensor_tensor(gtk[:, :, :], per_e(cnt[:, :]),
                                       thr[:, :].unsqueeze(1).broadcast_to([P, E1, NT]), ALU.is_gt))

            def first_blocks():
                then(dve.tensor_reduce(nblk[:, :], gtk[:, :, :], AX.X, ALU.add))
                then(dve.tensor_tensor_scan(end[:, :], ones[:, 0:E1], nblk[:, :], 0.0, ALU.mult, ALU.add))
                then(dve.tensor_tensor(beg[:, :], end[:, :], nblk[:, :], ALU.subtract))
                then(dve.tensor_scalar(beg[:, :], beg[:, :], float(P), None, ALU.mult))

            def slots():
                then(dve.tensor_tensor(off[:, :, :], off[:, :, :], per_e(beg[:, :]), ALU.add))
                then(dve.tensor_tensor(off[:, :, :], off[:, :, :], oh_all[:, :, :].rearrange("p t e -> p e t"),
                                       ALU.mult))
                then(dve.tensor_reduce(slot_f[:, :], off[:, :, :].rearrange("p e t -> p t e"), AX.X, ALU.add))
                dve.tensor_copy(slot[:, :], slot_f[:, :]).then_inc(t_slot, 1)

            def block_experts():
                then(dve.tensor_tensor(leb[:, :, :], end[:, :].unsqueeze(1).broadcast_to([P, NB, E1]),
                                       blk_no[:, :].unsqueeze(2).broadcast_to([P, NB, E1]), ALU.is_le))
                then(dve.tensor_reduce(ex_f[:, :], leb[:, :, :], AX.X, ALU.add))
                then(dve.tensor_scalar(ex_f[:, :], ex_f[:, :], float(E1 - 1), None, ALU.min))
                dve.tensor_copy(ex[:, :], ex_f[:, :]).then_inc(t_ex, 1)

            def store_v(bank, v, done):
                dve.wait_ge(n_V, done + 1)
                src = bank[:, :].rearrange("p (j m r d) -> p m j r d", j=HH, m=TT, r=2)
                for r in range(2):
                    ins = dve.tensor_copy(vt_next[r * HT:(r + 1) * HT, :, v * HH:(v + 1) * HH, :],
                                          src[r * HT:(r + 1) * HT, :, :, r, :])
                ins.then_inc(n_Vs, 1)

            def rest_of_pair(bank, par, g, done):
                dve.wait_ge(n_hi, done + 1)
                parts = bank[:, :].rearrange("p (s h k) -> p s h k", s=2, h=HH)
                dve.tensor_tensor(ql[par][:, :, g, :], parts[:, 0], hi[par][:, 0, :, g, :].bitcast(F32), ALU.subtract)
                low = hi[par][KS:P, 1, :, g, :]
                dve.tensor_tensor(low, parts[KS:P, 1], low.bitcast(F32), ALU.subtract).then_inc(n_lo, 1)

            def take_heads(bank, t):
                dve.wait_ge(n_T, t + 1)
                src = bank[:, :].rearrange("p (a b c j d) -> p b a c j d", a=2, b=2, c=TT, j=2)
                for half in range(2):
                    for j in range(2):
                        ins = dve.tensor_copy(
                            s1[half * HT:(half + 1) * HT, bass.ds(t * 2 - 2, 2), :]
                            .rearrange("p a (c j d) -> p a c j d", c=TT, j=2)[:, :, :, j, :],
                            src[j * HT:(j + 1) * HT, half, :, :, j, :])
                ins.then_inc(n_s1, 1)

            def rest_of_tokens(half, par):
                dve.wait_ge(n_xh, half + 1)
                dve.tensor_tensor(xp_lo[par][:, :], xn2T[:, half_tokens(half)], xp_hi[par][:, :].bitcast(F32),
                                  ALU.subtract).then_inc(n_xl, 1)

            for half in range(2):
                rest_of_tokens(half, half)
            for v in range(2):
                store_v(pair_bank(v), v, v)
            for g in range(HEADS):
                rest_of_pair(pair_bank(g), 0, g, g)
                if g in (1, 3, 5, 7):
                    (counts, first_blocks, slots, block_experts)[g // 2]()
            dve.wait_ge(ld_b, 16)

            def inverse(bt, n):
                dve.wait_ge(n_e, bt * ST + n + 1 + NS)
                dve.wait_ge(n_vs, bt * ST + n + 1)
                dve.reciprocal(rz[:, n % PB:n % PB + 1], zz[:, n % PB:n % PB + 1]).then_inc(n_rz, 1)

            def body(bt, kind, last):
                def maxima(n):
                    dve.wait_ge(n_s, bt * ST + n + 1)
                    dve.wait_ge(n_e, bt * ST + n + 1)
                    dve.tensor_reduce(nmx[:, n % PB:n % PB + 1], ring_bank(SCORE, n)[:, :], AX.X, ALU.max,
                                      negate=True).then_inc(n_mx, 1)

                for n in range(ST):
                    maxima(n)
                    if n > 1 or not kind == FIRST:
                        inverse(bt, n - 2)
                    if n - LO_LAG in pair_of and n % SH >= LO_LAG and not (last and n >= SH):
                        p = pair_of[n - LO_LAG]
                        rest_of_pair(pair_bank(p), 1 - p // HEADS, p % HEADS, bt * PAIRS + HEADS + p)
                    if n % SH == SPLIT_AT + 2 and not last:
                        rest_of_tokens(bt * 2 + n // SH + 2, n // SH)
                    if n - 1 in V_AT and not last:
                        v = V_AT.index(n - 1)
                        if v == 0:
                            dve.wait_ge(n_vt, bt + 1)
                        store_v(ring_bank(V_NEXT, v), v, bt * 2 + 2 + v)
                    if n % SH == HEADS_AT + 1 and not (kind == FIRST and n < SH):
                        take_heads(ring_bank(HEADS_T, n // SH), bt * 2 + n // SH)

            def make(stage, k, par):
                if stage == UP:
                    dve.wait_ge(m_up, k + 3)
                    dve.wait_ge(m_hT, k + 1)
                    dve.tensor_copy(hs[par][:, :], psum[(0, 1)[par]][:, :]).then_inc(m_hs, 1)
                elif stage == DN:
                    e = dve.value_load(ex[0:1, bass.ds(k, 1)], min_val=0, max_val=E1 - 1)
                    dve.wait_ge(m_dn, k + 3)
                    dve.wait_ge(m_st[par], (k - par + 2) * 8)
                    dve.tensor_tensor(ys[par][:, :], psum[(5, 6)[par]][:, 0:D],
                                      b2_bc[:, bass.ds(e, 1), :].rearrange("p a d -> p (a d)"), ALU.add)\
                       .then_inc(m_y, 1)

            layer1(dve, body, make)
            for n in (-2, -1):
                inverse(B, n)
            take_heads(pair_bank(0), B * 2)

        @blk.sync
        def _(sp):
            sp.sem_inc(n_vs, PB)
            sp.sem_inc(g_st, 16)
            for par in range(2):
                sp.sem_inc(m_st[par], 16)
            for s_ in (m_T, m_up, m_hT):
                sp.sem_inc(s_, 2)
            sp.wait_ge(f_x1, B)
            sp.wait_ge(f_dn, B * CH + NU)
            sp.wait_ge(f_k3, B + 1)
            sp.wait_ge(f_s3, B + 2)
            sp.dma_start(b2_bc[:, :, :], b2.rearrange("e d -> (e d)").partition_broadcast(P)).then_inc(ld_b, 16)
            sp.wait_ge(t_z, 1)
            sp.dma_start(x_sorted.rearrange("(k p) d -> p k d", p=P), zero[:, :].unsqueeze(1).broadcast_to([P, NB, D]))\
              .then_inc(t_z, 16)
            sp.wait_ge(t_sc, 16 * NT)
            xs_v = x_sorted.rearrange("(k p) d -> p k d", p=P)
            ys_v = y_sorted.rearrange("(k p) d -> p k d", p=P)
            flat = lambda a: a.rearrange("p a d -> p (a d)")

            def make(stage, k, par):
                if stage == LOAD:
                    sp.wait_ge(m_T, k + 1)
                    sp.dma_start(xg[par][:, :], flat(xs_v[:, bass.ds(k, 1), :])).then_inc(m_ld[par], 16)
                elif stage == DN:
                    sp.wait_ge(m_y, k + 3)
                    sp.dma_start(flat(ys_v[:, bass.ds(k, 1), :]), ys[par][:, :]).then_inc(m_st[par], 16)

            blocks(sp, make)
            ov = out.rearrange("b (t p) d -> p (b t) d", p=P)
            with sp.Fori(0, B) as k:
                sp.wait_ge(g_o, k + 2)
                sp.dma_start(ov[:, bass.ds(k * TT, TT), :], ob[:, :, :]).then_inc(g_st, 16)
            sp.wait_ge(g_st, 16 * B + 16)


_INS = ['L0_attn_x', 'L0_attn_W', 'L0_attn_b', 'L0_ffn_ln_g', 'L0_ffn_ln_b', 'L0_ffn_aw1', 'L0_ffn_ab1', 'L0_ffn_aw2',
        'L0_ffn_ab2', 'L0_ffn_gate_w', 'L0_ffn_gate_b', 'L0_ffn_ew1', 'L0_ffn_eb1', 'L0_ffn_ew2', 'L0_ffn_eb2',
        'L0_ffn_gens', 'L0_ffn_gc_w', 'L0_ffn_gc_b', 'L1_attn_Mq', 'L1_attn_Mk', 'L1_attn_Mv', 'L1_ffn_Wg', 'L1_ffn_bg',
        'L1_ffn_W1', 'L1_ffn_b1', 'L1_ffn_W2', 'L1_ffn_b2']
_OUTS = [((8, 512, 128), 'float32')]


def kernel(**inputs):
    import numpy as _np
    import concourse.bacc as _bacc
    from concourse import mybir as _mybir
    from concourse.bass_utils import run_bass_kernel_spmd as _run

    nc = _bacc.Bacc("TRN2", target_bir_lowering=False, num_devices=1)
    arrays, args = {}, []
    for name in _INS:
        a = _np.ascontiguousarray(inputs[name])
        arrays[f"in_{name}_dram"] = a
        args.append(nc.dram_tensor(f"in_{name}_dram", a.shape, _mybir.dt.from_np(a.dtype), kind="ExternalInput").ap())
    for i, (shape, dtype) in enumerate(_OUTS):
        dt = _mybir.dt.from_np(_np.dtype(dtype))
        args.append(nc.dram_tensor(f"out_{i}_dram", shape, dt, kind="ExternalOutput").ap())
    recurrent_d2_kernel(nc, *args)
    r = _run(nc, [arrays], core_ids=[0])
    got = tuple(r.results[0][f"out_{i}_dram"] for i in range(len(_OUTS)))
    return got[0]
```
